# Optimizing a Trainium2 kernel written in Bass

```python
import numpy as np
import jax
import jax.numpy as jnp

def _softmax(x, axis=-1):
    return jax.nn.softmax(x, axis=axis)

def _gelu(x):
    return jax.nn.gelu(x, approximate=True)

def _silu(x):
    return jax.nn.silu(x)

def _sigmoid(x):
    return jax.nn.sigmoid(x)

def _layernorm(x, axis=-1, eps=1e-05):
    m = jnp.mean(x, axis=axis, keepdims=True)
    v = jnp.var(x, axis=axis, keepdims=True)
    return (x - m) / jnp.sqrt(v + eps)

def _scatter_add(tgt, idx, src, axis=0):
    return tgt.at[idx].add(src)

def _segment_sum(src, seg, n):
    return jax.ops.segment_sum(src, seg, n)
kernel_name = 'mk_seq_preln_d2_jaxref_r8_4edf6a'

def setup_inputs(seed: int=0):
    np.random.seed(seed)
    _w = jnp.asarray

    def _L0_attn_setup():
        import jax, jax.numpy as jnp
        import numpy as np
        D_MODEL = 256
        N_HEAD = 16
        SEM_DIM = 128
        GEO_DIM = 128
        ATTN_DIM = 256
        ROPE_BASE = 10000.0

        def _rope(x, base=ROPE_BASE):
            S, d = (x.shape[-2], x.shape[-1])
            inv_freq = 1.0 / base ** (jnp.arange(0, d, 2, dtype=jnp.float32) / d)
            t = jnp.arange(S, dtype=jnp.float32)
            freqs = jnp.einsum('s,f->sf', t, inv_freq)
            cos, sin = (jnp.cos(freqs), jnp.sin(freqs))
            x1, x2 = (x[..., :d // 2], x[..., d // 2:])
            return jnp.concatenate([x1 * cos - x2 * sin, x1 * sin + x2 * cos], axis=-1).astype(x.dtype)

        def _split_heads(y, H):
            B, S, dim = y.shape
            return y.reshape(B, S, H, dim // H).transpose(0, 2, 1, 3)
        key = jax.random.key(seed)
        ks = jax.random.split(key, 7)
        B, S = (2, 256)
        sd = 0.02
        return {'x': jax.random.normal(ks[0], (B, S, D_MODEL), dtype=jnp.float32), 'Wq_sem': jax.random.normal(ks[1], (SEM_DIM, D_MODEL), dtype=jnp.float32) * sd, 'Wk_sem': jax.random.normal(ks[2], (SEM_DIM, D_MODEL), dtype=jnp.float32) * sd, 'Wq_geo': jax.random.normal(ks[3], (GEO_DIM, D_MODEL), dtype=jnp.float32) * sd, 'Wk_geo': jax.random.normal(ks[4], (GEO_DIM, D_MODEL), dtype=jnp.float32) * sd, 'Wv': jax.random.normal(ks[5], (ATTN_DIM, D_MODEL), dtype=jnp.float32) * sd, 'Wo': jax.random.normal(ks[6], (D_MODEL, ATTN_DIM), dtype=jnp.float32) * sd}
    _L0_attn_in = _L0_attn_setup()

    def _L0_ffn_setup():
        import jax, jax.numpy as jnp
        import numpy as np

        def _sparsify_2to4(h):
            B, S, I = h.shape
            g = h.reshape(B, S, I // 4, 4)
            a = jnp.abs(g)
            _, idx = jax.lax.top_k(a, 2)
            pos = jnp.arange(4)
            mask = (pos == idx[..., 0:1]) | (pos == idx[..., 1:2])
            return (g * mask.astype(g.dtype)).reshape(B, S, I)
        key = jax.random.key(seed)
        k1, k2, k3, k4 = jax.random.split(key, 4)
        B, S, H, I = (4, 256, 256, 1024)
        x = jax.random.normal(k1, (B, S, H), dtype=jnp.float32)
        w_gate = jax.random.normal(k2, (H, I), dtype=jnp.float32) / np.sqrt(H)
        w_up = jax.random.normal(k3, (H, I), dtype=jnp.float32) / np.sqrt(H)
        w_down = jax.random.normal(k4, (I, H), dtype=jnp.float32) / np.sqrt(I)
        return {'x': x, 'w_gate': w_gate, 'w_up': w_up, 'w_down': w_down}
    _L0_ffn_in = _L0_ffn_setup()

    def _L1_attn_setup():
        import jax, jax.numpy as jnp
        import numpy as np
        EPS = 1e-06

        def rmsnorm(x, w):
            return x * jax.lax.rsqrt(jnp.mean(x * x, axis=-1, keepdims=True) + EPS) * w

        def rope(x, freqs):
            xr = x.reshape(x.shape[:-1] + (-1, 2))
            c, s = (jnp.cos(freqs), jnp.sin(freqs))
            x0, x1 = (xr[..., 0], xr[..., 1])
            return jnp.stack([x0 * c - x1 * s, x0 * s + x1 * c], axis=-1).reshape(x.shape)
        B_, L, D = (2, 256, 256)
        Din, H, P, N = (512, 64, 64, 128)
        key = jax.random.key(seed)
        ks = jax.random.split(key, 10)
        sd = lambda fan: 1.0 / np.sqrt(fan)
        f32 = jnp.float32
        return {'x': jax.random.normal(ks[0], (B_, L, D), f32), 'Wx': (jax.random.normal(ks[1], (Din, D)) * sd(D)).astype(f32), 'Wz': (jax.random.normal(ks[2], (Din, D)) * sd(D)).astype(f32), 'WB': (jax.random.normal(ks[3], (H * N, D)) * sd(D)).astype(f32), 'WC': (jax.random.normal(ks[4], (H * N, D)) * sd(D)).astype(f32), 'Wdt': jax.random.uniform(ks[5], (H, D), f32, -0.0001, 0.0001), 'Wlam': (jax.random.normal(ks[6], (H, D)) * sd(D)).astype(f32), 'Wth': (jax.random.normal(ks[7], (H * (N // 2), D)) * sd(D)).astype(f32), 'A_log': jnp.log(jnp.linspace(1.0, N, H)).astype(f32), 'Bn_w': jnp.ones((N,), f32), 'Cn_w': jnp.ones((N,), f32), 'B_bias': jnp.ones((H, N), f32), 'C_bias': jnp.ones((H, N), f32), 'Wout': (jax.random.normal(ks[8], (D, Din)) * sd(Din)).astype(f32)}
    _L1_attn_in = _L1_attn_setup()

    def _L1_ffn_setup():
        import jax, jax.numpy as jnp
        import numpy as np
        TOP_K = 2
        key = jax.random.key(seed)
        k1, k2, k3, k4 = jax.random.split(key, 4)
        B, S, H, I, E = (2, 128, 256, 176, 8)
        hidden_states = jax.random.normal(k1, (B, S, H), dtype=jnp.float32)
        gate_w = jax.random.normal(k2, (E, H), dtype=jnp.float32) * (1.0 / np.sqrt(H))
        w1 = jax.random.normal(k3, (E, 2 * I, H), dtype=jnp.float32) * (1.0 / np.sqrt(H))
        w2 = jax.random.normal(k4, (E, H, I), dtype=jnp.float32) * (1.0 / np.sqrt(I))
        return {'hidden_states': hidden_states, 'gate_w': gate_w, 'w1': w1, 'w2': w2}
    _L1_ffn_in = _L1_ffn_setup()
    _d = {'L0_attn_x': _L0_attn_in['x'], 'L0_attn_Wq_sem': _L0_attn_in['Wq_sem'], 'L0_attn_Wk_sem': _L0_attn_in['Wk_sem'], 'L0_attn_Wq_geo': _L0_attn_in['Wq_geo'], 'L0_attn_Wk_geo': _L0_attn_in['Wk_geo'], 'L0_attn_Wv': _L0_attn_in['Wv'], 'L0_attn_Wo': _L0_attn_in['Wo'], 'L0_ffn_w_gate': _L0_ffn_in['w_gate'], 'L0_ffn_w_up': _L0_ffn_in['w_up'], 'L0_ffn_w_down': _L0_ffn_in['w_down'], 'L1_attn_Wx': _L1_attn_in['Wx'], 'L1_attn_Wz': _L1_attn_in['Wz'], 'L1_attn_WB': _L1_attn_in['WB'], 'L1_attn_WC': _L1_attn_in['WC'], 'L1_attn_Wdt': _L1_attn_in['Wdt'], 'L1_attn_Wlam': _L1_attn_in['Wlam'], 'L1_attn_Wth': _L1_attn_in['Wth'], 'L1_attn_A_log': _L1_attn_in['A_log'], 'L1_attn_Bn_w': _L1_attn_in['Bn_w'], 'L1_attn_Cn_w': _L1_attn_in['Cn_w'], 'L1_attn_B_bias': _L1_attn_in['B_bias'], 'L1_attn_C_bias': _L1_attn_in['C_bias'], 'L1_attn_Wout': _L1_attn_in['Wout'], 'L1_ffn_gate_w': _L1_ffn_in['gate_w'], 'L1_ffn_w1': _L1_ffn_in['w1'], 'L1_ffn_w2': _L1_ffn_in['w2']}
    _x0 = _d['L0_attn_x']
    _d['L0_attn_x'] = jax.random.normal(jax.random.fold_in(jax.random.key(seed), 1), (8, 512, 256), dtype=_x0.dtype)
    del _x0
    return _d

def reference(L0_attn_x, L0_attn_Wq_sem, L0_attn_Wk_sem, L0_attn_Wq_geo, L0_attn_Wk_geo, L0_attn_Wv, L0_attn_Wo, L0_ffn_w_gate, L0_ffn_w_up, L0_ffn_w_down, L1_attn_Wx, L1_attn_Wz, L1_attn_WB, L1_attn_WC, L1_attn_Wdt, L1_attn_Wlam, L1_attn_Wth, L1_attn_A_log, L1_attn_Bn_w, L1_attn_Cn_w, L1_attn_B_bias, L1_attn_C_bias, L1_attn_Wout, L1_ffn_gate_w, L1_ffn_w1, L1_ffn_w2):

    def _L0_attn_ref(x, Wq_sem, Wk_sem, Wq_geo, Wk_geo, Wv, Wo):
        import jax, jax.numpy as jnp
        import numpy as np
        D_MODEL = 256
        N_HEAD = 16
        SEM_DIM = 128
        GEO_DIM = 128
        ATTN_DIM = 256
        ROPE_BASE = 10000.0

        def _rope(x, base=ROPE_BASE):
            S, d = (x.shape[-2], x.shape[-1])
            inv_freq = 1.0 / base ** (jnp.arange(0, d, 2, dtype=jnp.float32) / d)
            t = jnp.arange(S, dtype=jnp.float32)
            freqs = jnp.einsum('s,f->sf', t, inv_freq)
            cos, sin = (jnp.cos(freqs), jnp.sin(freqs))
            x1, x2 = (x[..., :d // 2], x[..., d // 2:])
            return jnp.concatenate([x1 * cos - x2 * sin, x1 * sin + x2 * cos], axis=-1).astype(x.dtype)

        def _split_heads(y, H):
            B, S, dim = y.shape
            return y.reshape(B, S, H, dim // H).transpose(0, 2, 1, 3)
        B, S, _ = x.shape
        H = N_HEAD
        q_sem = _split_heads(x @ Wq_sem.T, H)
        k_sem = _split_heads(x @ Wk_sem.T, H)
        q_geo = _rope(_split_heads(x @ Wq_geo.T, H))
        k_geo = _rope(_split_heads(x @ Wk_geo.T, H))
        v = _split_heads(x @ Wv.T, H)
        q = jnp.concatenate([q_sem, q_geo], axis=-1)
        k = jnp.concatenate([k_sem, k_geo], axis=-1)
        scale = 1.0 / jnp.sqrt(jnp.asarray(q.shape[-1], dtype=jnp.float32))
        scores = jnp.einsum('bhqd,bhkd->bhqk', q, k).astype(jnp.float32) * scale
        causal = jnp.tril(jnp.ones((S, S), dtype=bool))
        scores = jnp.where(causal, scores, jnp.finfo(jnp.float32).min)
        attn = jax.nn.softmax(scores, axis=-1).astype(v.dtype)
        out = jnp.einsum('bhqk,bhkd->bhqd', attn, v)
        out = out.transpose(0, 2, 1, 3).reshape(B, S, ATTN_DIM)
        return out @ Wo.T

    def _L0_ffn_ref(x, w_gate, w_up, w_down):
        import jax, jax.numpy as jnp
        import numpy as np

        def _sparsify_2to4(h):
            B, S, I = h.shape
            g = h.reshape(B, S, I // 4, 4)
            a = jnp.abs(g)
            _, idx = jax.lax.top_k(a, 2)
            pos = jnp.arange(4)
            mask = (pos == idx[..., 0:1]) | (pos == idx[..., 1:2])
            return (g * mask.astype(g.dtype)).reshape(B, S, I)
        h = jax.nn.silu(jnp.einsum('bsh,hi->bsi', x, w_gate)) * jnp.einsum('bsh,hi->bsi', x, w_up)
        h_sparse = _sparsify_2to4(h)
        return jnp.einsum('bsi,ih->bsh', h_sparse, w_down)

    def _L1_attn_ref(x, Wx, Wz, WB, WC, Wdt, Wlam, Wth, A_log, Bn_w, Cn_w, B_bias, C_bias, Wout):
        import jax, jax.numpy as jnp
        import numpy as np
        EPS = 1e-06

        def rmsnorm(x, w):
            return x * jax.lax.rsqrt(jnp.mean(x * x, axis=-1, keepdims=True) + EPS) * w

        def rope(x, freqs):
            xr = x.reshape(x.shape[:-1] + (-1, 2))
            c, s = (jnp.cos(freqs), jnp.sin(freqs))
            x0, x1 = (xr[..., 0], xr[..., 1])
            return jnp.stack([x0 * c - x1 * s, x0 * s + x1 * c], axis=-1).reshape(x.shape)
        B_, L, D = x.shape
        H = A_log.shape[0]
        N = B_bias.shape[1]
        Din = Wx.shape[0]
        P = Din // H
        xp = x @ Wx.T
        z = x @ Wz.T
        Bm = (x @ WB.T).reshape(B_, L, H, N)
        Cm = (x @ WC.T).reshape(B_, L, H, N)
        Bm = rmsnorm(Bm, Bn_w) + B_bias
        Cm = rmsnorm(Cm, Cn_w) + C_bias
        dt = jax.nn.softplus(x @ Wdt.T)
        lam = jax.nn.sigmoid(x @ Wlam.T)
        theta = (x @ Wth.T).reshape(B_, L, H, N // 2)
        theta_cumsum = jnp.cumsum(theta * dt[..., None], axis=1)
        Bm = rope(Bm, theta_cumsum)
        Cm = rope(Cm, theta_cumsum)
        xh = xp.reshape(B_, L, H, P)
        A = -jnp.exp(A_log)
        alpha = jnp.exp(dt * A)
        beta = (1.0 - lam) * dt * alpha
        gamma = lam * dt

        def step(carry, inputs):
            h, B_prev, x_prev = carry
            Bt, Ct, xt, at, bt, gt = inputs
            h = at[..., None, None] * h + jnp.einsum('bh,bhn,bhp->bhnp', bt, B_prev, x_prev) + jnp.einsum('bh,bhn,bhp->bhnp', gt, Bt, xt)
            yt = jnp.einsum('bhn,bhnp->bhp', Ct, h)
            return ((h, Bt, xt), yt)
        h0 = jnp.zeros((B_, H, N, P), x.dtype)
        carry0 = (h0, jnp.zeros((B_, H, N), x.dtype), jnp.zeros((B_, H, P), x.dtype))
        seq = (Bm.transpose(1, 0, 2, 3), Cm.transpose(1, 0, 2, 3), xh.transpose(1, 0, 2, 3), alpha.transpose(1, 0, 2), beta.transpose(1, 0, 2), gamma.transpose(1, 0, 2))
        _, ys = jax.lax.scan(step, carry0, seq)
        y = ys.transpose(1, 0, 2, 3).reshape(B_, L, H * P)
        y = y * jax.nn.silu(z)
        return y @ Wout.T

    def _L1_ffn_ref(hidden_states, gate_w, w1, w2):
        import jax, jax.numpy as jnp
        import numpy as np
        TOP_K = 2
        B, S, H = hidden_states.shape
        E = gate_w.shape[0]
        T = B * S
        x = hidden_states.reshape(T, H)
        logits = jnp.einsum('th,eh->te', x, gate_w)
        probs = jax.nn.softmax(logits, axis=-1)
        topw, sel = jax.lax.top_k(probs, TOP_K)
        topw = topw / jnp.sum(topw, axis=-1, keepdims=True)
        combine = jnp.zeros((T, E), dtype=x.dtype).at[jnp.arange(T)[:, None], sel].add(topw)
        gate_up = jnp.einsum('th,eoh->eto', x, w1)
        g, u = jnp.split(gate_up, 2, axis=-1)
        act = jax.nn.silu(g) * u
        expert_out = jnp.einsum('eti,ehi->eth', act, w2)
        out = jnp.einsum('eth,te->th', expert_out, combine)
        return out.reshape(B, S, H)
    x = L0_attn_x
    x = x + _L0_attn_ref(_layernorm(x, axis=-1), L0_attn_Wq_sem, L0_attn_Wk_sem, L0_attn_Wq_geo, L0_attn_Wk_geo, L0_attn_Wv, L0_attn_Wo)
    x = x + _L0_ffn_ref(_layernorm(x, axis=-1), L0_ffn_w_gate, L0_ffn_w_up, L0_ffn_w_down)
    x = x + _L1_attn_ref(_layernorm(x, axis=-1), L1_attn_Wx, L1_attn_Wz, L1_attn_WB, L1_attn_WC, L1_attn_Wdt, L1_attn_Wlam, L1_attn_Wth, L1_attn_A_log, L1_attn_Bn_w, L1_attn_Cn_w, L1_attn_B_bias, L1_attn_C_bias, L1_attn_Wout)
    x = x + _L1_ffn_ref(_layernorm(x, axis=-1), L1_ffn_gate_w, L1_ffn_w1, L1_ffn_w2)
    return x

_drawn_inputs = setup_inputs


def setup_inputs(seed=0):
    import zlib

    import numpy as np

    out = dict(_drawn_inputs(seed))
    spreads = {'L1_attn_Bn_w': (1.0, 0.6),
     'L1_attn_Cn_w': (1.0, 0.6),
     'L1_attn_B_bias': (1.0, 0.2),
     'L1_attn_C_bias': (1.0, 0.2)}
    factors = {'L0_attn_Wq_sem': 8.0,
     'L0_attn_Wk_sem': 8.0,
     'L0_attn_Wq_geo': 8.0,
     'L0_attn_Wk_geo': 8.0,
     'L1_attn_Wdt': 25.251,
     'L1_attn_Wth': 3.313,
     'L1_ffn_gate_w': 4.509,
     'L1_ffn_w1': 3.949,
     'L1_ffn_w2': 3.966}
    for name, (base, spread) in spreads.items():
        noise = np.random.default_rng([zlib.crc32(name.encode()), seed]).standard_normal(out[name].shape)
        drawn = base * np.exp(spread * noise) if base else spread * noise
        out[name] = jnp.asarray(drawn.astype(out[name].dtype))
    for name, factor in factors.items():
        out[name] = (out[name] * factor).astype(out[name].dtype)
    return out
```

```python
from concourse import mybir
from contextlib import ExitStack
from contextlib import contextmanager
import concourse.bass as bass
import math
import numpy as np

FP32 = mybir.dt.float32
FP32R = mybir.dt.float32r
BF16 = mybir.dt.bfloat16
ALU = mybir.AluOpType
ACT = mybir.ActivationFunctionType
AX = mybir.AxisListType

P = 128
BATCH, SEQ, DM = 8, 512, 256
TOK = BATCH * SEQ
TILES = TOK // P
KD = DM // P
TPB = SEQ // P
LN_EPS = 1e-5
ds = bass.ds

class Chain:

    def __init__(self, eng, sem, base=0):
        self.eng, self.sem, self.base, self.n = eng, sem, base, 0

    def mark(self, ins):
        self.n += 1
        ins.then_inc(self.sem, 1)
        return self.n

    def wait(self, n=None):
        self.eng.wait_ge(self.sem, self.base + (self.n if n is None else n))

    def __call__(self, ins):
        self.mark(ins)
        self.wait()

def matmul3(nc, out, w_hi, w_lo, x_hi, x_lo, first, last):
    nc.tensor.matmul(out, w_hi, x_hi, start=first, stop=False)
    nc.tensor.matmul(out, w_hi, x_lo, start=False, stop=False)
    return nc.tensor.matmul(out, w_lo, x_hi, start=False, stop=last)

def layernorm_transposed(nc, ctx, name, src, g):
    GROUPS = 8
    PER = TILES // GROUPS
    sem = lambda n: nc.alloc_semaphore(name=f"{name}_{n}")
    loaded = [sem(f"loaded{q}") for q in range(GROUPS)]
    stats_done, var_ready, std_ready, norm_ready = sem("stats"), sem("var"), sem("std"), sem("normed")
    transposed, hi_ready, lo_ready, chain_sem = sem("transposed"), sem("hi"), sem("lo"), sem("chain")
    with ExitStack() as mem:
        sb = lambda n, s, d=FP32: mem.enter_context(nc.sbuf_tensor(f"{name}_{n}", s, d))
        x = sb("x", [P, TILES, DM])
        stats = sb("stats6", [P, TILES, 6])
        mean, diff, var, rstd = (sb(n, [P, TILES]) for n in ("mean", "diff", "var", "rstd"))
        normed = sb("normedx", [P, 2, DM])
        eps = sb("eps", [P, 1])
        turned = [mem.enter_context(nc.psum_tensor(f"{name}_ps{i}", [P, KD, P], FP32)) for i in range(2)]
        block = mem.enter_context(nc.Block())
        src_v = src.rearrange("(q n p) d -> q p n d", p=P, n=PER)

        @block.sync
        def _(sp):
            for q in range(GROUPS):
                sp.dma_start(x[:, q * PER:(q + 1) * PER, :], src_v[q]).then_inc(loaded[q], 16)

        @block.vector
        def _(dve):
            nc.vector.memset(eps[:], LN_EPS).then_inc(stats_done, 1)
            for q in range(GROUPS):
                dve.wait_ge(loaded[q], 16)
                for n in range(PER):
                    t = q * PER + n
                    last = nc.vector.bn_stats(stats[:, t, :], x[:, t, :])
                last.then_inc(stats_done, 1)
            dve.wait_ge(stats_done, 1 + GROUPS)
            link = Chain(dve, chain_sem)
            link.mark(nc.vector.tensor_tensor(mean[:], stats[:, :, 1], stats[:, :, 4], ALU.add))
            link.mark(nc.vector.tensor_tensor(diff[:], stats[:, :, 1], stats[:, :, 4], ALU.subtract))
            link(nc.vector.tensor_tensor(var[:], stats[:, :, 2], stats[:, :, 5], ALU.add))
            link.mark(nc.vector.tensor_scalar(mean[:], mean[:], 0.5, None, ALU.mult))
            link.mark(nc.vector.scalar_tensor_tensor(diff[:], diff[:], 0.25, diff[:], ALU.mult, ALU.mult))
            link(nc.vector.tensor_scalar(var[:], var[:], 1.0 / DM, None, ALU.mult))
            nc.vector.tensor_tensor(var[:], var[:], diff[:], ALU.add).then_inc(var_ready, 1)
            dve.wait_ge(std_ready, 1)
            link(nc.vector.reciprocal(rstd[:], rstd[:]))
            dve.sem_inc(lo_ready, 2)
            with dve.Fori(0, TILES // 2) as i:
                for p in range(2):
                    t = i * 2 + p
                    dve.wait_ge(transposed, i * 2)
                    nc.vector.tensor_scalar(normed[:, p, :], x[:, ds(t, 1), :], mean[:, ds(t, 1)],
                                            rstd[:, ds(t, 1)], ALU.subtract, ALU.mult).then_inc(norm_ready, 1)
                for p in range(2):
                    t = i * 2 + p
                    dve.wait_ge(hi_ready, t + 1)
                    cols = ds(t * P, P)
                    nc.vector.tensor_tensor(g.x_lo[:, :, cols], turned[p][:], g.x_hi[:, :, cols].bitcast(FP32),
                                            ALU.subtract).then_inc(lo_ready, 1)

        @block.scalar
        def _(act):
            act.wait_ge(var_ready, 1)
            act.wait_ge(stats_done, 1)
            nc.scalar.activation(rstd[:], var[:], ACT.Sqrt, bias=eps[:, 0:1]).then_inc(std_ready, 1)
            with act.Fori(0, TILES // 2) as i:
                for p in range(2):
                    t = i * 2 + p
                    act.wait_ge(transposed, t + 1)
                    nc.scalar.activation(g.x_hi[:, :, ds(t * P, P)], turned[p][:], ACT.Copy).then_inc(hi_ready, 1)

        @block.tensor
        def _(pe):
            with pe.Fori(0, TILES // 2) as i:
                for p in range(2):
                    t = i * 2 + p
                    pe.wait_ge(norm_ready, t + 1)
                    pe.wait_ge(lo_ready, t + 1)
                    for k in range(KD):
                        last = nc.tensor.transpose(turned[p][:, k, :], normed[:, p, k * P:(k + 1) * P], g.ident[:])
                    last.then_inc(transposed, 1)

class OnChip:
    pass

def constants(nc, ctx):
    g = OnChip()
    sb = lambda n, s, d=FP32: ctx.enter_context(nc.sbuf_tensor(n, s, d))
    g.ident = sb("ident", [P, P])
    g.ident16 = sb("ident16", [P, P], BF16)
    g.x_hi = sb("x_hi", [P, KD, TOK], FP32R)
    g.x_lo = sb("x_lo", [P, KD, TOK], FP32R)
    made = ctx.enter_context(nc.semaphore("ident_made"))
    with nc.Block() as block:
        @block.gpsimd
        def _(pool):
            nc.gpsimd.memset(g.ident[:], 0.0).then_inc(made, 1)
            pool.wait_ge(made, 1)
            nc.gpsimd.affine_select(out=g.ident[:], in_=g.ident[:], compare_op=ALU.not_equal, fill=1.0, base=0,
                                    pattern=[[-1, P]], channel_multiplier=1).then_inc(made, 1)
            pool.wait_ge(made, 2)
            nc.gpsimd.tensor_copy(g.ident16[:], g.ident[:]).then_inc(made, 1)
            pool.wait_ge(made, 3)
    return g

H0, DH = 16, 16
HG = 4
G0 = H0 // HG
QKC = 2 * 2 * G0 * P

def causal_attention(nc, ctx, src, dst, w_d, wo_d, tables_d, lower_d, below_d, g):
    sem = lambda n: nc.alloc_semaphore(name=f"a0_{n}")
    w_loaded, w_split, t_loaded = sem("wload"), sem("wsplit"), sem("tload")
    ab_done, rope_read, rope_done, chain_sem = sem("ab"), sem("roperead"), sem("rope"), sem("chain")
    v_done, v_taken, vt_done, v_ready = sem("v"), sem("vtaken"), sem("vt"), sem("vready")
    s_done, max_done, exp_done, t_done = sem("s"), sem("max"), sem("exp"), sem("t")
    tv_done, ta_done, pv_done, norm_done = sem("tv"), sem("ta"), sem("pv"), sem("norm")
    ot_done, ot_ready, wo_done, out_done = sem("ot"), sem("otready"), sem("wo"), sem("out")
    stored, res_loaded = [sem("st0"), sem("st1")], [sem("res0"), sem("res1")]
    STEPS = H0 * TPB
    CH = 512
    CHUNKS = QKC // CH
    with ExitStack() as mem:
        sb = lambda n, s, d=FP32: mem.enter_context(nc.sbuf_tensor(f"a0_{n}", s, d))
        w_hi, w_lo = sb("whi", [P, KD, QKC + DM], FP32R), sb("wlo", [P, KD, QKC + DM], FP32R)
        raw = sb("raw", [P, KD, CH])
        wo = sb("wo", [P, KD, DM])
        tables = sb("tables", [P, 4, SEQ])
        lower = sb("lower", [P, 1])
        below_f, below = sb("belowf", [P, P]), sb("below", [P, P], BF16)
        t1, t2 = sb("t1", [P, SEQ]), sb("t2", [P, SEQ])
        y, y_hi = sb("y", [P, 2, SEQ]), sb("yhi", [P, SEQ], FP32R)
        q1, k1, k2 = (sb(n, [P, G0, SEQ], FP32R) for n in ("q1", "k1", "k2"))
        vt, v = sb("vt", [P, KD, SEQ]), sb("vv", [P, TPB, DM])
        nmax = sb("nmax", [P, 4])
        prob = sb("prob", [P, 3, SEQ])
        probt = sb("probt", [P, 2, SEQ])
        sums = sb("sums", [P, TPB * H0])
        o = sb("o", [P, TPB, DM])
        ot = sb("ot", [P, KD, SEQ])
        out = sb("outt", [P, 2, TPB, DM])
        ps = lambda n, s: mem.enter_context(nc.psum_tensor(f"a0_ps_{n}", s, FP32))
        p_s = [ps(f"s{i}", [P, SEQ]) for i in range(2)]
        p_t = [ps(f"t{i}", [P, SEQ]) for i in range(2)]
        p_o = ps("o", [P, TPB, DM])
        p_p = [ps(f"p{i}", [P, SEQ]) for i in range(2)]
        block = mem.enter_context(nc.Block())
        src_v = src.rearrange("(b n p) d -> b p n d", p=P, n=TPB)
        dst_v = dst.rearrange("(b n p) d -> b p n d", p=P, n=TPB)
        pieces = [(c * CH, CH) for c in range(CHUNKS)] + [(QKC, DM)]
        on_act = lambda i: i == TPB - 1

        @block.sync
        def _(sp):
            for n, (at, w) in enumerate(pieces):
                if n:
                    sp.wait_ge(w_split, 2 * n)
                sp.dma_start(raw[:, :, 0:w], w_d[:, :, at:at + w]).then_inc(w_loaded, 16)
                if n == 0:
                    sp.dma_start(tables[:], tables_d).then_inc(t_loaded, 16)
                    sp.dma_start(wo[:], wo_d).then_inc(t_loaded, 16)
                    sp.dma_start(lower[:], lower_d).then_inc(t_loaded, 16)
                    sp.dma_start(below_f[:], below_d).then_inc(t_loaded, 16)
            with sp.Fori(0, BATCH // 2) as i:
                for p in range(2):
                    b = i * 2 + p
                    sp.wait_ge(stored[p], 16 * i)
                    sp.dma_start(out[:, p], src_v[ds(b, 1)].rearrange("a p n d -> p (a n) d")).then_inc(res_loaded[p], 16)
                for p in range(2):
                    b = i * 2 + p
                    sp.wait_ge(out_done, b + 1)
                    sp.dma_start(dst_v[ds(b, 1)].rearrange("a p n d -> p (a n) d"), out[:, p]).then_inc(stored[p], 16)
            for p in range(2):
                sp.wait_ge(stored[p], 16 * (BATCH // 2))

        @block.gpsimd
        def _(pool):
            for n, (at, w) in enumerate(pieces):
                pool.wait_ge(w_split, 2 * n + 1)
                nc.gpsimd.tensor_tensor(w_lo[:, :, at:at + w], raw[:, :, 0:w], w_hi[:, :, at:at + w].bitcast(FP32),
                                        ALU.subtract).then_inc(w_split, 1)

        @block.tensor
        def _(pe):
            pe.wait_ge(w_split, 2 * len(pieces))
            pe.wait_ge(t_loaded, 65)
            with pe.Fori(0, BATCH) as b:
                tok = ds(b * SEQ, SEQ)

                def project(col, psum):
                    for k in range(KD):
                        cols = slice(col, col + P)
                        last = matmul3(nc, psum, w_hi[:, k, cols], w_lo[:, k, cols], g.x_hi[:, k, tok],
                                       g.x_lo[:, k, tok], k == 0, k == KD - 1)
                    return last

                pe.wait_ge(ot_ready, b)
                for n in range(2 * G0):
                    grp, qk = divmod(n, 2)
                    pe.wait_ge(rope_read, b * (2 * G0) + n)
                    project(((qk * 2 + 0) * G0 + grp) * P, p_p[0][:])
                    project(((qk * 2 + 1) * G0 + grp) * P, p_p[1][:]).then_inc(ab_done, 1)
                pe.wait_ge(rope_read, (b + 1) * (2 * G0))
                for k in range(KD):
                    project(QKC + k * P, p_p[k][:]).then_inc(v_done, 1)
                for n in range(TPB):
                    if n % 2 == 0:
                        pe.wait_ge(v_taken, (b + 1) * KD)
                    for k in range(KD):
                        last = nc.tensor.transpose(p_p[n // 2][:, ((n % 2) * KD + k) * P:((n % 2) * KD + k + 1) * P],
                                                   vt[:, k, n * P:(n + 1) * P], g.ident[:])
                    if n % 2:
                        last.then_inc(vt_done, 1)
                pe.wait_ge(rope_done, (b + 1) * (2 * G0))
                pe.wait_ge(v_ready, (b + 1) * 2)
                pe.wait_ge(out_done, b)
                for n in range(STEPS + 3):
                    if n < STEPS:
                        h, i = divmod(n, TPB)
                        grp, j = divmod(h, HG)
                        rows, width = slice(32 * j, 32 * j + 32), (i + 1) * P
                        if n >= 2:
                            pe.wait_ge(exp_done, b * STEPS + n - 1)
                        else:
                            pe.wait_ge(exp_done, b * STEPS)
                        s = p_s[n % 2]
                        nc.tensor.matmul(s[:, 0:width], q1[rows, grp, i * P:(i + 1) * P], k1[rows, grp, 0:width],
                                         start=True, stop=False)
                        nc.tensor.matmul(s[:, width - P:width], g.ident16[:], below[:], start=False, stop=False,
                                         skip_group_check=True)
                        nc.tensor.matmul(s[:, 0:width], q1[rows, grp, i * P:(i + 1) * P], k2[rows, grp, 0:width],
                                         start=False, stop=True).then_inc(s_done, 1)
                    if 2 <= n < STEPS + 2:
                        m = n - 2
                        i = m % TPB
                        pe.wait_ge(exp_done, b * STEPS + m + 1)
                        before = m - 2
                        if before >= 0:
                            if on_act(before % TPB):
                                pe.wait_ge(ta_done, b * H0 + before // TPB + 1)
                            else:
                                pe.wait_ge(tv_done, b * (STEPS - H0) + before - before // TPB + 1)
                        for kt in range(i + 1):
                            last = nc.tensor.transpose(p_t[m % 2][:, kt * P:(kt + 1) * P],
                                                       prob[:, m % 3, kt * P:(kt + 1) * P], g.ident[:])
                        last.then_inc(t_done, 1)
                    if n >= 3:
                        m = n - 3
                        h, i = divmod(m, TPB)
                        if on_act(i):
                            pe.wait_ge(ta_done, b * H0 + h + 1)
                        else:
                            pe.wait_ge(tv_done, b * (STEPS - H0) + m - h + 1)
                        for kt in range(i + 1):
                            last = nc.tensor.matmul(p_o[:, i, h * DH:(h + 1) * DH], probt[:, m % 2, kt * P:(kt + 1) * P],
                                                    v[:, kt, h * DH:(h + 1) * DH], start=kt == 0, stop=kt == i)
                        last.then_inc(pv_done, 1)
                pe.wait_ge(norm_done, b + 1)
                for k in range(KD):
                    for n in range(TPB):
                        last = nc.tensor.transpose(p_p[k][:, n * P:(n + 1) * P], o[:, n, k * P:(k + 1) * P], g.ident[:])
                last.then_inc(ot_done, 1)
                pe.wait_ge(ot_ready, b + 1)
                for n in range(TPB):
                    for k in range(KD):
                        last = nc.tensor.matmul(p_o[:, n, :], ot[:, k, n * P:(n + 1) * P], wo[:, k, :],
                                                start=k == 0, stop=k == KD - 1)
                last.then_inc(wo_done, 1)

        @block.scalar
        def _(act):
            A = nc.scalar.activation
            for n, (at, w) in enumerate(pieces):
                act.wait_ge(w_loaded, 16 * (n + 1))
                A(w_hi[:, :, at:at + w], raw[:, :, 0:w], ACT.Copy).then_inc(w_split, 1)
                if n < len(pieces) - 1:
                    act.wait_ge(w_split, 2 * n + 2)
            nc.scalar.preload_act_table(ACT.Exp)
            with act.Fori(0, BATCH) as b:
                for k in range(KD):
                    act.wait_ge(v_done, b * KD + k + 1)
                    A(vt[:, k, :], p_p[k][:], ACT.Copy).then_inc(v_taken, 1)
                act.wait_ge(pv_done, b * STEPS)
                for n in range(2):
                    act.wait_ge(vt_done, b * 2 + n + 1)
                    A(v[:, n * 2:(n + 1) * 2, :], p_p[n][:].rearrange("p (n d) -> p n d", n=2), ACT.Copy).then_inc(v_ready, 1)
                act.wait_ge(norm_done, b)
                for n in range(STEPS + 2):
                    if n < STEPS:
                        h, i = divmod(n, TPB)
                        act.wait_ge(max_done, b * STEPS + n + 1)
                        act.wait_ge(t_done, b * STEPS + max(n - 2, 0))
                        A(prob[:, n % 3, 0:(i + 1) * P], p_s[n % 2][:, 0:(i + 1) * P], ACT.Exp, bias=nmax[:, n % 4:n % 4 + 1],
                          accum_out=sums[:, i * H0 + h:i * H0 + h + 1]).then_inc(exp_done, 1)
                    if n >= 2 and on_act((n - 2) % TPB):
                        m = n - 2
                        act.wait_ge(t_done, b * STEPS + m + 1)
                        act.wait_ge(pv_done, b * STEPS + max(m - 1, 0))
                        A(probt[:, m % 2, :], p_t[m % 2][:], ACT.Copy).then_inc(ta_done, 1)
                act.wait_ge(ot_done, b + 1)
                for k in range(KD):
                    last = A(ot[:, k, :], p_p[k][:], ACT.Copy)
                last.then_inc(ot_ready, 1)

        @block.vector
        def _(dve):
            V = nc.vector
            dve.wait_ge(t_loaded, 64)
            V.tensor_copy(below[:], below_f[:]).then_inc(t_loaded, 1)
            PER = 2 * G0 * 2 + 1
            with dve.Fori(0, BATCH) as b:
                link = Chain(dve, chain_sem, b * PER)
                dve.wait_ge(s_done, b * STEPS)
                for n in range(2 * G0):
                    grp, qk = divmod(n, 2)
                    dve.wait_ge(ab_done, b * (2 * G0) + n + 1)
                    V.tensor_tensor(t1[:], p_p[0][:], tables[:, qk * 2, :], ALU.mult)
                    V.tensor_tensor(t2[:], p_p[1][:], tables[:, qk * 2 + 1, :], ALU.mult).then_inc(rope_read, 1)
                    dve.wait_ge(rope_read, b * (2 * G0) + n + 1)
                    link(V.tensor_tensor(y[:, qk, :], t1[:], t2[:], ALU.add))
                    if qk == 0:
                        link(V.tensor_copy(y_hi[:], y[:, 0, :]))
                        V.scalar_tensor_tensor(q1[:, grp, :], y_hi[:].bitcast(FP32), lower[:, 0:1], y[:, 0, :],
                                               ALU.mult, ALU.add).then_inc(rope_done, 1)
                    else:
                        link(V.tensor_copy(k1[:, grp, :], y[:, 1, :]))
                        V.tensor_tensor(k2[:, grp, :], y[:, 1, :], k1[:, grp, :].bitcast(FP32),
                                        ALU.subtract).then_inc(rope_done, 1)
                    dve.wait_ge(rope_done, b * (2 * G0) + n + 1)
                for n in range(STEPS + 2):
                    if n < STEPS:
                        i = n % TPB
                        dve.wait_ge(s_done, b * STEPS + n + 1)
                        dve.wait_ge(exp_done, b * STEPS + max(n - 3, 0))
                        V.tensor_reduce(nmax[:, n % 4:n % 4 + 1], p_s[n % 2][:, 0:(i + 1) * P], AX.X, ALU.max,
                                        negate=True).then_inc(max_done, 1)
                    if n >= 2 and not on_act((n - 2) % TPB):
                        m = n - 2
                        i = m % TPB
                        dve.wait_ge(t_done, b * STEPS + m + 1)
                        dve.wait_ge(pv_done, b * STEPS + max(m - 1, 0))
                        V.tensor_copy(probt[:, m % 2, 0:(i + 1) * P], p_t[m % 2][:, 0:(i + 1) * P]).then_inc(tv_done, 1)
                dve.wait_ge(exp_done, (b + 1) * STEPS)
                link(V.reciprocal(sums[:], sums[:]))
                dve.wait_ge(pv_done, (b + 1) * STEPS)
                inv = sums[:].rearrange("p (n o) -> p n o", o=1).broadcast_to([P, TPB * H0, DH])
                V.tensor_tensor(o[:].rearrange("p i (h d) -> p (i h) d", d=DH),
                                p_o[:].rearrange("p i (h d) -> p (i h) d", d=DH), inv, ALU.mult).then_inc(norm_done, 1)
                dve.wait_ge(wo_done, b + 1)
                dve.wait_ge(res_loaded[0], (b // 2 + 1) * 16)
                dve.wait_ge(res_loaded[1], (b // 2 + 1) * 16)
                V.tensor_tensor(out[:, ds(b % 2, 1)], p_o[:].rearrange("p (o n) d -> p o n d", o=1),
                                out[:, ds(b % 2, 1)], ALU.add).then_inc(out_done, 1)
                PER_ = link.n
            assert PER_ == PER, (PER_, PER)

I0 = 1024
GROUP = 4
GT = I0 // GROUP // P
SLOTS = GT * GROUP

def sparse_swiglu(nc, ctx, src, dst, gate_d, up_d, down_d, g):
    sem = lambda n: nc.alloc_semaphore(name=f"f0_{n}")
    w_loaded, w_split, chain_sem = sem("wload"), sem("wsplit"), sem("chain")
    d_loaded = sem("dload")
    gate_done, up_done, silu_done = sem("gate"), sem("up"), sem("silu")
    h_done, kept_done, mag_done = sem("h"), sem("kept"), sem("mag")
    down_done, out_done, stored, res_loaded = sem("down"), sem("out"), [sem("st0"), sem("st1")], [sem("res0"), sem("res1")]
    with ExitStack() as mem:
        sb = lambda n, s, d=FP32: mem.enter_context(nc.sbuf_tensor(f"f0_{n}", s, d))
        wg_hi, wg_lo, wu_hi, wu_lo = (sb(n, [P, KD, I0], FP32R) for n in ("wgh", "wgl", "wuh", "wul"))
        raw = sb("raw", [P, KD, I0])
        wd = sb("wd", [P, SLOTS, DM])
        silu = sb("silu", [P, 2, SEQ])
        h = sb("h", [P, 2, SLOTS, SEQ])
        mag = sb("mag", [P, GROUP, SEQ])
        beats = sb("beats", [P, 6, SEQ], BF16)
        count = sb("count", [P, GROUP, SEQ], BF16)
        res = sb("res", [P, 2, TPB, DM])
        out = sb("outt", [P, 2, TPB, DM])
        ps = lambda n, s: mem.enter_context(nc.psum_tensor(f"f0_{n}", s, FP32))
        pg = [ps(f"pg{i}", [P, SEQ]) for i in range(2)]
        pu = [ps(f"pu{i}", [P, SEQ]) for i in range(2)]
        pd = [ps(f"pd{i}", [P, TPB, DM]) for i in range(2)]
        block = mem.enter_context(nc.Block())
        src_v = src.rearrange("(b n p) d -> b p n d", p=P, n=TPB)
        dst_v = dst.rearrange("(b n p) d -> b p n d", p=P, n=TPB)

        @block.sync
        def _(sp):
            sp.dma_start(raw[:], gate_d).then_inc(w_loaded, 16)
            sp.dma_start(wd[:], down_d).then_inc(d_loaded, 16)
            sp.wait_ge(w_split, 2)
            sp.dma_start(raw[:], up_d).then_inc(w_loaded, 16)
            sp.sem_inc(stored[0], 16)
            sp.sem_inc(stored[1], 16)
            with sp.Fori(0, BATCH // 2) as i:
                for p in range(2):
                    b = i * 2 + p
                    sp.wait_ge(out_done, b - p)
                    sp.dma_start(res[:, p], src_v[ds(b, 1)].rearrange("a p n d -> p (a n) d")).then_inc(res_loaded[p], 16)
                for p in range(2):
                    b = i * 2 + p
                    sp.wait_ge(out_done, b + 1)
                    sp.dma_start(dst_v[ds(b, 1)].rearrange("a p n d -> p (a n) d"), out[:, p]).then_inc(stored[p], 16)
            for p in range(2):
                sp.wait_ge(stored[p], 16 * (BATCH // 2 + 1))

        def gate_up(pe, b, gt):
            for r in range(GROUP):
                n = b * SLOTS + gt * GROUP + r
                s = gt * GROUP + r
                cols = slice(s * P, (s + 1) * P)
                pe.wait_ge(silu_done, n + 1)
                for k in range(KD):
                    last = matmul3(nc, pg[r % 2][:], wg_hi[:, k, cols], wg_lo[:, k, cols],
                                   g.x_hi[:, k, ds(b * SEQ, SEQ)], g.x_lo[:, k, ds(b * SEQ, SEQ)],
                                   k == 0, k == KD - 1)
                last.then_inc(gate_done, 1)
                pe.wait_ge(h_done, n + 1)
                for k in range(KD):
                    last = matmul3(nc, pu[r % 2][:], wu_hi[:, k, cols], wu_lo[:, k, cols],
                                   g.x_hi[:, k, ds(b * SEQ, SEQ)], g.x_lo[:, k, ds(b * SEQ, SEQ)],
                                   k == 0, k == KD - 1)
                last.then_inc(up_done, 1)

        def down(pe, b, p):
            pe.wait_ge(kept_done, (b + 1) * GT)
            if not (isinstance(b, int) and b < 2):
                pe.wait_ge(out_done, b - 1)
            for n in range(TPB):
                for s in range(SLOTS):
                    last = nc.tensor.matmul(pd[p][:, n, :], h[:, p, s, n * P:(n + 1) * P], wd[:, s, :],
                                            start=s == 0, stop=s == SLOTS - 1)
            last.then_inc(down_done, 1)

        @block.tensor
        def _(pe):
            pe.wait_ge(w_split, 4)
            pe.wait_ge(d_loaded, 16)
            gate_up(pe, 0, 0)
            gate_up(pe, 0, 1)
            gate_up(pe, 1, 0)
            down(pe, 0, 0)
            gate_up(pe, 1, 1)
            with pe.Fori(1, BATCH // 2) as i:
                for p in range(2):
                    b = i * 2 + p
                    gate_up(pe, b, 0)
                    down(pe, b - 1, 1 - p)
                    gate_up(pe, b, 1)
            down(pe, BATCH - 1, 1)

        @block.scalar
        def _(act):
            act.sem_inc(silu_done, 2)
            act.wait_ge(w_loaded, 16)
            nc.scalar.activation(wg_hi[:], raw[:], ACT.Copy).then_inc(w_split, 1)
            act.wait_ge(w_loaded, 32)
            nc.scalar.activation(wu_hi[:], raw[:], ACT.Copy).then_inc(w_split, 1)
            nc.scalar.preload_act_table(ACT.Silu)
            with act.Fori(0, BATCH // 2) as i:
              for p in range(2):
                b = i * 2 + p
                for s in range(SLOTS):
                    n = b * SLOTS + s
                    act.wait_ge(gate_done, n + 1)
                    act.wait_ge(h_done, n + 1)
                    nc.scalar.activation(silu[:, s % 2], pg[s % 2][:], ACT.Silu).then_inc(silu_done, 1)
                    act.wait_ge(h_done, n + 3)
                    if s % GROUP == 0:
                        act.wait_ge(kept_done, b * GT + s // GROUP)
                    nc.scalar.activation(mag[:, s % GROUP], h[:, p, s], ACT.Abs).then_inc(mag_done, 1)

        @block.vector
        def _(dve):
            dve.sem_inc(h_done, 2)
            dve.wait_ge(w_split, 1)
            nc.vector.tensor_tensor(wg_lo[:], raw[:], wg_hi[:].bitcast(FP32), ALU.subtract).then_inc(w_split, 1)
            dve.wait_ge(w_split, 3)
            nc.vector.tensor_tensor(wu_lo[:], raw[:], wu_hi[:].bitcast(FP32), ALU.subtract).then_inc(w_split, 1)
            PER = 6 + 8

            def group_tile(b, p, gt):
                link = Chain(dve, chain_sem, b * (PER * GT) + gt * PER)
                for r in range(GROUP):
                    n = b * SLOTS + gt * GROUP + r
                    s = gt * GROUP + r
                    dve.wait_ge(silu_done, n + 3)
                    dve.wait_ge(up_done, n + 1)
                    nc.vector.tensor_tensor(h[:, p, s], pu[r % 2][:], silu[:, r % 2], ALU.mult).then_inc(h_done, 1)
                pairs = [(0, 1), (0, 2), (0, 3), (1, 2), (1, 3), (2, 3)]
                dve.wait_ge(mag_done, (b * GT + gt + 1) * GROUP)
                for q, (i, j) in enumerate(pairs):
                    link.mark(nc.vector.tensor_tensor(beats[:, q], mag[:, i], mag[:, j], ALU.is_ge))
                link.wait()
                c01, c02, c03, c12, c13, c23 = (beats[:, q] for q in range(6))
                c = [count[:, r] for r in range(GROUP)]
                link.mark(nc.vector.tensor_tensor(c[0], c01, c02, ALU.add))
                link.mark(nc.vector.tensor_tensor(c[1], c12, c13, ALU.add))
                link.mark(nc.vector.tensor_tensor(c[2], c23, c12, ALU.subtract))
                link.mark(nc.vector.tensor_tensor(c[3], c23, c13, ALU.add))
                link.wait(link.n - 3)
                link.mark(nc.vector.tensor_tensor(c[0], c[0], c03, ALU.add))
                link.wait(link.n - 3)
                link.mark(nc.vector.tensor_tensor(c[1], c[1], c01, ALU.subtract))
                link.wait(link.n - 3)
                link.mark(nc.vector.tensor_tensor(c[2], c[2], c02, ALU.subtract))
                link.wait(link.n - 3)
                link.mark(nc.vector.tensor_tensor(c[3], c[3], c03, ALU.add))
                keep = [(ALU.is_ge, 2.0), (ALU.is_ge, 1.0), (ALU.is_ge, 0.0), (ALU.is_le, 1.0)]
                for r, (op, least) in enumerate(keep):
                    link.wait(link.n - 3 + r)
                    s = gt * GROUP + r
                    last = nc.vector.scalar_tensor_tensor(h[:, p, s], c[r], least, h[:, p, s], op, ALU.mult)
                last.then_inc(kept_done, 1)
                dve.wait_ge(kept_done, b * GT + gt + 1)
                assert link.n == PER

            def finish(b, p):
                dve.wait_ge(down_done, b + 1)
                dve.wait_ge(res_loaded[p], (b - p) * 8 + 16)
                dve.wait_ge(stored[p], (b - p) * 8 + 16)
                nc.vector.tensor_tensor(out[:, p], pd[p][:], res[:, p], ALU.add).then_inc(out_done, 1)

            group_tile(0, 0, 0)
            group_tile(0, 0, 1)
            group_tile(1, 1, 0)
            finish(0, 0)
            group_tile(1, 1, 1)
            with dve.Fori(1, BATCH // 2) as i:
                for p in range(2):
                    b = i * 2 + p
                    group_tile(b, p, 0)
                    finish(b - 1, 1 - p)
                    group_tile(b, p, 1)
            finish(BATCH - 1, 1)

H1, N1 = 64, 128
P1 = 8
DIN = H1 * P1
PAIRS = H1 // 2
PW = 2 * P1
COLS = TOK // 2 // P
CW = TOK // 2
UNITS = PAIRS * BATCH
TURN = 2.0 * math.pi
UNDER_TURN = 6.283185
MAGIC = 1.5 * 2.0 ** 23
RMS_EPS = 1e-6
WC = 5 * P
WCH = WC // BATCH

def gates(nc, ctx, w_d, alog_d, tk_dram, rows_dram, g):
    sem = lambda n: nc.alloc_semaphore(name=f"ga_{n}")
    loaded, w_split, z_done, z_taken, chain_sem, act_sem = (sem(n) for n in ("load", "split", "z", "ztaken", "chain", "act"))
    dve_to_act, turned, taken, stored, rows_ready = sem("dve2act"), sem("turned"), sem("taken"), sem("stored"), sem("rows")
    quantity = sem("quantity")
    with ExitStack() as mem:
        sb = lambda n, s, d=FP32: mem.enter_context(nc.sbuf_tensor(f"ga_{n}", s, d))
        raw = sb("raw", [P, KD, 2, 2, P])
        w_hi, w_lo = sb("whi", [P, KD, 2, 2, P], FP32R), sb("wlo", [P, KD, 2, 2, P], FP32R)
        ea = sb("ea", [P, 1])
        z, lam, dt, kap, gam, tmp = (sb(n, [P, CW]) for n in ("z", "lam", "dt", "kap", "gam", "tmp"))
        cum, keep = sb("cum", [P, CW]), sb("keep", [P, CW])
        part = sb("part", [P, 3, 2, CW], BF16)
        tk = sb("tk", [P, PAIRS, 4, 2, COLS, 2])
        ps = lambda n, s: mem.enter_context(nc.psum_tensor(f"ga_{n}", s, FP32))
        pz = [ps(f"z{i}", [P, SEQ]) for i in range(2)]
        pt = [ps(f"t{i}", [P, 4, P]) for i in range(2)]
        block = mem.enter_context(nc.Block())
        PB = BATCH // 2

        @block.sync
        def _(sp):
            sp.dma_start(raw[:], w_d).then_inc(loaded, 16)
            sp.dma_start(ea[:], alog_d).then_inc(loaded, 16)
            sp.wait_ge(rows_ready, 1)
            sp.dma_start(rows_dram.rearrange("(r s) q c -> r s q c", s=3), part[:]).then_inc(stored, 16)
            sp.wait_ge(taken, 16 * 2)
            sp.dma_start(tk_dram.rearrange("a p c -> p a c"), tk[:].rearrange("p a q j c h -> p a (q j c h)")).then_inc(stored, 16)
            sp.wait_ge(stored, 32)

        @block.tensor
        def _(pe):
            pe.wait_ge(w_split, 2)
            for n in range(2 * PB):
                q, c = divmod(n, PB)
                if n >= 2:
                    pe.wait_ge(z_taken, n - 1)
                for j in range(2):
                    for k in range(KD):
                        tok = slice((2 * c + j) * SEQ, (2 * c + j + 1) * SEQ)
                        last = matmul3(nc, pz[n % 2][:], w_hi[:, k, q, j, :], w_lo[:, k, q, j, :], g.x_hi[:, k, tok],
                                       g.x_lo[:, k, tok], j == 0 and k == 0, j == 1 and k == KD - 1)
                last.then_inc(z_done, 1)
            for n in range(16):
                q, f = divmod(n, 4)
                if n == 0:
                    pe.wait_ge(quantity, 3)
                if n >= 2:
                    pe.wait_ge(taken, 2 * (n - 1))
                for c in range(4):
                    col = f * 4 + c
                    last = nc.tensor.transpose(pt[n % 2][:, c, :], (kap, tmp, gam, lam)[q][:, col * P:(col + 1) * P], g.ident[:])
                last.then_inc(turned, 1)

        @block.scalar
        def _(act):
            A = nc.scalar.activation
            for n in range(2 * PB):
                q, c = divmod(n, PB)
                act.wait_ge(z_done, n + 1)
                A((z, lam)[q][:, c * SEQ:(c + 1) * SEQ], pz[n % 2][:], ACT.Copy).then_inc(z_taken, 1)
            act.wait_ge(z_taken, 2 * PB)
            act.wait_ge(loaded, 32)
            A(lam[:], lam[:], ACT.Sigmoid).then_inc(act_sem, 1)
            A(dt[:], z[:], ACT.Abs).then_inc(act_sem, 1)
            A(ea[:], ea[:], ACT.Exp).then_inc(act_sem, 1)
            act.wait_ge(act_sem, 3)
            A(dt[:], dt[:], ACT.Exp, scale=-1.0).then_inc(act_sem, 1)
            act.wait_ge(act_sem, 4)
            A(dt[:], dt[:], ACT.Ln, bias=1.0).then_inc(act_sem, 1)
            act.wait_ge(dve_to_act, 1)
            A(tmp[:], tmp[:], ACT.Exp).then_inc(act_sem, 1)
            act.wait_ge(dve_to_act, 2)
            A(lam[:], cum[:], ACT.Exp).then_inc(quantity, 1)
            for n in range(16):
                q, f = divmod(n, 4)
                act.wait_ge(turned, n + 1)
                for j in range(2):
                    A(tk[:, :, q, j, f * 4:f * 4 + 4, :],
                      pt[n % 2][:, :, j * H1:(j + 1) * H1].rearrange("p c (a h) -> p a c h", h=2),
                      ACT.Copy).then_inc(taken, 1)

        @block.vector
        def _(dve):
            V = nc.vector
            link = Chain(dve, chain_sem)
            dve.wait_ge(loaded, 32)
            V.tensor_copy(w_hi[:], raw[:]).then_inc(w_split, 1)
            dve.wait_ge(w_split, 1)
            V.tensor_tensor(w_lo[:], raw[:], w_hi[:].bitcast(FP32), ALU.subtract).then_inc(w_split, 1)
            link(V.memset(keep[:], 1.0))
            link(V.memset(keep[:].rearrange("p (c t) -> p c t", t=P)[:, :, 0:1], 0.0))
            dve.wait_ge(act_sem, 5)
            link(V.scalar_tensor_tensor(dt[:], z[:], 0.0, dt[:], ALU.max, ALU.add))
            link.mark(V.tensor_tensor(gam[:], lam[:], dt[:], ALU.mult))
            link(V.tensor_scalar(z[:], dt[:], ea[:, 0:1], -1.0, ALU.mult, ALU.mult))
            link.mark(V.tensor_tensor_scan(cum[:], keep[:], z[:], 0.0, ALU.mult, ALU.add))
            link.mark(V.tensor_tensor(tmp[:], dt[:], gam[:], ALU.subtract))
            link.wait()
            link.mark(V.tensor_tensor(kap[:, 0:CW - 1], gam[:, 0:CW - 1], tmp[:, 1:CW], ALU.add))
            link(V.tensor_copy(kap[:, CW - 1:CW], gam[:, CW - 1:CW]))
            chunks = cum[:].rearrange("p (c t) -> p c t", t=P)
            ends = chunks[:, :, P - 1:P].broadcast_to([P, COLS, P])
            V.tensor_tensor(tmp[:].rearrange("p (c t) -> p c t", t=P), ends, chunks, ALU.subtract).then_inc(dve_to_act, 1)
            link(V.tensor_scalar(z[:], kap[:], 1e-37, None, ALU.max))
            link(V.reciprocal(z[:], z[:]))
            V.tensor_tensor(gam[:], gam[:], z[:], ALU.mult).then_inc(quantity, 1)
            dve.wait_ge(act_sem, 6)
            V.tensor_tensor(tmp[:], tmp[:], kap[:], ALU.mult).then_inc(quantity, 1)
            link(V.tensor_scalar(dt[:], dt[:], 1.0 / TURN, None, ALU.mult))
            nc.vector.tensor_copy(keep[:], cum[:]).then_inc(dve_to_act, 1)
            dve.wait_ge(dve_to_act, 2)
            for q, v in enumerate((dt, keep)):
                for s in range(2):
                    link(V.tensor_copy(part[:, s, q, :], v[:]))
                    link(V.tensor_tensor(v[:], v[:], part[:, s, q, :], ALU.subtract))
                last = V.tensor_copy(part[:, 2, q, :], v[:])
                if q == 0:
                    link(last)
            last.then_inc(rows_ready, 1)

def input_projection(nc, ctx, w_d, xp_dram, g):
    sem = lambda n: nc.alloc_semaphore(name=f"xp_{n}")
    loaded, w_split, staged, done, taken = sem("load"), sem("split"), sem("staged"), sem("done"), sem("taken")
    stored = [sem("st0"), sem("st1")]
    with ExitStack() as mem:
        sb = lambda n, s, d=FP32: mem.enter_context(nc.sbuf_tensor(f"xp_{n}", s, d))
        raw = sb("raw", [P, KD, DIN])
        w_hi, w_lo = sb("whi", [P, KD, DIN], FP32R), sb("wlo", [P, KD, DIN], FP32R)
        s_hi, s_lo = sb("shi", [P, 2, KD, P], FP32R), sb("slo", [P, 2, KD, P], FP32R)
        out = sb("outt", [P, 2, DIN])
        px = [mem.enter_context(nc.psum_tensor(f"xp_ps{i}", [P, DIN], FP32)) for i in range(2)]
        block = mem.enter_context(nc.Block())
        xp_v = xp_dram.rearrange("(n p) d -> n p d", p=P)

        @block.sync
        def _(sp):
            sp.dma_start(raw[:], w_d).then_inc(loaded, 16)
            with sp.Fori(0, TILES // 2) as i:
                for p in range(2):
                    t = i * 2 + p
                    sp.wait_ge(taken, t + 3)
                    sp.dma_start(xp_v[ds(t, 1)].rearrange("a p d -> p (a d)"), out[:, p]).then_inc(stored[p], 16)
            for p in range(2):
                sp.wait_ge(stored[p], 16 * (TILES // 2))

        @block.vector
        def _(dve):
            dve.wait_ge(loaded, 16)
            nc.vector.tensor_copy(w_hi[:], raw[:]).then_inc(w_split, 1)
            dve.wait_ge(w_split, 1)
            nc.vector.tensor_tensor(w_lo[:], raw[:], w_hi[:].bitcast(FP32), ALU.subtract).then_inc(w_split, 1)
            with dve.Fori(0, TILES // 2) as i:
                for p in range(2):
                    t = i * 2 + p
                    dve.wait_ge(done, t + 1)
                    cols = ds(t * P, P)
                    nc.vector.tensor_copy(s_hi[:, p], g.x_hi[:, :, cols].bitcast(FP32))
                    nc.vector.tensor_copy(s_lo[:, p], g.x_lo[:, :, cols].bitcast(FP32)).then_inc(staged, 1)

        @block.tensor
        def _(pe):
            pe.sem_inc(done, 2)
            pe.wait_ge(w_split, 2)
            with pe.Fori(0, TILES // 2) as i:
                for p in range(2):
                    t = i * 2 + p
                    pe.wait_ge(staged, t + 1)
                    pe.wait_ge(taken, t + 1)
                    for k in range(KD):
                        last = matmul3(nc, px[p][:], s_hi[:, p, k], s_lo[:, p, k], w_hi[:, k], w_lo[:, k],
                                       k == 0, k == KD - 1)
                    last.then_inc(done, 1)

        @block.scalar
        def _(act):
            act.sem_inc(taken, 2)
            with act.Fori(0, TILES // 2) as i:
                for p in range(2):
                    t = i * 2 + p
                    act.wait_ge(done, t + 3)
                    act.wait_ge(stored[p], 16 * i)
                    nc.scalar.activation(out[:, p], px[p][:], ACT.Copy).then_inc(taken, 1)

def output_projection(nc, ctx, src, dst, wz_d, wout_d, y_dram, g):
    sem = lambda n: nc.alloc_semaphore(name=f"op_{n}")
    loaded, w_split, staged, z_done, silu_done, gated = (sem(n) for n in ("load", "split", "staged", "z", "silu", "gated"))
    turned, yt_ready, out_done, added = sem("turned"), sem("yt"), sem("outd"), sem("added")
    stored = [sem("st0"), sem("st1")]
    in_y, in_x = [sem("iny0"), sem("iny1")], [sem("inx0"), sem("inx1")]
    KO = DIN // P
    with ExitStack() as mem:
        sb = lambda n, s, d=FP32: mem.enter_context(nc.sbuf_tensor(f"op_{n}", s, d))
        raw = sb("raw", [P, KD, DIN])
        w_hi, w_lo = sb("whi", [P, KD, DIN], FP32R), sb("wlo", [P, KD, DIN], FP32R)
        wo = sb("wo", [P, KO, DM])
        s_hi, s_lo = sb("shi", [P, 2, KD, P], FP32R), sb("slo", [P, 2, KD, P], FP32R)
        y, silu, yt, out = sb("y", [P, 2, DIN]), sb("silu", [P, 2, DIN]), sb("yt", [P, 2, KO, P]), sb("outt", [P, 2, DM])
        ps = lambda n, s: [mem.enter_context(nc.psum_tensor(f"op_ps{n}{i}", s, FP32)) for i in range(2)]
        pz, pt, po = ps("z", [P, DIN]), ps("t", [P, KO, P]), ps("o", [P, DM])
        block = mem.enter_context(nc.Block())
        y_v = y_dram.rearrange("(n p) d -> n p d", p=P)
        src_v = src.rearrange("(n p) d -> n p d", p=P)
        dst_v = dst.rearrange("(n p) d -> n p d", p=P)

        @block.sync
        def _(sp):
            sp.dma_start(raw[:], wz_d).then_inc(loaded, 16)
            sp.dma_start(wo[:], wout_d).then_inc(loaded, 16)
            with sp.Fori(0, TILES // 2) as i:
                for p in range(2):
                    t = i * 2 + p
                    sp.wait_ge(turned, i * 2)
                    sp.dma_start(y[:, p], y_v[ds(t, 1)].rearrange("a p d -> p (a d)")).then_inc(in_y[p], 16)
                    sp.wait_ge(stored[p], 16 * i)
                    sp.dma_start(out[:, p], src_v[ds(t, 1)].rearrange("a p d -> p (a d)")).then_inc(in_x[p], 16)
                for p in range(2):
                    t = i * 2 + p
                    sp.wait_ge(added, t + 1)
                    sp.dma_start(dst_v[ds(t, 1)].rearrange("a p d -> p (a d)"), out[:, p]).then_inc(stored[p], 16)
            for p in range(2):
                sp.wait_ge(stored[p], 16 * (TILES // 2))

        @block.gpsimd
        def _(pool):
            with pool.Fori(0, TILES // 2) as i:
                for p in range(2):
                    t = i * 2 + p
                    pool.wait_ge(z_done, i * 2)
                    cols = ds(t * P, P)
                    nc.gpsimd.tensor_copy(s_hi[:, p], g.x_hi[:, :, cols].bitcast(FP32))
                    nc.gpsimd.tensor_copy(s_lo[:, p], g.x_lo[:, :, cols].bitcast(FP32)).then_inc(staged, 1)

        @block.tensor
        def _(pe):
            pe.wait_ge(w_split, 2)
            pe.wait_ge(loaded, 32)
            with pe.Fori(0, TILES // 2) as i:
                for p in range(2):
                    t = i * 2 + p
                    pe.wait_ge(staged, t + 1)
                    pe.wait_ge(silu_done, i * 2)
                    for k in range(KD):
                        last = matmul3(nc, pz[p][:], s_hi[:, p, k], s_lo[:, p, k], w_hi[:, k], w_lo[:, k],
                                       k == 0, k == KD - 1)
                    last.then_inc(z_done, 1)
                for p in range(2):
                    t = i * 2 + p
                    pe.wait_ge(gated, t + 1)
                    pe.wait_ge(yt_ready, i * 2)
                    for k in range(KO):
                        last = nc.tensor.transpose(pt[p][:, k, :], y[:, p, k * P:(k + 1) * P], g.ident[:])
                    last.then_inc(turned, 1)
                for p in range(2):
                    t = i * 2 + p
                    pe.wait_ge(yt_ready, t + 1)
                    pe.wait_ge(added, i * 2)
                    for k in range(KO):
                        last = nc.tensor.matmul(po[p][:], yt[:, p, k, :], wo[:, k, :], start=k == 0, stop=k == KO - 1)
                    last.then_inc(out_done, 1)

        @block.scalar
        def _(act):
            A = nc.scalar.activation
            act.wait_ge(loaded, 32)
            A(w_hi[:], raw[:], ACT.Copy).then_inc(w_split, 1)
            nc.scalar.preload_act_table(ACT.Silu)
            with act.Fori(0, TILES // 2) as i:
                for p in range(2):
                    t = i * 2 + p
                    act.wait_ge(z_done, t + 1)
                    act.wait_ge(gated, i * 2)
                    A(silu[:, p], pz[p][:], ACT.Silu).then_inc(silu_done, 1)
                for p in range(2):
                    t = i * 2 + p
                    act.wait_ge(turned, t + 1)
                    act.wait_ge(out_done, i * 2)
                    A(yt[:, p], pt[p][:], ACT.Copy).then_inc(yt_ready, 1)

        @block.vector
        def _(dve):
            dve.wait_ge(w_split, 1)
            nc.vector.tensor_tensor(w_lo[:], raw[:], w_hi[:].bitcast(FP32), ALU.subtract).then_inc(w_split, 1)
            with dve.Fori(0, TILES // 2) as i:
                for p in range(2):
                    t = i * 2 + p
                    dve.wait_ge(silu_done, t + 1)
                    dve.wait_ge(in_y[p], 16 * i + 16)
                    nc.vector.tensor_tensor(y[:, p], y[:, p], silu[:, p], ALU.mult).then_inc(gated, 1)
                for p in range(2):
                    t = i * 2 + p
                    dve.wait_ge(out_done, t + 1)
                    dve.wait_ge(in_x[p], 16 * i + 16)
                    nc.vector.tensor_tensor(out[:, p], po[p][:], out[:, p], ALU.add).then_inc(added, 1)

def state_space(nc, ctx, w_dram, norm_d, bias_d, const_d, strict_d, blocks_d, tk_dram, rows_dram, xp_dram, y_dram, g):
    sem = lambda n: nc.alloc_semaphore(name=f"ss_{n}")
    const_in, const_ready = sem("constin"), sem("constready")
    rows_in, wraw_in, pair_in = [sem("rows0"), sem("rows1")], [sem("wraw0"), sem("wraw1")], [sem("pair0"), sem("pair1")]
    y_out = [sem("yout0"), sem("yout1")]
    w_split = sem("wsplit")
    dtb_done, th_done, bc_done, e_done, ss_done, g_done = (sem(n) for n in ("dtb", "th", "bc", "e", "ss", "g"))
    t_done, u_done, yp_done = sem("t"), sem("u"), sem("yp")
    dtb_copied, xw_done, d_done, r_done, bt_done, trig_done, abs_done = (sem(n) for n in ("dtbc", "xw", "d", "r", "bt", "trig", "abs"))
    ln_done = sem("ln")
    thdt_done, fr_done, rope_b, rope_c, gm_done, s_ready, y_ready, chain_sem = (
        sem(n) for n in ("thdt", "fr", "ropeb", "ropec", "gm", "sready", "yready", "chain"))
    sq_done, xk_done, dd_done, um_done, yb_done, pool_chain = (sem(n) for n in ("sq", "xk", "dd", "um", "yb", "pchain"))
    with ExitStack() as mem:
        sb = lambda n, s, d=FP32: mem.enter_context(nc.sbuf_tensor(f"ss_{n}", s, d))
        w_hi, w_lo = sb("whi", [P, 2, KD, WC], FP32R), sb("wlo", [P, 2, KD, WC], FP32R)
        w_raw = sb("wraw", [P, 2, KD, WCH])
        xp = sb("xp", [P, 2, TILES, PW])
        tk = sb("tk", [P, 2, 4, 2, COLS * 2])
        yo = sb("yo", [P, 2, TILES, PW])
        rows = sb("rows", [6, 2, 2, SEQ], BF16)
        norm = sb("norm", [P, 4])
        bias = sb("bias", [P, PAIRS, 4])
        con_f, con = sb("conf", [6, 5, P]), sb("con", [6, 5, P], BF16)
        strict_f, strict = sb("strictf", [P, P]), sb("strict", [P, 4, P], BF16)
        blocks = sb("blocks", [P, PW])
        eps, quarter = sb("eps", [P, 1]), sb("quarter", [P, 1])
        dtb, th, fr = sb("dtb", [P, SEQ]), sb("th", [P, SEQ]), sb("fr", [P, SEQ])
        sin, cos = sb("sin", [P, 2, SEQ]), sb("cos", [P, 2, SEQ])
        sq = sb("sq", [P, 4, SEQ])
        xw = sb("xw", [P, 2, 4, SEQ])
        r = sb("r", [P, 2, SEQ])
        tmp = sb("tmp", [P, 4, SEQ])
        rot = sb("rot", [P, 2, 4, SEQ])
        dec = sb("dec", [P, 2, 8, P])
        pairs_sum = sb("pairssum", [P, P])
        ones = sb("ones", [P, SEQ])
        own = sb("own", [P, 8, P])
        gm = sb("gm", [P, 8, P])
        bt = sb("bt", [P, 3, 2, P])
        xk, xe = sb("xk", [P, 2, TPB, PW]), sb("xe", [P, 2, TPB, PW])
        aend = sb("aend", [P, 2, TPB])
        state = sb("state", [P, 3, 2 * PW])
        inter = sb("inter", [P, 3, PW])
        ps = lambda n, s: mem.enter_context(nc.psum_tensor(f"ss_ps{n}", s, FP32))
        ring = [ps(f"r{i}", [P, SEQ]) for i in range(3)]
        pe_g = ps("eg", [P, 8, P])
        p_st = ps("st", [P, 8, P])
        p_u = ps("u", [P, SEQ])
        p_y = p_st[:, 6:8, :].rearrange("p a b -> p (a b)")
        y_in, y_far = p_y[:, 0:TPB * PW], p_y[:, TPB * PW:(2 * TPB - 1) * PW]
        p_ae = p_u[:, 256:256 + TPB]
        block = mem.enter_context(nc.Block())
        xp_v = xp_dram.rearrange("(t p) (a c) -> a p t c", p=P, c=PW)
        y_v = y_dram.rearrange("(t p) (a c) -> a p t c", p=P, c=PW)
        at_start = 12 + 1
        HP = H1

        @block.sync
        def _(sp):
            for dst, s in ((norm, norm_d), (bias, bias_d), (con_f, const_d), (strict_f, strict_d), (blocks, blocks_d)):
                sp.dma_start(dst[:], s).then_inc(const_in, 16)

            def load_pair(pair, par):
                sp.dma_start(xp[:, par], xp_v[ds(pair, 1)].rearrange("a p t c -> p (a t) c")).then_inc(pair_in[par], 16)
                sp.dma_start(tk[:, par].rearrange("p q j c -> p (q j c)"),
                             tk_dram[ds(pair, 1)].rearrange("a p c -> p (a c)")).then_inc(pair_in[par], 16)

            def load_chunk(pair, b, j):
                sp.dma_start(w_raw[:, j], w_dram[ds(pair, 1), :, :, ds(b * WCH, WCH)]
                             .rearrange("a p k c -> p (a k) c")).then_inc(wraw_in[j], 16)

            load_pair(0, 0)
            for b in range(BATCH):
                if b >= 2:
                    sp.wait_ge(w_split, b - 1)
                load_chunk(0, b, b % 2)
            def turns(pair, nxt, i):
                for j in range(2):
                    u = pair * BATCH + i * 2 + j
                    sp.wait_ge(w_split, u + 7)
                    load_chunk(nxt, i * 2 + j, j)
                    sp.wait_ge(e_done, u)
                    sp.dma_start(rows[:, j], rows_dram[ds((j * H1 + pair * 2) * 3, 6), :, ds(i * SEQ, SEQ)])\
                      .then_inc(rows_in[j], 16)

            with sp.Fori(0, PAIRS // 2) as pp:
                for par in range(2):
                    pair = pp * 2 + par
                    nxt = (pair + 1) % PAIRS
                    turns(pair, nxt, 0)
                    sp.wait_ge(y_ready, pair * BATCH + 1)
                    load_pair(nxt, 1 - par)
                    sp.dma_start(y_v[ds((pair + PAIRS - 1) % PAIRS, 1)].rearrange("a p t c -> p (a t) c"),
                                 yo[:, 1 - par]).then_inc(y_out[1 - par], 16)
                    with sp.Fori(1, BATCH // 2) as i:
                        turns(pair, nxt, i)
            sp.wait_ge(y_ready, UNITS + 1)
            sp.dma_start(y_v[PAIRS - 1], yo[:, 1]).then_inc(y_out[1], 16)
            sp.wait_ge(y_out[0], 16 * (PAIRS // 2))
            sp.wait_ge(y_out[1], 16 * (PAIRS // 2 + 1))
            for j in range(2):
                sp.wait_ge(pair_in[j], 32 * (PAIRS // 2 + (1 - j)))

        @block.gpsimd
        def _(pool):
            G = nc.gpsimd
            G.memset(rot[:, 1], 0.0).then_inc(const_ready, 1)
            G.memset(dec[:, 1], 0.0).then_inc(const_ready, 1)
            G.memset(xk[:, 1], 0.0).then_inc(const_ready, 1)
            G.memset(xe[:, 1], 0.0).then_inc(const_ready, 1)
            G.memset(aend[:, 1], 0.0).then_inc(const_ready, 1)
            G.memset(tk[:, 1], 0.0).then_inc(const_ready, 1)
            G.memset(yo[:, 1], 0.0).then_inc(const_ready, 1)

            for b in range(BATCH):
                pool.wait_ge(wraw_in[b % 2], 16 * (b // 2 + 1))
                cols = slice(b * WCH, (b + 1) * WCH)
                G.tensor_copy(w_hi[:, 0, :, cols], w_raw[:, b % 2]).then_inc(pool_chain, 1)
                pool.wait_ge(pool_chain, b + 1)
                G.tensor_tensor(w_lo[:, 0, :, cols], w_raw[:, b % 2], w_hi[:, 0, :, cols].bitcast(FP32),
                                ALU.subtract).then_inc(w_split, 1)
            pool.wait_ge(const_in, 16 * 5)
            with pool.Fori(0, UNITS // 2) as i:
                for j in range(2):
                    u = i * 2 + j
                    b, pair = u % BATCH, u // BATCH
                    par = pair % 2
                    for q in range(2):
                        pool.wait_ge(xw_done, 4 * u + 2 * q + 6)
                        pool.wait_ge(ss_done, 2 * u)
                        G.tensor_tensor(sq[:, 2 * q], sq[:, 2 * q], sq[:, 2 * q + 1], ALU.add).then_inc(sq_done, 1)
                    pool.wait_ge(wraw_in[j], (i + 5) * 16)
                    G.tensor_copy(w_hi[:, ds(1 - par, 1), :, ds(b * WCH, WCH)], w_raw[:, j:j + 1]).then_inc(pool_chain, 1)
                    pool.wait_ge(pool_chain, u + BATCH + 1)
                    G.tensor_tensor(w_lo[:, ds(1 - par, 1), :, ds(b * WCH, WCH)], w_raw[:, j:j + 1],
                                    w_hi[:, ds(1 - par, 1), :, ds(b * WCH, WCH)].bitcast(FP32), ALU.subtract)\
                     .then_inc(w_split, 1)
                    pool.wait_ge(pair_in[0], (pair // 2 + 1) * 32)
                    pool.wait_ge(pair_in[1], ((pair + 1) // 2) * 32)
                    pool.wait_ge(yp_done, u)
                    tk_of = lambda q: tk[:, ds(par, 1), q, j, ds((b // 2) * 8, 8)].rearrange("p a (g o) -> p (a g) o", o=1)
                    xp_u = xp[:, ds(par, 1), ds(b * TPB, TPB), :].rearrange("p a c (h d) -> p (a c h) d", d=P1)
                    G.tensor_tensor(xk[:, j].rearrange("p c (h d) -> p (c h) d", d=P1), xp_u,
                                    tk_of(0).broadcast_to([P, 8, P1]), ALU.mult)
                    G.tensor_tensor(xe[:, j].rearrange("p c (h d) -> p (c h) d", d=P1), xp_u,
                                    tk_of(1).broadcast_to([P, 8, P1]), ALU.mult).then_inc(xk_done, 1)
                    at_diagonal = tk[:, ds(par, 1), 2, j, ds((b // 2) * 8, 8)].rearrange("p a (c h o) -> p (a h) c o", h=2, o=1)
                    G.tensor_tensor(own[:].rearrange("p (h c) t -> p h c t", h=2),
                                    g.ident[:].rearrange("p (a o t) -> p a o t", a=1, o=1).broadcast_to([P, 2, TPB, P]),
                                    at_diagonal.broadcast_to([P, 2, TPB, P]), ALU.mult).then_inc(xk_done, 1)
                    pool.wait_ge(xk_done, 2 * u + 2)
                    pool.wait_ge(d_done, u + 1)
                    G.tensor_tensor(dec[:, j], dec[:, j], own[:], ALU.add).then_inc(dd_done, 1)
                    for e, op in ((0, ALU.subtract), (1, ALU.add)):
                        pool.wait_ge(rope_b, 2 * u + e + 1)
                        G.tensor_tensor(rot[:, j, e], rot[:, j, e], tmp[:, e], op).then_inc(yb_done, 1)

        @block.tensor
        def _(pe):
            M, T = nc.tensor.matmul, nc.tensor.transpose

            def project(n, w, wpar, b, k_tok=None):
                for k in range(KD):
                    cols = slice(w * P, (w + 1) * P)
                    tok = ds(b * SEQ, SEQ)
                    last = matmul3(nc, ring[n][:], w_hi[:, wpar, k, cols], w_lo[:, wpar, k, cols],
                                   g.x_hi[:, k, tok], g.x_lo[:, k, tok], k == 0, k == KD - 1)
                return last

            def scores(bank, j):
                for blk in range(4):
                    n = bank * 4 + blk
                    h, c = divmod(n, TPB)
                    at, cols = slice(h * HP, (h + 1) * HP), slice(c * P, (c + 1) * P)
                    for e in range(2):
                        last = M(pe_g[:, n, :], rot[at, j, e, cols], rot[at, j, 2 + e, cols], start=e == 0, stop=e == 1)
                return last

            def second(u, j, halves):
                pe.wait_ge(yb_done, 2 * u)
                pe.wait_ge(rope_c, 2 * u + 2)
                pe.wait_ge(xk_done, 2 * u)
                halves[0]()
                scores(0, j).then_inc(g_done, 1)
                halves[1]()
                scores(1, j).then_inc(g_done, 1)
                halves[2]()
                for c in range(3):
                    for e in range(2):
                        last = T(p_st[:, c * 2 + e, :], rot[:, j, e, c * P:(c + 1) * P], g.ident[:])
                last.then_inc(t_done, 1)
                pe.wait_ge(bt_done, u + 1)
                pe.wait_ge(s_ready, u)
                for c in range(3):
                    for e in range(2):
                        last = M(p_u[:, (c * 2 + e) * PW:(c * 2 + e + 1) * PW], bt[:, c, e, :], xe[:, j, c, :],
                                 start=True, stop=True)
                last.then_inc(u_done, 1)
                for half in range(2):
                    pe.wait_ge(gm_done, 2 * u + half + 1)
                    for blk in range(4):
                        cols = slice((blk * 2 + half) * P1, (blk * 2 + half + 1) * P1)
                        M(y_in[:, cols], gm[:, half * 4 + blk, :], xk[:, j, blk, half * P1:(half + 1) * P1],
                          start=True, stop=True)
                pe.wait_ge(s_ready, u + 1)
                for c in range(1, TPB):
                    for e in range(2):
                        last = M(y_far[:, (c - 1) * PW:c * PW], rot[:, j, 2 + e, c * P:(c + 1) * P],
                                 state[:, c - 1, e * PW:(e + 1) * PW], start=e == 0, stop=e == 1)
                last.then_inc(yp_done, 1)

            def turn(u, b, j, wpar, i):
                rw = rows[:, j]
                pe.wait_ge(rows_in[j], i)
                pe.wait_ge(xw_done, 4 * u + 2)
                M(ring[0][:], con[:, 0, :], rw[:, 0, :], start=True, stop=True).then_inc(dtb_done, 1)
                pe.wait_ge(xw_done, 4 * u + 3)
                project(1, 0, wpar, b).then_inc(th_done, 1)
                pe.wait_ge(xw_done, 4 * u + 4)
                project(2, 1, wpar, b).then_inc(bc_done, 1)
                pe.wait_ge(dtb_copied, u + 1)
                project(0, 2, wpar, b).then_inc(bc_done, 1)
                pe.wait_ge(gm_done, 2 * u)
                for half in range(2):
                    bank = pe_g[:, half * 4:half * 4 + 4, :]
                    M(bank.rearrange("p a b -> p (a b)"), g.ident16[:], strict[:].rearrange("p a b -> p (a b)"),
                      start=True, stop=False, skip_group_check=True)
                    for blk in range(4):
                        n = half * 4 + blk
                        h, c = divmod(n, TPB)
                        cols = slice(c * P, (c + 1) * P)
                        M(pe_g[:, n, :], con[:, 1 + h, :], rw[:, 1, cols], start=False, stop=False, skip_group_check=True)
                        M(pe_g[:, n, :], rw[:, 1, cols], con[:, 3 + h, :], start=False, stop=True, skip_group_check=True)
                pe.wait_ge(s_ready, u)
                M(p_ae, con[:, 0, :], rw[:, 1, :].rearrange("p (c t) -> p c t", t=P)[:, :, P - 1],
                  start=True, stop=True).then_inc(e_done, 1)
                pe.wait_ge(thdt_done, u + 1)
                project(1, 3, wpar, b).then_inc(bc_done, 1)
                pe.wait_ge(xw_done, 4 * u + 5)
                project(2, 4, wpar, b).then_inc(bc_done, 1)

                def squares(q):
                    pe.wait_ge(sq_done, 2 * u + q + 1)
                    pe.wait_ge(y_ready, u)
                    M(p_st[:, q * 4:q * 4 + 4, :].rearrange("p a b -> p (a b)"), pairs_sum[:], sq[:, 2 * q],
                      start=True, stop=True).then_inc(ss_done, 1)

                def before_first():
                    squares(0)
                    pe.wait_ge(d_done, u + 1)
                def before_second():
                    squares(1)
                def before_turn():
                    pe.wait_ge(ln_done, 2 * u + 2)
                second(u, 1 - j, (before_first, before_second, before_turn))

            pe.wait_ge(const_ready, at_start)
            pe.sem_inc(e_done, 1)
            with pe.Fori(0, PAIRS // 2) as pp:
                for par in range(2):
                    with pe.Fori(0, BATCH // 2) as i:
                        for j in range(2):
                            b = i * 2 + j
                            u = (pp * 2 + par) * BATCH + b
                            if j == 0:
                                pe.wait_ge(w_split, (pp * 2 + par + 1) * BATCH)
                            turn(u, b, j, par, ((pp * 2 + par) * (BATCH // 2) + i + 1) * 16)
            nothing = lambda: None
            second(UNITS, 1, (nothing, nothing, nothing))

        @block.scalar
        def _(act):
            A = nc.scalar.activation
            act.wait_ge(const_in, 16 * 5)
            act.wait_ge(const_ready, at_start)
            act.sem_inc(xw_done, 4)
            nc.scalar.preload_act_table(ACT.Exp)

            def take_b(u):
                act.wait_ge(t_done, u + 1)
                act.wait_ge(u_done, u)
                A(bt[:].rearrange("p c e t -> p (c e) t"), p_st[:, 0:6, :], ACT.Copy).then_inc(bt_done, 1)

            with act.Fori(0, UNITS // 2) as i:
                for j in range(2):
                    u = i * 2 + j
                    act.wait_ge(dtb_done, u + 1)
                    act.wait_ge(thdt_done, u)
                    A(dtb[:], ring[0][:], ACT.Copy).then_inc(dtb_copied, 1)

                    def tile(n, bank):
                        act.wait_ge(bc_done, 4 * u + n + 1)
                        if n == 0:
                            act.wait_ge(ss_done, 2 * u)
                            act.wait_ge(rope_c, 2 * u)
                        A(sq[:, n], ring[bank][:], ACT.Square)
                        A(xw[:, j, n], ring[bank][:], ACT.Identity, scale=norm[:, n:n + 1]).then_inc(xw_done, 1)
                    tile(0, 2)
                    tile(1, 0)
                    act.wait_ge(e_done, u + 2)
                    act.wait_ge(gm_done, 2 * u)
                    act.wait_ge(s_ready, u)
                    A(aend[:, j], p_ae, ACT.Exp)
                    A(dec[:, j], pe_g[:], ACT.Exp).then_inc(d_done, 1)
                    tile(2, 1)
                    tile(3, 2)
                    act.wait_ge(fr_done, u + 1)
                    A(sin[:, j], fr[:], ACT.Sin, scale=-UNDER_TURN)
                    A(cos[:, j], fr[:], ACT.Abs).then_inc(abs_done, 1)
                    act.wait_ge(abs_done, u + 1)
                    A(cos[:, j], cos[:, j], ACT.Sin, bias=quarter[:, 0:1], scale=-UNDER_TURN).then_inc(trig_done, 1)
                    for q in range(2):
                        act.wait_ge(ss_done, 2 * u + q + 1)
                        act.wait_ge(um_done, 2 * u)
                        A(r[:, q], p_st[:, q * 4:q * 4 + 4, :].rearrange("p a b -> p (a b)"), ACT.Ln,
                          scale=1.0 / N1, bias=eps[:, 0:1]).then_inc(ln_done, 1)
                    for q in range(2):
                        act.wait_ge(ln_done, 2 * u + q + 1)
                        A(r[:, q], r[:, q], ACT.Exp, scale=-0.5).then_inc(r_done, 1)
                    take_b(u)
            take_b(UNITS)

        @block.vector
        def _(dve):
            V = nc.vector
            dve.wait_ge(const_in, 16 * 5)
            V.tensor_copy(con[:], con_f[:]).then_inc(const_ready, 1)
            V.tensor_copy(strict[:], strict_f[:].rearrange("p (o t) -> p o t", o=1).broadcast_to([P, 4, P])).then_inc(const_ready, 1)
            V.memset(eps[:], RMS_EPS).then_inc(const_ready, 1)
            V.memset(quarter[:], math.pi / 2).then_inc(const_ready, 1)
            V.memset(ones[:], 1.0).then_inc(const_ready, 1)
            V.tensor_copy(pairs_sum[:].rearrange("p (h d) -> p h d", d=HP),
                          blocks[:].rearrange("p (h d) -> p h d", d=P1)[:, :, 0:1].broadcast_to([P, 2, HP])).then_inc(const_ready, 1)
            dve.wait_ge(const_ready, at_start)
            dve.sem_inc(rope_c, 2)
            PER = 7

            def masked(u, j):
                dve.wait_ge(dd_done, u)
                for half in range(2):
                    dve.wait_ge(g_done, 2 * u + half + 1)
                    if half == 0:
                        dve.wait_ge(yp_done, u)
                    at = slice(half * 4, half * 4 + 4)
                    V.tensor_tensor(gm[:, at, :], pe_g[:, at, :], dec[:, j, at, :], ALU.mult).then_inc(gm_done, 1)

            def states(u, j, link):
                dve.wait_ge(u_done, u + 1)
                link(V.tensor_tensor(state[:].rearrange("p c (e d) -> p (c e) d", d=PW),
                                     p_u[:, 0:6 * PW].rearrange("p (g d) -> p g d", d=PW),
                                     blocks[:].rearrange("p (o d) -> p o d", o=1).broadcast_to([P, 6, PW]), ALU.mult))
                link(V.scalar_tensor_tensor(state[:, 1], state[:, 0], aend[:, j, 1:2], state[:, 1], ALU.mult, ALU.add))
                V.scalar_tensor_tensor(state[:, 2], state[:, 1], aend[:, j, 2:3], state[:, 2], ALU.mult, ALU.add)\
                 .then_inc(s_ready, 1)

            def combine(u, par, b, j, link):
                dve.wait_ge(yp_done, u + 1)
                el = tk[:, ds(par, 1), 3, j, ds((b // 2) * 8 + 2, 6)].rearrange("p a (g o) -> p (a g) o", o=1)
                link(V.tensor_tensor(inter[:].rearrange("p c (h d) -> p (c h) d", d=P1),
                                     y_far.rearrange("p (g d) -> p g d", d=P1),
                                     el.broadcast_to([P, 6, P1]), ALU.mult))
                V.tensor_copy(yo[:, ds(par, 1), ds(b * TPB, 1), :], y_in[:, 0:PW].rearrange("p (a c d) -> p a c d", a=1, c=1))
                V.tensor_tensor(yo[:, ds(par, 1), ds(b * TPB + 1, TPB - 1), :],
                                y_in[:, PW:TPB * PW].rearrange("p (a c d) -> p a c d", a=1, d=PW),
                                inter[:].rearrange("p (a c) d -> p a c d", a=1), ALU.add).then_inc(y_ready, 1)

            with dve.Fori(0, UNITS // 2) as i:
                for j in range(2):
                    u = i * 2 + j
                    pair = u // BATCH
                    before = (u + UNITS - 1) % UNITS
                    bpar, bb = (before // BATCH) % 2, before % BATCH
                    link = Chain(dve, chain_sem, u * PER)
                    dve.wait_ge(dtb_copied, u + 1)
                    dve.wait_ge(th_done, u + 1)
                    V.tensor_tensor(th[:], ring[1][:], dtb[:], ALU.mult).then_inc(thdt_done, 1)
                    dve.wait_ge(thdt_done, u + 1)
                    link(V.tensor_tensor_scan(th[:], ones[:], th[:], 0.0, ALU.mult, ALU.add))
                    dve.wait_ge(trig_done, u)
                    link(V.tensor_scalar(fr[:], th[:], MAGIC, None, ALU.add))
                    V.scalar_tensor_tensor(fr[:], fr[:], MAGIC, th[:], ALU.subtract, ALU.subtract).then_inc(fr_done, 1)
                    masked(u, 1 - j)
                    states(u, 1 - j, link)
                    dve.wait_ge(trig_done, u + 1)
                    for q in range(2):
                        dve.wait_ge(r_done, 2 * u + q + 1)
                        if q == 0:
                            dve.wait_ge(yb_done, 2 * u)
                        x0, x1 = xw[:, j, 2 * q], xw[:, j, 2 * q + 1]
                        V.tensor_tensor(x0, x0, r[:, q], ALU.mult)
                        V.tensor_tensor(x1, x1, r[:, q], ALU.mult).then_inc(um_done, 1)
                        dve.wait_ge(um_done, 2 * u + q + 1)
                        b0 = bias[:, ds(pair, 1), 2 * q]
                        b1 = bias[:, ds(pair, 1), 2 * q + 1]
                        dve.wait_ge(yp_done, u)
                        S = V.scalar_tensor_tensor
                        S(rot[:, j, 2 * q], x0, b0, cos[:, j], ALU.add, ALU.mult)
                        a = S(tmp[:, 2 * q], x1, b1, sin[:, j], ALU.add, ALU.mult)
                        if q == 0:
                            a.then_inc(rope_b, 1)
                        else:
                            link.mark(a)
                        S(rot[:, j, 2 * q + 1], x0, b0, sin[:, j], ALU.add, ALU.mult)
                        a = S(tmp[:, 2 * q + 1], x1, b1, cos[:, j], ALU.add, ALU.mult)
                        if q == 0:
                            a.then_inc(rope_b, 1)
                            for s in range(2):
                                dve.wait_ge(y_out[s], ((u + 7) // 16) * 16)
                            combine(u, bpar, bb, 1 - j, link)
                        else:
                            link.mark(a)
                            link.wait(link.n - 1)
                            V.tensor_tensor(rot[:, j, 2], rot[:, j, 2], tmp[:, 2], ALU.subtract).then_inc(rope_c, 1)
                            link.wait()
                            V.tensor_tensor(rot[:, j, 3], rot[:, j, 3], tmp[:, 3], ALU.add).then_inc(rope_c, 1)
                    n_ = link.n
            assert n_ == PER, n_
            link = Chain(dve, chain_sem, UNITS * PER)
            masked(UNITS, 1)
            states(UNITS, 1, link)
            combine(UNITS, 1, BATCH - 1, 1, link)

E1, I1 = 8, 176
WIDE = E1 * I1
ET = WIDE // P

def route(nc, ctx, gate_d, below_d, g):
    sem = lambda n: nc.alloc_semaphore(name=f"rt_{n}")
    loaded, w_split, logit_done, logit_out = sem("load"), sem("wsplit"), sem("logit"), sem("logitout")
    turned, taken, chain_sem, exp_ready, exp_done = sem("turned"), sem("taken"), sem("chain"), sem("expready"), sem("exp")
    staged, back, back_used, cleared = sem("staged"), sem("back"), sem("backused"), sem("cleared")
    with ExitStack() as mem:
        sb = lambda n, s, d=FP32: mem.enter_context(nc.sbuf_tensor(f"rt_{n}", s, d))
        raw, w_hi, w_lo = sb("raw", [P, KD, E1]), sb("whi", [P, KD, E1], FP32R), sb("wlo", [P, KD, E1], FP32R)
        below = sb("below", [P, E1, E1])
        lg = sb("lg", [E1, 2, SEQ])
        prob = sb("prob", [P, TILES, E1])
        top, total = sb("top", [P, TILES]), sb("total", [P, TILES])
        ge, gt = sb("ge", [P, TILES, E1, E1]), sb("gt", [P, TILES, E1, E1])
        rank = sb("rank", [P, TILES, E1])
        stage = sb("stage", [P, 2, TPB, E1])
        rest, part = sb("rest", [E1, 2, SEQ]), sb("part", [E1, 2, SEQ], BF16)
        ps = lambda n, s: mem.enter_context(nc.psum_tensor(f"rt_{n}", s, FP32))
        pl = [ps(f"pl{i}", [E1, SEQ]) for i in range(2)]
        pt = [ps(f"pt{i}", [P, TPB, E1]) for i in range(2)]
        pc = [ps(f"pc{i}", [E1, SEQ]) for i in range(2)]
        block = mem.enter_context(nc.Block())

        @block.sync
        def _(sp):
            sp.dma_start(raw[:], gate_d).then_inc(loaded, 16)
            sp.dma_start(below[:], below_d).then_inc(loaded, 16)

        @block.gpsimd
        def _(pool):
            nc.gpsimd.memset(g.combine[:], 0.0).then_inc(cleared, 1)

        @block.tensor
        def _(pe):
            pe.wait_ge(w_split, 2)
            with pe.Fori(0, BATCH // 2) as i:
                for p in range(2):
                    b = i * 2 + p
                    pe.wait_ge(logit_out, b + 1)
                    for k in range(KD):
                        last = matmul3(nc, pl[p][:], w_hi[:, k, :], w_lo[:, k, :], g.x_hi[:, k, ds(b * SEQ, SEQ)],
                                       g.x_lo[:, k, ds(b * SEQ, SEQ)], k == 0, k == KD - 1)
                    last.then_inc(logit_done, 1)
                for p in range(2):
                    b = i * 2 + p
                    pe.wait_ge(logit_out, b + 3)
                    pe.wait_ge(taken, b + 1)
                    for n in range(TPB):
                        last = nc.tensor.matmul(pt[p][:, n, :], lg[:, p, n * P:(n + 1) * P], g.ident[0:E1, 0:E1],
                                                start=True, stop=True)
                    last.then_inc(turned, 1)
            with pe.Fori(0, BATCH // 2) as i:
                for p in range(2):
                    b = i * 2 + p
                    pe.wait_ge(staged, b + 1)
                    pe.wait_ge(back_used, i * 2)
                    for n in range(TPB):
                        last = nc.tensor.transpose(pc[p][:, n * P:(n + 1) * P], stage[:, p, n, :], g.ident[:])
                    last.then_inc(back, 1)

        @block.scalar
        def _(act):
            act.sem_inc(logit_out, 2)
            with act.Fori(0, BATCH // 2) as i:
                for p in range(2):
                    b = i * 2 + p
                    act.wait_ge(logit_done, b + 1)
                    act.wait_ge(turned, i * 2)
                    nc.scalar.activation(lg[:, p], pl[p][:], ACT.Copy).then_inc(logit_out, 1)
            act.wait_ge(exp_ready, 1)
            nc.scalar.activation(prob[:], prob[:], ACT.Exp).then_inc(exp_done, 1)

        @block.vector
        def _(dve):
            V = nc.vector
            link = Chain(dve, chain_sem)
            dve.wait_ge(loaded, 32)
            V.tensor_copy(w_hi[:], raw[:]).then_inc(w_split, 1)
            dve.wait_ge(w_split, 1)
            V.tensor_tensor(w_lo[:], raw[:], w_hi[:].bitcast(FP32), ALU.subtract).then_inc(w_split, 1)
            dve.sem_inc(taken, 2)
            with dve.Fori(0, BATCH // 2) as i:
                for p in range(2):
                    b = i * 2 + p
                    dve.wait_ge(turned, b + 1)
                    V.tensor_copy(prob[:, ds(b * TPB, TPB), :], pt[p][:]).then_inc(taken, 1)
            dve.wait_ge(taken, BATCH + 2)
            over_e = lambda a: a[:].rearrange("p (t o) -> p t o", o=1).broadcast_to([P, TILES, E1])
            link(V.tensor_reduce(top[:], prob[:], AX.X, ALU.max))
            V.tensor_tensor(prob[:], prob[:], over_e(top), ALU.subtract).then_inc(exp_ready, 1)
            dve.wait_ge(exp_done, 1)
            link(V.tensor_reduce(total[:], prob[:], AX.X, ALU.add))
            link(V.reciprocal(total[:], total[:]))
            link(V.tensor_tensor(prob[:], prob[:], over_e(total), ALU.mult))
            p_j = prob[:].rearrange("p t (o j) -> p t o j", o=1).broadcast_to([P, TILES, E1, E1])
            p_e = prob[:].rearrange("p t (e o) -> p t e o", o=1).broadcast_to([P, TILES, E1, E1])
            low = below[:].rearrange("p (o e) j -> p o e j", o=1).broadcast_to([P, TILES, E1, E1])
            link.mark(V.tensor_tensor(ge[:], p_j, p_e, ALU.is_ge))
            link(V.tensor_tensor(gt[:], p_j, p_e, ALU.is_gt))
            link(V.tensor_tensor(ge[:], ge[:], gt[:], ALU.subtract))
            link(V.tensor_tensor(ge[:], ge[:], low, ALU.mult))
            link(V.tensor_tensor(gt[:], gt[:], ge[:], ALU.add))
            link(V.tensor_reduce(rank[:], gt[:], AX.X, ALU.add))
            link(V.scalar_tensor_tensor(prob[:], rank[:], 2.0, prob[:], ALU.is_lt, ALU.mult))
            link(V.tensor_reduce(total[:], prob[:], AX.X, ALU.add))
            link(V.reciprocal(total[:], total[:]))
            link(V.tensor_tensor(prob[:], prob[:], over_e(total), ALU.mult))
            dve.wait_ge(cleared, 1)
            base = link.n
            PER = 4
            with dve.Fori(0, BATCH // 2) as i:
                for p in range(2):
                    b = i * 2 + p
                    dve.wait_ge(back, i * 2)
                    V.tensor_copy(stage[:, p], prob[:, ds(b * TPB, TPB), :]).then_inc(staged, 1)
                for p in range(2):
                    b = i * 2 + p
                    link = Chain(dve, chain_sem, base + b * PER)
                    cols = ds(b * SEQ, SEQ)
                    dve.wait_ge(back, b + 1)
                    link(V.tensor_copy(g.combine[0:E1, cols], pc[p][:]))
                    link(V.tensor_tensor(rest[:, p], pc[p][:], g.combine[0:E1, cols], ALU.subtract))
                    link(V.tensor_copy(part[:, p], rest[:, p]))
                    link.mark(V.tensor_copy(g.combine[32:32 + E1, cols], part[:, p]))
                    V.tensor_tensor(g.combine[64:64 + E1, cols], rest[:, p], part[:, p], ALU.subtract).then_inc(back_used, 1)

def experts(nc, ctx, src, dst, w1_d, w2_d, owner_d, g):
    sem = lambda n: nc.alloc_semaphore(name=f"mo_{n}")
    w_loaded, w_split, d_loaded = sem("wload"), sem("wsplit"), sem("dload")
    gate_done, up_done, bc_done, silu_done, t_done, h_done = (sem(n) for n in ("gate", "up", "bc", "silu", "t", "h"))
    down_step, out_done = sem("down"), sem("out")
    stored, res_loaded = [sem("st0"), sem("st1")], [sem("res0"), sem("res1")]
    with ExitStack() as mem:
        sb = lambda n, s, d=FP32: mem.enter_context(nc.sbuf_tensor(f"mo_{n}", s, d))
        w_hi, w_lo = ([sb(f"w{n}{q}", [P, KD, WIDE], FP32R) for q in "gu"] for n in ("hi", "lo"))
        raw = sb("raw", [P, WIDE])
        wd = sb("wd", [P, ET, DM])
        owner_f, owner = sb("ownf", [96, ET, P]), sb("own", [96, ET, P], BF16)
        silu, h = sb("silu", [P, 2, SEQ]), sb("h", [P, 2, SEQ])
        out = sb("outt", [P, 2, TPB, DM])
        ps = lambda n, s: mem.enter_context(nc.psum_tensor(f"mo_{n}", s, FP32))
        pg, pu, pb = ([ps(f"p{n}{i}", [P, SEQ]) for i in range(2)] for n in "gub")
        pd = ps("pd", [P, TPB, DM])
        block = mem.enter_context(nc.Block())
        src_v = src.rearrange("(b n p) d -> b p n d", p=P, n=TPB)
        dst_v = dst.rearrange("(b n p) d -> b p n d", p=P, n=TPB)
        parts = [(q, k) for q in range(2) for k in range(KD)]

        @block.sync
        def _(sp):
            sp.dma_start(wd[:], w2_d).then_inc(d_loaded, 16)
            sp.dma_start(owner_f[:], owner_d).then_inc(d_loaded, 16)
            for n, (q, k) in enumerate(parts):
                if n:
                    sp.wait_ge(w_split, 2 * n)
                sp.dma_start(raw[:], w1_d[:, q, k, :]).then_inc(w_loaded, 16)
            with sp.Fori(0, BATCH // 2) as i:
                for p in range(2):
                    b = i * 2 + p
                    sp.wait_ge(stored[p], 16 * i)
                    sp.dma_start(out[:, p], src_v[ds(b, 1)].rearrange("a p n d -> p (a n) d")).then_inc(res_loaded[p], 16)
                for p in range(2):
                    b = i * 2 + p
                    sp.wait_ge(out_done, b + 1)
                    sp.dma_start(dst_v[ds(b, 1)].rearrange("a p n d -> p (a n) d"), out[:, p]).then_inc(stored[p], 16)
            for p in range(2):
                sp.wait_ge(stored[p], 16 * (BATCH // 2))

        @block.gpsimd
        def _(pool):
            for n in range(len(parts)):
                q, k = parts[n]
                pool.wait_ge(w_split, 2 * n + 1)
                nc.gpsimd.tensor_tensor(w_lo[q][:, k, :], raw[:], w_hi[q][:, k, :].bitcast(FP32),
                                        ALU.subtract).then_inc(w_split, 1)

        def product(w, b, s, psum):
            for k in range(KD):
                cols = slice(s * P, (s + 1) * P)
                last = matmul3(nc, psum, w_hi[w][:, k, cols], w_lo[w][:, k, cols], g.x_hi[:, k, ds(b * SEQ, SEQ)],
                               g.x_lo[:, k, ds(b * SEQ, SEQ)], k == 0, k == KD - 1)
            return last

        @block.tensor
        def _(pe):
            pe.wait_ge(w_split, 2 * len(parts))
            pe.wait_ge(d_loaded, 33)

            def down(b, q, s):
                pe.wait_ge(h_done, b * ET + s + 3)
                for n in range(TPB):
                    last = nc.tensor.matmul(pd[:, n, :], h[:, q % 2, n * P:(n + 1) * P], wd[:, s, :],
                                            start=s == 0 and n % 2 == 0, stop=s == ET - 1 and n % 2 == 1,
                                            skip_group_check=True)
                last.then_inc(down_step, 1)

            pe.sem_inc(down_step, 2)
            with pe.Fori(0, BATCH // 2) as i:
                for q in range(2 * ET):
                    p, s = divmod(q, ET)
                    b = i * 2 + p
                    n = b * ET + s
                    pe.wait_ge(silu_done, n + 1)
                    product(0, b, s, pg[q % 2][:]).then_inc(gate_done, 1)
                    pe.wait_ge(h_done, n + 1)
                    product(1, b, s, pu[q % 2][:]).then_inc(up_done, 1)
                    nc.tensor.matmul(pb[q % 2][:], owner[:, s, :], g.combine[:, ds(b * SEQ, SEQ)],
                                     start=True, stop=True).then_inc(bc_done, 1)
                    if s == 1:
                        pe.wait_ge(out_done, b)
                    if s:
                        down(b, q - 1, s - 1)
                    if s == ET - 1:
                        down(b, q, s)

        @block.scalar
        def _(act):
            act.sem_inc(silu_done, 2)
            for n, (q, k) in enumerate(parts):
                act.wait_ge(w_loaded, 16 * (n + 1))
                nc.scalar.activation(w_hi[q][:, k, :], raw[:], ACT.Copy).then_inc(w_split, 1)
                if n < len(parts) - 1:
                    act.wait_ge(w_split, 2 * n + 2)
            nc.scalar.preload_act_table(ACT.Silu)
            with act.Fori(0, BATCH // 2) as i:
                for q in range(2 * ET):
                    n = i * (2 * ET) + q
                    act.wait_ge(gate_done, n + 1)
                    act.wait_ge(h_done, n + 1)
                    nc.scalar.activation(silu[:, q % 2], pg[q % 2][:], ACT.Silu).then_inc(silu_done, 1)

        @block.vector
        def _(dve):
            V = nc.vector
            dve.wait_ge(d_loaded, 32)
            V.tensor_copy(owner[:], owner_f[:]).then_inc(d_loaded, 1)
            dve.sem_inc(h_done, 2)
            with dve.Fori(0, BATCH // 2) as i:
                for q in range(2 * ET):
                    p, s = divmod(q, ET)
                    b = i * 2 + p
                    n = b * ET + s
                    dve.wait_ge(silu_done, n + 3)
                    dve.wait_ge(up_done, n + 1)
                    V.tensor_tensor(silu[:, q % 2], pu[q % 2][:], silu[:, q % 2], ALU.mult).then_inc(t_done, 1)
                    dve.wait_ge(t_done, n + 1)
                    dve.wait_ge(bc_done, n + 1)
                    dve.wait_ge(down_step, n + 1)
                    V.tensor_tensor(h[:, q % 2], pb[q % 2][:], silu[:, q % 2], ALU.mult).then_inc(h_done, 1)
                    if s == ET - 1:
                        dve.wait_ge(down_step, (b + 1) * ET + 2)
                        dve.wait_ge(res_loaded[p], i * 16 + 16)
                        V.tensor_tensor(out[:, p], pd[:], out[:, p], ALU.add).then_inc(out_done, 1)

def ffn0_weights(gate, up, down):
    def cols(w):
        w = w.reshape(KD, P, GT, P, GROUP).transpose(1, 0, 2, 4, 3)
        return np.ascontiguousarray(w).reshape(P, KD, I0)
    d = down.reshape(GT, P, GROUP, DM).transpose(1, 0, 2, 3)
    return cols(gate), cols(up), np.ascontiguousarray(d).reshape(P, SLOTS, DM)

def moe_weights(gate_w, w1, w2):
    wt = np.ascontiguousarray(gate_w.T.reshape(KD, P, E1).transpose(1, 0, 2))
    w = w1.reshape(E1, 2, I1, KD, P).transpose(4, 1, 3, 0, 2)
    d = w2.transpose(0, 2, 1).reshape(ET, P, DM).transpose(1, 0, 2)
    below = np.broadcast_to(np.tril(np.ones((E1, E1), np.float32), -1), (P, E1, E1))
    owner = np.zeros((3, 32, ET, P), np.float32)
    rows = np.arange(WIDE)
    owner[:, rows // I1, rows // P, rows % P] = 1.0
    return (wt, np.ascontiguousarray(w).reshape(P, 2, KD, WIDE), np.ascontiguousarray(d),
            np.ascontiguousarray(below), owner.reshape(96, ET, P))

def attention0_weights(q_sem, k_sem, q_geo, k_geo, v, o):
    half = DH // 2
    quarter = half // 2

    def cols(sem, geo):
        sem, geo = sem.reshape(H0, half, DM), geo.reshape(H0, half, DM)
        plain = np.concatenate([sem, geo], 1)
        turned = np.concatenate([np.zeros_like(sem), geo[:, quarter:], geo[:, :quarter]], 1)
        both = np.stack([plain, turned])
        both = np.concatenate([both, both], 2).reshape(2 * G0 * P, DM)
        return both

    w = np.concatenate([cols(q_sem, q_geo), cols(k_sem, k_geo), v])
    w = np.ascontiguousarray(w.T.reshape(KD, P, -1).transpose(1, 0, 2))
    return w, np.ascontiguousarray(o.T.reshape(KD, P, DM).transpose(1, 0, 2))

def attention0_tables():
    half = DH // 2
    quarter = half // 2
    inv = (1.0 / np.float32(10000.0) ** (np.arange(0, half, 2, dtype=np.float32) / np.float32(half))).astype(np.float32)
    freq = (np.arange(SEQ, dtype=np.float32)[:, None] * inv[None, :]).astype(np.float32)
    cos, sin = np.cos(freq).T, np.sin(freq).T
    one, nil = np.ones((half, SEQ), np.float32), np.zeros((half, SEQ), np.float32)
    c = np.concatenate([one, cos, cos])
    s = np.concatenate([nil, -sin, sin])
    c, s = np.tile(c, (2 * HG, 1)), np.tile(s, (2 * HG, 1))
    scale = np.float32(DH ** -0.5)
    tables = np.stack([c * scale, s * scale, c, s], 1).astype(np.float32)
    lower = np.where(np.arange(P) % (2 * DH) >= DH, -1.0, 0.0).astype(np.float32)[:, None]
    above = np.where(np.arange(P)[None, :] > np.arange(P)[:, None], -3e38, 0.0).astype(np.float32)
    return tables, np.ascontiguousarray(lower), above

def kmajor(w):
    return np.ascontiguousarray(w.T.reshape(-1, P, w.shape[0]).transpose(1, 0, 2))

def gate_weights(wdt, wlam, a_log):
    w = np.zeros((2, 2, 2, H1, DM), np.float32)
    for j in range(2):
        w[0, j, j], w[1, j, j] = wdt, wlam
    w = w.reshape(2, 2, P, KD, P).transpose(4, 3, 0, 1, 2)
    return np.ascontiguousarray(w), np.ascontiguousarray(np.tile(a_log, 2)[:, None])

def state_weights(wth, wb, wc):
    half = N1 // 2
    parts = [wth.reshape(PAIRS, 2, half, DM)]
    for w in (wb, wc):
        w = w.reshape(PAIRS, 2, half, 2, DM)
        parts += [w[:, :, :, 0], w[:, :, :, 1]]
    w = np.stack(parts, 1)
    return np.ascontiguousarray(w.reshape(PAIRS, WC, KD, P).transpose(0, 3, 2, 1))

def state_norm(bn, cn):
    return np.ascontiguousarray(np.stack([np.tile(w[e::2], 2) for w in (bn, cn) for e in range(2)], 1))

def state_bias(b, c):
    b = np.stack([w.reshape(PAIRS, P, 2)[:, :, e] for w in (b, c) for e in range(2)], 2)
    return np.ascontiguousarray(b.transpose(1, 0, 2))

def state_constants():
    con = np.zeros((6, 5, P), np.float32)
    for h in range(2):
        rows = slice(3 * h, 3 * h + 3)
        con[rows, 0, h * H1:(h + 1) * H1] = 1.0
        con[rows, 1 + h] = 1.0
        con[rows, 3 + h] = -1.0
    t = np.arange(P)
    strict = np.where(t[None, :] > t[:, None], 0.0, -3e38).astype(np.float32)
    blocks = (t[:, None] // H1 == np.arange(PW)[None, :] // P1).astype(np.float32)
    return con, strict, np.ascontiguousarray(blocks)

@contextmanager
def phase(nc):
    before = nc.snapshot_sems()
    yield
    nc.clear_and_free_semaphores(nc.allocated_since(before))
    nc.all_engine_barrier()

def program(nc, i, scratch, out):
    x1, x2, x3, tk, rows, xp, y = scratch
    with ExitStack() as ctx:
        g = constants(nc, ctx)
        with phase(nc):
            layernorm_transposed(nc, ctx, "ln0", i["x"], g)
        with phase(nc):
            causal_attention(nc, ctx, i["x"], x1, i["w_qkv"], i["w_o"], i["rope"], i["lower"], i["above"], g)
        with phase(nc):
            layernorm_transposed(nc, ctx, "ln1", x1, g)
        with phase(nc):
            sparse_swiglu(nc, ctx, x1, x2, i["w_gate"], i["w_up"], i["w_down"], g)
        with phase(nc):
            layernorm_transposed(nc, ctx, "ln2", x2, g)
        with phase(nc):
            gates(nc, ctx, i["w_dt"], i["a_log"], tk, rows, g)
        with phase(nc):
            input_projection(nc, ctx, i["w_x"], xp, g)
        with phase(nc):
            state_space(nc, ctx, i["w_state"], i["state_norm"], i["state_bias"], i["state_con"], i["strict"], i["blocks"],
                        tk, rows, xp, y, g)
        with phase(nc):
            output_projection(nc, ctx, x2, x3, i["w_z"], i["w_out"], y, g)
        with phase(nc):
            layernorm_transposed(nc, ctx, "ln3", x3, g)
        g.combine = ctx.enter_context(nc.sbuf_tensor("combine", [96, TOK], BF16))
        with phase(nc):
            route(nc, ctx, i["w_route"], i["below"], g)
        with phase(nc):
            experts(nc, ctx, x3, out, i["w_1"], i["w_2"], i["owner"], g)

def kernel(**inputs):
    from concourse.bacc import Bacc
    from concourse.bass_utils import run_bass_kernel_spmd

    a = {n: np.ascontiguousarray(v) for n, v in inputs.items()}
    x = a["L0_attn_x"]
    i = {"x": x.reshape(TOK, DM)}
    i["w_qkv"], i["w_o"] = attention0_weights(*(a[f"L0_attn_{n}"] for n in ("Wq_sem", "Wk_sem", "Wq_geo", "Wk_geo", "Wv", "Wo")))
    i["rope"], i["lower"], i["above"] = attention0_tables()
    i["w_gate"], i["w_up"], i["w_down"] = ffn0_weights(*(a[f"L0_ffn_{n}"] for n in ("w_gate", "w_up", "w_down")))
    i["w_dt"], i["a_log"] = gate_weights(a["L1_attn_Wdt"], a["L1_attn_Wlam"], a["L1_attn_A_log"])
    i["w_x"], i["w_z"], i["w_out"] = (kmajor(a[f"L1_attn_{n}"]) for n in ("Wx", "Wz", "Wout"))
    i["w_state"] = state_weights(a["L1_attn_Wth"], a["L1_attn_WB"], a["L1_attn_WC"])
    i["state_norm"] = state_norm(a["L1_attn_Bn_w"], a["L1_attn_Cn_w"])
    i["state_bias"] = state_bias(a["L1_attn_B_bias"], a["L1_attn_C_bias"])
    i["state_con"], i["strict"], i["blocks"] = state_constants()
    i["w_route"], i["w_1"], i["w_2"], i["below"], i["owner"] = moe_weights(a["L1_ffn_gate_w"], a["L1_ffn_w1"], a["L1_ffn_w2"])

    nc = Bacc("TRN2", target_bir_lowering=False, num_devices=1)
    arrays = {f"in_{n}": np.ascontiguousarray(v) for n, v in i.items()}
    ins = {n: nc.dram_tensor(f"in_{n}", list(v.shape), FP32, kind="ExternalInput").ap() for n, v in i.items()}
    inner = lambda n, s, d=FP32: nc.dram_tensor(n, s, d, kind="Internal").ap()
    scratch = [inner(f"x{n}", [TOK, DM]) for n in (1, 2, 3)]
    scratch += [inner("token_gates", [PAIRS, P, 256]), inner("gate_rows", [384, 2, CW], BF16),
                inner("x_heads", [TOK, DIN]), inner("y_heads", [TOK, DIN])]
    out = nc.dram_tensor("out", [TOK, DM], FP32, kind="ExternalOutput").ap()
    program(nc, ins, scratch, out)
    r = run_bass_kernel_spmd(nc, [arrays], core_ids=[0])
    return r.results[0]["out"].reshape(x.shape)
```

```python
from concourse import mybir
from contextlib import ExitStack
from contextlib import contextmanager
import concourse.bass as bass
import math
import numpy as np

FP32 = mybir.dt.float32
FP32R = mybir.dt.float32r
BF16 = mybir.dt.bfloat16
ALU = mybir.AluOpType
ACT = mybir.ActivationFunctionType
AX = mybir.AxisListType

P = 128
BATCH, SEQ, DM = 8, 512, 256
TOK = BATCH * SEQ
TILES = TOK // P
KD = DM // P
TPB = SEQ // P
LN_EPS = 1e-5
ds = bass.ds

class Chain:

    def __init__(self, eng, sem, base=0):
        self.eng, self.sem, self.base, self.n = eng, sem, base, 0

    def mark(self, ins):
        self.n += 1
        ins.then_inc(self.sem, 1)
        return self.n

    def wait(self, n=None):
        self.eng.wait_ge(self.sem, self.base + (self.n if n is None else n))

    def __call__(self, ins):
        self.mark(ins)
        self.wait()

def matmul3(nc, out, w_hi, w_lo, x_hi, x_lo, first, last):
    nc.tensor.matmul(out, w_hi, x_hi, start=first, stop=False)
    nc.tensor.matmul(out, w_hi, x_lo, start=False, stop=False)
    return nc.tensor.matmul(out, w_lo, x_hi, start=False, stop=last)

def layernorm_transposed(nc, ctx, name, src, g):
    GROUPS = 8
    RING = 4
    PER = TILES // GROUPS
    sem = lambda n: nc.alloc_semaphore(name=f"{name}_{n}")
    loaded = [sem(f"loaded{q}") for q in range(GROUPS)]
    stats_done, var_ready, std_ready, norm_ready = sem("stats"), sem("var"), sem("std"), sem("normed")
    transposed, hi_ready, lo_ready, chain_sem = sem("transposed"), sem("hi"), sem("lo"), sem("chain")
    with ExitStack() as mem:
        sb = lambda n, s, d=FP32: mem.enter_context(nc.sbuf_tensor(f"{name}_{n}", s, d))
        x = sb("x", [P, TILES, DM])
        stats = sb("stats6", [P, TILES, 6])
        mean, diff, var, rstd = (sb(n, [P, TILES]) for n in ("mean", "diff", "var", "rstd"))
        normed = sb("normedx", [P, RING, DM])
        eps = sb("eps", [P, 1])
        turned = [mem.enter_context(nc.psum_tensor(f"{name}_ps{i}", [P, KD, P], FP32)) for i in range(RING)]
        block = mem.enter_context(nc.Block())
        src_v = src.rearrange("(q n p) d -> q p n d", p=P, n=PER)

        @block.sync
        def _(sp):
            for q in range(0, GROUPS, 2):
                sp.dma_start(x[:, q * PER:(q + 1) * PER, :], src_v[q]).then_inc(loaded[q], 16)

        @block.vector
        def _(dve):
            nc.vector.memset(eps[:], LN_EPS).then_inc(stats_done, 1)
            for q in range(GROUPS):
                dve.wait_ge(loaded[q], 16)
                for n in range(PER):
                    t = q * PER + n
                    last = nc.vector.bn_stats(stats[:, t, :], x[:, t, :])
                last.then_inc(stats_done, 1)
            dve.wait_ge(stats_done, 1 + GROUPS)
            link = Chain(dve, chain_sem)
            link.mark(nc.vector.tensor_tensor(mean[:], stats[:, :, 1], stats[:, :, 4], ALU.add))
            link.mark(nc.vector.tensor_tensor(diff[:], stats[:, :, 1], stats[:, :, 4], ALU.subtract))
            link(nc.vector.tensor_tensor(var[:], stats[:, :, 2], stats[:, :, 5], ALU.add))
            link.mark(nc.vector.tensor_scalar(mean[:], mean[:], 0.5, None, ALU.mult))
            link.mark(nc.vector.scalar_tensor_tensor(diff[:], diff[:], 0.25, diff[:], ALU.mult, ALU.mult))
            link(nc.vector.tensor_scalar(var[:], var[:], 1.0 / DM, None, ALU.mult))
            nc.vector.tensor_tensor(var[:], var[:], diff[:], ALU.add).then_inc(var_ready, 1)
            dve.wait_ge(std_ready, 1)
            link(nc.vector.reciprocal(rstd[:], rstd[:]))
            dve.sem_inc(lo_ready, RING)

            def normalize(t, p):
                nc.vector.tensor_scalar(normed[:, p, :], x[:, ds(t, 1), :], mean[:, ds(t, 1)],
                                        rstd[:, ds(t, 1)], ALU.subtract, ALU.mult).then_inc(norm_ready, 1)

            def rests(i):
                for p in range(RING):
                    t = i * RING + p
                    dve.wait_ge(hi_ready, t + 1)
                    cols = ds(t * P, P)
                    nc.vector.tensor_tensor(g.x_lo[:, :, cols], turned[p][:], g.x_hi[:, :, cols].bitcast(FP32),
                                            ALU.subtract).then_inc(lo_ready, 1)

            for p in range(RING):
                normalize(p, p)
            with dve.Fori(0, TILES // RING - 1) as i:
                for p in range(RING):
                    t = i * RING + p
                    dve.wait_ge(transposed, t + 1)
                    normalize(t + RING, p)
                rests(i)
            rests(TILES // RING - 1)

        @block.scalar
        def _(act):
            for q in range(1, GROUPS, 2):
                act.dma_start(x[:, q * PER:(q + 1) * PER, :], src_v[q]).then_inc(loaded[q], 16)
            act.wait_ge(var_ready, 1)
            act.wait_ge(stats_done, 1)
            nc.scalar.activation(rstd[:], var[:], ACT.Sqrt, bias=eps[:, 0:1]).then_inc(std_ready, 1)
            with act.Fori(0, TILES // RING) as i:
                for p in range(RING):
                    t = i * RING + p
                    act.wait_ge(transposed, t + 1)
                    nc.scalar.activation(g.x_hi[:, :, ds(t * P, P)], turned[p][:], ACT.Copy).then_inc(hi_ready, 1)

        @block.tensor
        def _(pe):
            with pe.Fori(0, TILES // RING) as i:
                for p in range(RING):
                    t = i * RING + p
                    pe.wait_ge(norm_ready, t + 1)
                    pe.wait_ge(lo_ready, t + 1)
                    for k in range(KD):
                        last = nc.tensor.transpose(turned[p][:, k, :], normed[:, p, k * P:(k + 1) * P], g.ident[:])
                    last.then_inc(transposed, 1)

class OnChip:
    pass

def constants(nc, ctx):
    g = OnChip()
    sb = lambda n, s, d=FP32: ctx.enter_context(nc.sbuf_tensor(n, s, d))
    g.ident = sb("ident", [P, P])
    g.ident16 = sb("ident16", [P, P], BF16)
    g.x_hi = sb("x_hi", [P, KD, TOK], FP32R)
    g.x_lo = sb("x_lo", [P, KD, TOK], FP32R)
    made = ctx.enter_context(nc.semaphore("ident_made"))
    with nc.Block() as block:
        @block.gpsimd
        def _(pool):
            nc.gpsimd.memset(g.ident[:], 0.0).then_inc(made, 1)
            pool.wait_ge(made, 1)
            nc.gpsimd.affine_select(out=g.ident[:], in_=g.ident[:], compare_op=ALU.not_equal, fill=1.0, base=0,
                                    pattern=[[-1, P]], channel_multiplier=1).then_inc(made, 1)
            pool.wait_ge(made, 2)
            nc.gpsimd.tensor_copy(g.ident16[:], g.ident[:]).then_inc(made, 1)
            pool.wait_ge(made, 3)
    return g

H0, DH = 16, 16
HG = 4
G0 = H0 // HG
QKC = 2 * 2 * G0 * P

def causal_attention(nc, ctx, src, dst, w_d, wo_d, tables_d, lower_d, below_d, g):
    sem = lambda n: nc.alloc_semaphore(name=f"a0_{n}")
    w_loaded, w_split, t_loaded = sem("wload"), sem("wsplit"), sem("tload")
    ab_done, rope_read, rope_done, y_done = sem("ab"), sem("roperead"), sem("rope"), sem("y")
    v_done, v_taken, vt_done, v_ready = sem("v"), sem("vtaken"), sem("vt"), sem("vready")
    s_done, max_done, exp_done, t_done = sem("s"), sem("max"), sem("exp"), sem("t")
    tv_done, ta_done, pv_done, norm_done = sem("tv"), sem("ta"), sem("pv"), sem("norm")
    vh_ready, head_done, cleared, inv_done, ot_ready, wo_done, out_done = sem("vh"), sem("head"), sem("cleared"), sem("inv"), sem("otready"), sem("wo"), sem("out")
    stored, res_loaded = [sem("st0"), sem("st1")], [sem("res0"), sem("res1")]
    STEPS = H0 * TPB
    PROBS, PROBTS = 5, 3
    RING = 4
    LAG = 3
    CH = 512
    CHUNKS = QKC // CH
    with ExitStack() as mem:
        sb = lambda n, s, d=FP32: mem.enter_context(nc.sbuf_tensor(f"a0_{n}", s, d))
        w_hi, w_lo = sb("whi", [P, KD, QKC + DM], FP32R), sb("wlo", [P, KD, QKC + DM], FP32R)
        raw = sb("raw", [P, KD, CH])
        wo = sb("wo", [P, KD, DM])
        tables = sb("tables", [P, 4, SEQ])
        lower = sb("lower", [P, 1])
        below_f, below = sb("belowf", [P, P]), sb("below", [P, P], BF16)
        t1, t2 = sb("t1", [P, SEQ]), sb("t2", [P, SEQ])
        y, y_hi = sb("y", [P, 2, SEQ]), sb("yhi", [P, SEQ], FP32R)
        q1, k1, k2 = (sb(n, [P, G0, SEQ], FP32R) for n in ("q1", "k1", "k2"))
        vt, v = sb("vt", [P, KD, SEQ]), sb("vv", [P, TPB, DM])
        nmax = sb("nmax", [P, 8])
        prob = sb("prob", [P, PROBS, SEQ])
        probt = sb("probt", [P, PROBTS, SEQ])
        sums = sb("sums", [P, TPB * H0])
        nil = sb("nil", [P, SEQ], BF16)
        v_head = sb("vhead", [P, 2, TPB, 2 * P - DH])
        ot = sb("ot", [P, KD, SEQ])
        out = sb("outt", [P, 2, TPB, DM])
        ps = lambda n, s: mem.enter_context(nc.psum_tensor(f"a0_ps_{n}", s, FP32))
        p_s = [ps(f"s{i}", [P, SEQ]) for i in range(2)]
        p_t = [ps(f"t{i}", [P, SEQ]) for i in range(2)]
        p_o = [ps(f"o{i}", [P, SEQ]) for i in range(KD)]
        p_p = [ps(f"p{i}", [P, SEQ]) for i in range(2)]
        ring = p_s + p_p
        block = mem.enter_context(nc.Block())
        src_v = src.rearrange("(b n p) d -> b p n d", p=P, n=TPB)
        dst_v = dst.rearrange("(b n p) d -> b p n d", p=P, n=TPB)
        pieces = [(c * CH, CH) for c in range(CHUNKS)] + [(QKC, DM)]
        on_act = lambda i: i % 2 == 1

        @block.sync
        def _(sp):
            for n, (at, w) in enumerate(pieces):
                if n:
                    sp.wait_ge(w_split, 2 * n)
                sp.dma_start(raw[:, :, 0:w], w_d[:, :, at:at + w]).then_inc(w_loaded, 16)
                if n == 0:
                    sp.dma_start(tables[:], tables_d).then_inc(t_loaded, 16)
                    sp.dma_start(wo[:], wo_d).then_inc(t_loaded, 16)
                    sp.dma_start(lower[:], lower_d).then_inc(t_loaded, 16)
                    sp.dma_start(below_f[:], below_d).then_inc(t_loaded, 16)
            with sp.Fori(0, BATCH // 2) as i:
                for p in range(2):
                    b = i * 2 + p
                    sp.wait_ge(stored[p], 16 * i)
                    sp.dma_start(out[:, p], src_v[ds(b, 1)].rearrange("a p n d -> p (a n) d")).then_inc(res_loaded[p], 16)
                for p in range(2):
                    b = i * 2 + p
                    sp.wait_ge(out_done, b + 1)
                    sp.dma_start(dst_v[ds(b, 1)].rearrange("a p n d -> p (a n) d"), out[:, p]).then_inc(stored[p], 16)
            for p in range(2):
                sp.wait_ge(stored[p], 16 * (BATCH // 2))

        @block.gpsimd
        def _(pool):
            for n, (at, w) in enumerate(pieces):
                pool.wait_ge(w_split, 2 * n + 1)
                nc.gpsimd.tensor_tensor(w_lo[:, :, at:at + w], raw[:, :, 0:w], w_hi[:, :, at:at + w].bitcast(FP32),
                                        ALU.subtract).then_inc(w_split, 1)
            nc.gpsimd.memset(v_head[:], 0.0).then_inc(cleared, 1)
            nc.gpsimd.memset(nil[:], 0.0).then_inc(cleared, 1)

        @block.tensor
        def _(pe):
            pe.wait_ge(w_split, 2 * len(pieces))
            pe.wait_ge(t_loaded, 65)
            pe.wait_ge(cleared, 2)
            with pe.Fori(0, BATCH) as b:
                tok = ds(b * SEQ, SEQ)

                def project(col, psum):
                    for k in range(KD):
                        cols = slice(col, col + P)
                        last = matmul3(nc, psum, w_hi[:, k, cols], w_lo[:, k, cols], g.x_hi[:, k, tok],
                                       g.x_lo[:, k, tok], k == 0, k == KD - 1)
                    return last

                pe.wait_ge(exp_done, b * STEPS)
                for n in range(2 * G0):
                    grp, qk = divmod(n, 2)
                    pair = (p_p, p_s)[n % 2]
                    if n == 1:
                        pe.wait_ge(out_done, b)
                    pe.wait_ge(rope_read, b * (2 * G0) + max(n - 1, 0))
                    project(((qk * 2 + 0) * G0 + grp) * P, pair[0][:])
                    project(((qk * 2 + 1) * G0 + grp) * P, pair[1][:]).then_inc(ab_done, 1)
                pe.wait_ge(rope_read, (b + 1) * (2 * G0))
                for k in range(KD):
                    project(QKC + k * P, p_p[k][:]).then_inc(v_done, 1)
                for n in range(TPB):
                    if n % 2 == 0:
                        pe.wait_ge(v_taken, (b + 1) * KD)
                    for k in range(KD):
                        last = nc.tensor.transpose(p_p[n // 2][:, ((n % 2) * KD + k) * P:((n % 2) * KD + k + 1) * P],
                                                   vt[:, k, n * P:(n + 1) * P], g.ident[:])
                    if n % 2:
                        last.then_inc(vt_done, 1)
                pe.wait_ge(rope_done, (b + 1) * (2 * G0))
                pe.wait_ge(v_ready, (b + 1) * 2)
                for n in range(STEPS + LAG + 1):
                    if n < STEPS:
                        h, i = divmod(n, TPB)
                        grp, j = divmod(h, HG)
                        rows, width = slice(32 * j, 32 * j + 32), (i + 1) * P
                        pe.wait_ge(exp_done, b * STEPS + max(n - RING + 1, 0))
                        s = ring[n % RING]
                        nc.tensor.matmul(s[:, 0:width], q1[rows, grp, i * P:(i + 1) * P], k1[rows, grp, 0:width],
                                         start=True, stop=False)
                        nc.tensor.matmul(s[:, width - P:width], g.ident16[:], below[:], start=False, stop=False,
                                         skip_group_check=True)
                        nc.tensor.matmul(s[:, 0:width], q1[rows, grp, i * P:(i + 1) * P], k2[rows, grp, 0:width],
                                         start=False, stop=True).then_inc(s_done, 1)
                    if LAG <= n < STEPS + LAG:
                        m = n - LAG
                        i = m % TPB
                        pe.wait_ge(norm_done, b * STEPS + m + 1)
                        before = m - 2
                        if before >= 0:
                            pe.wait_ge(ta_done if on_act(before) else tv_done, b * (STEPS // 2) + before // 2 + 1)
                        for kt in range(i + 1):
                            last = nc.tensor.transpose(p_t[m % 2][:, kt * P:(kt + 1) * P],
                                                       prob[:, m % PROBS, kt * P:(kt + 1) * P], g.ident[:])
                        last.then_inc(t_done, 1)
                    if n >= LAG + 1:
                        m = n - LAG - 1
                        h, i = divmod(m, TPB)
                        if i == 0:
                            pe.wait_ge(vh_ready, b * H0 + h + 1)
                        pe.wait_ge(ta_done if on_act(m) else tv_done, b * (STEPS // 2) + m // 2 + 1)
                        half, at = divmod(h, P // DH)
                        if at == 0 and i == 0:
                            nc.tensor.matmul(p_o[half][:], g.ident16[:], nil[:], start=True, stop=False, skip_group_check=True)
                        for kt in range(i + 1):
                            last = nc.tensor.matmul(p_o[half][:, i * P:(i + 1) * P],
                                                    v_head[:, h % 2, kt, P - DH - at * DH:2 * P - DH - at * DH],
                                                    probt[:, m % PROBTS, kt * P:(kt + 1) * P],
                                                    start=False, stop=at == P // DH - 1 and kt == i,
                                                    skip_group_check=True)
                        last.then_inc(pv_done, 1)
                pe.wait_ge(ot_ready, b + 1)
                for n in range(TPB):
                    for k in range(KD):
                        last = nc.tensor.matmul(p_s[n // 2][:, (n % 2) * DM:(n % 2 + 1) * DM], ot[:, k, n * P:(n + 1) * P],
                                                wo[:, k, :], start=k == 0, stop=k == KD - 1)
                last.then_inc(wo_done, 1)

        @block.scalar
        def _(act):
            A = nc.scalar.activation
            for n, (at, w) in enumerate(pieces):
                act.wait_ge(w_loaded, 16 * (n + 1))
                A(w_hi[:, :, at:at + w], raw[:, :, 0:w], ACT.Copy).then_inc(w_split, 1)
                if n < len(pieces) - 1:
                    act.wait_ge(w_split, 2 * n + 2)
            nc.scalar.preload_act_table(ACT.Exp)
            act.wait_ge(cleared, 2)
            with act.Fori(0, BATCH) as b:
                act.wait_ge(s_done, b * STEPS)
                for n in range(2 * G0):
                    grp, qk = divmod(n, 2)
                    act.wait_ge(y_done, b * (2 * G0) + n + 1)
                    if qk == 0:
                        act.wait_ge(rope_done, b * (2 * G0) + max(n - 1, 0))
                        A(y_hi[:], y[:, 0, :], ACT.Copy).then_inc(head_done, 1)
                    else:
                        A(k1[:, grp, :], y[:, 1, :], ACT.Copy).then_inc(head_done, 1)
                for k in range(KD):
                    act.wait_ge(v_done, b * KD + k + 1)
                    A(vt[:, k, :], p_p[k][:], ACT.Copy).then_inc(v_taken, 1)
                act.wait_ge(pv_done, b * STEPS)
                for n in range(2):
                    act.wait_ge(vt_done, b * 2 + n + 1)
                    A(v[:, n * 2:(n + 1) * 2, :], p_p[n][:].rearrange("p (n d) -> p n d", n=2), ACT.Copy).then_inc(v_ready, 1)
                act.wait_ge(norm_done, b * STEPS)
                for n in range(STEPS + LAG):
                    if n < STEPS:
                        h, i = divmod(n, TPB)
                        act.wait_ge(max_done, b * STEPS + n + 1)
                        act.wait_ge(t_done, b * STEPS + max(n - PROBS + 1, 0))
                        A(prob[:, n % PROBS, 0:(i + 1) * P], ring[n % RING][:, 0:(i + 1) * P], ACT.Exp, bias=nmax[:, n % 8:n % 8 + 1],
                          accum_out=sums[:, i * H0 + h:i * H0 + h + 1]).then_inc(exp_done, 1)
                    if n >= LAG and on_act((n - LAG) % TPB):
                        m = n - LAG
                        act.wait_ge(t_done, b * STEPS + m + 1)
                        act.wait_ge(pv_done, b * STEPS + max(m - PROBTS + 1, 0))
                        width = (m % TPB + 1) * P
                        A(probt[:, m % PROBTS, 0:width], p_t[m % 2][:, 0:width], ACT.Copy).then_inc(ta_done, 1)
                    if n % TPB == 1 and n < STEPS:
                        h = n // TPB
                        act.wait_ge(pv_done, b * STEPS + max(h - 1, 0) * TPB)
                        A(v_head[:, h % 2, :, P - DH:P], v[:, :, h * DH:(h + 1) * DH], ACT.Copy).then_inc(vh_ready, 1)
                act.wait_ge(pv_done, (b + 1) * STEPS)
                act.wait_ge(wo_done, b)
                for k in range(KD):
                    last = A(ot[:, k, :], p_o[k][:], ACT.Copy)
                last.then_inc(ot_ready, 1)

        @block.vector
        def _(dve):
            V = nc.vector
            dve.wait_ge(t_loaded, 64)
            V.tensor_copy(below[:], below_f[:]).then_inc(t_loaded, 1)
            with dve.Fori(0, BATCH) as b:
                dve.wait_ge(s_done, b * STEPS)
                for n in range(2 * G0 + 1):
                    if n < 2 * G0:
                        qk = n % 2
                        pair = (p_p, p_s)[n % 2]
                        dve.wait_ge(y_done, b * (2 * G0) + n)
                        dve.wait_ge(ab_done, b * (2 * G0) + n + 1)
                        V.tensor_tensor(t1[:], pair[0][:], tables[:, qk * 2, :], ALU.mult)
                        V.tensor_tensor(t2[:], pair[1][:], tables[:, qk * 2 + 1, :], ALU.mult).then_inc(rope_read, 1)
                    if n >= 1:
                        grp, qk = divmod(n - 1, 2)
                        dve.wait_ge(head_done, b * (2 * G0) + n)
                        if qk == 0:
                            V.scalar_tensor_tensor(q1[:, grp, :], y_hi[:].bitcast(FP32), lower[:, 0:1], y[:, 0, :],
                                                   ALU.mult, ALU.add).then_inc(rope_done, 1)
                        else:
                            V.tensor_tensor(k2[:, grp, :], y[:, 1, :], k1[:, grp, :].bitcast(FP32),
                                            ALU.subtract).then_inc(rope_done, 1)
                    if n < 2 * G0:
                        dve.wait_ge(rope_read, b * (2 * G0) + n + 1)
                        V.tensor_tensor(y[:, n % 2, :], t1[:], t2[:], ALU.add).then_inc(y_done, 1)
                for n in range(STEPS + LAG):
                    if n < STEPS:
                        i = n % TPB
                        dve.wait_ge(s_done, b * STEPS + n + 1)
                        dve.wait_ge(exp_done, b * STEPS + max(n - 7, 0))
                        V.tensor_reduce(nmax[:, n % 8:n % 8 + 1], ring[n % RING][:, 0:(i + 1) * P], AX.X, ALU.max,
                                        negate=True).then_inc(max_done, 1)
                    if 1 <= n <= STEPS:
                        h, i = divmod(n - 1, TPB)
                        total = sums[:, i * H0 + h:i * H0 + h + 1]
                        dve.wait_ge(exp_done, b * STEPS + n)
                        V.reciprocal(total, total).then_inc(inv_done, 1)
                    if 2 <= n <= STEPS + 1:
                        h, i = divmod(n - 2, TPB)
                        rows = prob[:, (n - 2) % PROBS, 0:(i + 1) * P]
                        dve.wait_ge(inv_done, b * STEPS + n - 1)
                        V.tensor_scalar(rows, rows, sums[:, i * H0 + h:i * H0 + h + 1], None, ALU.mult).then_inc(norm_done, 1)
                    if n >= LAG and not on_act((n - LAG) % TPB):
                        m = n - LAG
                        i = m % TPB
                        dve.wait_ge(t_done, b * STEPS + m + 1)
                        dve.wait_ge(pv_done, b * STEPS + max(m - PROBTS + 1, 0))
                        V.tensor_copy(probt[:, m % PROBTS, 0:(i + 1) * P], p_t[m % 2][:, 0:(i + 1) * P]).then_inc(tv_done, 1)
                dve.wait_ge(wo_done, b + 1)
                dve.wait_ge(res_loaded[0], (b // 2 + 1) * 16)
                dve.wait_ge(res_loaded[1], (b // 2 + 1) * 16)
                for n in range(2):
                    rows = out[:, ds(b % 2, 1), n * 2:(n + 1) * 2, :]
                    last = V.tensor_tensor(rows, p_s[n][:].rearrange("p (o n d) -> p o n d", o=1, n=2), rows, ALU.add)
                last.then_inc(out_done, 1)

I0 = 1024
GROUP = 4
GT = I0 // GROUP // P
SLOTS = GT * GROUP

def sparse_swiglu(nc, ctx, src, dst, gate_d, up_d, down_d, g):
    sem = lambda n: nc.alloc_semaphore(name=f"f0_{n}")
    w_loaded, w_split, chain_sem = sem("wload"), sem("wsplit"), sem("chain")
    d_loaded = sem("dload")
    gate_done, up_done, silu_done = sem("gate"), sem("up"), sem("silu")
    h_done, kept_done, mag_done = sem("h"), sem("kept"), sem("mag")
    down_done, out_done, stored, res_loaded = sem("down"), sem("out"), [sem("st0"), sem("st1")], [sem("res0"), sem("res1")]
    with ExitStack() as mem:
        sb = lambda n, s, d=FP32: mem.enter_context(nc.sbuf_tensor(f"f0_{n}", s, d))
        wg_hi, wg_lo, wu_hi, wu_lo = (sb(n, [P, KD, I0], FP32R) for n in ("wgh", "wgl", "wuh", "wul"))
        raw = sb("raw", [P, KD, I0])
        wd = sb("wd", [P, SLOTS, DM])
        silu = sb("silu", [P, 2, SEQ])
        h = sb("h", [P, 2, SLOTS, SEQ])
        mag = sb("mag", [P, GROUP, SEQ])
        beats = sb("beats", [P, 6, SEQ], BF16)
        count = sb("count", [P, GROUP, SEQ], BF16)
        res = sb("res", [P, 2, TPB, DM])
        out = sb("outt", [P, 2, TPB, DM])
        ps = lambda n, s: mem.enter_context(nc.psum_tensor(f"f0_{n}", s, FP32))
        pg = [ps(f"pg{i}", [P, SEQ]) for i in range(2)]
        pu = [ps(f"pu{i}", [P, SEQ]) for i in range(2)]
        pd = [ps(f"pd{i}", [P, TPB, DM]) for i in range(2)]
        block = mem.enter_context(nc.Block())
        src_v = src.rearrange("(b n p) d -> b p n d", p=P, n=TPB)
        dst_v = dst.rearrange("(b n p) d -> b p n d", p=P, n=TPB)

        @block.sync
        def _(sp):
            sp.dma_start(raw[:], gate_d).then_inc(w_loaded, 16)
            sp.dma_start(wd[:], down_d).then_inc(d_loaded, 16)
            sp.wait_ge(w_split, 2)
            sp.dma_start(raw[:], up_d).then_inc(w_loaded, 16)
            sp.sem_inc(stored[0], 16)
            sp.sem_inc(stored[1], 16)
            with sp.Fori(0, BATCH // 2) as i:
                for p in range(2):
                    b = i * 2 + p
                    sp.wait_ge(out_done, b - p)
                    sp.dma_start(res[:, p], src_v[ds(b, 1)].rearrange("a p n d -> p (a n) d")).then_inc(res_loaded[p], 16)
                for p in range(2):
                    b = i * 2 + p
                    sp.wait_ge(out_done, b + 1)
                    sp.dma_start(dst_v[ds(b, 1)].rearrange("a p n d -> p (a n) d"), out[:, p]).then_inc(stored[p], 16)
            for p in range(2):
                sp.wait_ge(stored[p], 16 * (BATCH // 2 + 1))

        def gate_up(pe, b, gt):
            for r in range(GROUP):
                n = b * SLOTS + gt * GROUP + r
                s = gt * GROUP + r
                cols = slice(s * P, (s + 1) * P)
                pe.wait_ge(silu_done, n + 1)
                for k in range(KD):
                    last = matmul3(nc, pg[r % 2][:], wg_hi[:, k, cols], wg_lo[:, k, cols],
                                   g.x_hi[:, k, ds(b * SEQ, SEQ)], g.x_lo[:, k, ds(b * SEQ, SEQ)],
                                   k == 0, k == KD - 1)
                last.then_inc(gate_done, 1)
                pe.wait_ge(h_done, n + 1)
                for k in range(KD):
                    last = matmul3(nc, pu[r % 2][:], wu_hi[:, k, cols], wu_lo[:, k, cols],
                                   g.x_hi[:, k, ds(b * SEQ, SEQ)], g.x_lo[:, k, ds(b * SEQ, SEQ)],
                                   k == 0, k == KD - 1)
                last.then_inc(up_done, 1)

        def down(pe, b, p):
            pe.wait_ge(kept_done, (b + 1) * GT)
            if not (isinstance(b, int) and b < 2):
                pe.wait_ge(out_done, b - 1)
            for n in range(TPB):
                for s in range(SLOTS):
                    last = nc.tensor.matmul(pd[p][:, n, :], h[:, p, s, n * P:(n + 1) * P], wd[:, s, :],
                                            start=s == 0, stop=s == SLOTS - 1)
            last.then_inc(down_done, 1)

        @block.tensor
        def _(pe):
            pe.wait_ge(w_split, 4)
            pe.wait_ge(d_loaded, 16)
            gate_up(pe, 0, 0)
            gate_up(pe, 0, 1)
            gate_up(pe, 1, 0)
            down(pe, 0, 0)
            gate_up(pe, 1, 1)
            with pe.Fori(1, BATCH // 2) as i:
                for p in range(2):
                    b = i * 2 + p
                    gate_up(pe, b, 0)
                    down(pe, b - 1, 1 - p)
                    gate_up(pe, b, 1)
            down(pe, BATCH - 1, 1)

        @block.scalar
        def _(act):
            act.sem_inc(silu_done, 2)
            act.wait_ge(w_loaded, 16)
            nc.scalar.activation(wg_hi[:], raw[:], ACT.Copy).then_inc(w_split, 1)
            act.wait_ge(w_loaded, 32)
            nc.scalar.activation(wu_hi[:], raw[:], ACT.Copy).then_inc(w_split, 1)
            nc.scalar.preload_act_table(ACT.Silu)
            with act.Fori(0, BATCH // 2) as i:
              for p in range(2):
                b = i * 2 + p
                for s in range(SLOTS):
                    n = b * SLOTS + s
                    act.wait_ge(gate_done, n + 1)
                    act.wait_ge(h_done, n + 1)
                    nc.scalar.activation(silu[:, s % 2], pg[s % 2][:], ACT.Silu).then_inc(silu_done, 1)
                    act.wait_ge(h_done, n + 3)
                    if s % GROUP == 0:
                        act.wait_ge(kept_done, b * GT + s // GROUP)
                    nc.scalar.activation(mag[:, s % GROUP], h[:, p, s], ACT.Abs).then_inc(mag_done, 1)

        @block.vector
        def _(dve):
            dve.sem_inc(h_done, 2)
            dve.wait_ge(w_split, 1)
            nc.vector.tensor_tensor(wg_lo[:], raw[:], wg_hi[:].bitcast(FP32), ALU.subtract).then_inc(w_split, 1)
            dve.wait_ge(w_split, 3)
            nc.vector.tensor_tensor(wu_lo[:], raw[:], wu_hi[:].bitcast(FP32), ALU.subtract).then_inc(w_split, 1)
            PER = 6 + 8

            def group_tile(b, p, gt):
                link = Chain(dve, chain_sem, b * (PER * GT) + gt * PER)
                for r in range(GROUP):
                    n = b * SLOTS + gt * GROUP + r
                    s = gt * GROUP + r
                    dve.wait_ge(silu_done, n + 3)
                    dve.wait_ge(up_done, n + 1)
                    nc.vector.tensor_tensor(h[:, p, s], pu[r % 2][:], silu[:, r % 2], ALU.mult).then_inc(h_done, 1)
                pairs = [(0, 1), (0, 2), (0, 3), (1, 2), (1, 3), (2, 3)]
                dve.wait_ge(mag_done, (b * GT + gt + 1) * GROUP)
                for q, (i, j) in enumerate(pairs):
                    link.mark(nc.vector.tensor_tensor(beats[:, q], mag[:, i], mag[:, j], ALU.is_ge))
                link.wait()
                c01, c02, c03, c12, c13, c23 = (beats[:, q] for q in range(6))
                c = [count[:, r] for r in range(GROUP)]
                link.mark(nc.vector.tensor_tensor(c[0], c01, c02, ALU.add))
                link.mark(nc.vector.tensor_tensor(c[1], c12, c13, ALU.add))
                link.mark(nc.vector.tensor_tensor(c[2], c23, c12, ALU.subtract))
                link.mark(nc.vector.tensor_tensor(c[3], c23, c13, ALU.add))
                link.wait(link.n - 3)
                link.mark(nc.vector.tensor_tensor(c[0], c[0], c03, ALU.add))
                link.wait(link.n - 3)
                link.mark(nc.vector.tensor_tensor(c[1], c[1], c01, ALU.subtract))
                link.wait(link.n - 3)
                link.mark(nc.vector.tensor_tensor(c[2], c[2], c02, ALU.subtract))
                link.wait(link.n - 3)
                link.mark(nc.vector.tensor_tensor(c[3], c[3], c03, ALU.add))
                keep = [(ALU.is_ge, 2.0), (ALU.is_ge, 1.0), (ALU.is_ge, 0.0), (ALU.is_le, 1.0)]
                for r, (op, least) in enumerate(keep):
                    link.wait(link.n - 3 + r)
                    s = gt * GROUP + r
                    last = nc.vector.scalar_tensor_tensor(h[:, p, s], c[r], least, h[:, p, s], op, ALU.mult)
                last.then_inc(kept_done, 1)
                dve.wait_ge(kept_done, b * GT + gt + 1)
                assert link.n == PER

            def finish(b, p):
                dve.wait_ge(down_done, b + 1)
                dve.wait_ge(res_loaded[p], (b - p) * 8 + 16)
                dve.wait_ge(stored[p], (b - p) * 8 + 16)
                nc.vector.tensor_tensor(out[:, p], pd[p][:], res[:, p], ALU.add).then_inc(out_done, 1)

            group_tile(0, 0, 0)
            group_tile(0, 0, 1)
            group_tile(1, 1, 0)
            finish(0, 0)
            group_tile(1, 1, 1)
            with dve.Fori(1, BATCH // 2) as i:
                for p in range(2):
                    b = i * 2 + p
                    group_tile(b, p, 0)
                    finish(b - 1, 1 - p)
                    group_tile(b, p, 1)
            finish(BATCH - 1, 1)

H1, N1 = 64, 128
P1 = 8
DIN = H1 * P1
PAIRS = H1 // 2
PW = 2 * P1
COLS = TOK // 2 // P
CW = TOK // 2
UNITS = PAIRS * BATCH
TURN = 2.0 * math.pi
UNDER_TURN = 6.283185
MAGIC = 1.5 * 2.0 ** 23
RMS_EPS = 1e-6
WC = 5 * P
WCH = WC // BATCH

def gates(nc, ctx, w_d, alog_d, tk_dram, rows_dram, g):
    sem = lambda n: nc.alloc_semaphore(name=f"ga_{n}")
    loaded, w_split, z_done, z_taken, chain_sem, act_sem = (sem(n) for n in ("load", "split", "z", "ztaken", "chain", "act"))
    dve_to_act, turned, taken, stored, rows_ready = sem("dve2act"), sem("turned"), sem("taken"), sem("stored"), sem("rows")
    quantity = sem("quantity")
    with ExitStack() as mem:
        sb = lambda n, s, d=FP32: mem.enter_context(nc.sbuf_tensor(f"ga_{n}", s, d))
        raw = sb("raw", [P, KD, 2, 2, P])
        w_hi, w_lo = sb("whi", [P, KD, 2, 2, P], FP32R), sb("wlo", [P, KD, 2, 2, P], FP32R)
        ea = sb("ea", [P, 1])
        z, lam, dt, kap, gam, tmp = (sb(n, [P, CW]) for n in ("z", "lam", "dt", "kap", "gam", "tmp"))
        cum, keep = sb("cum", [P, CW]), sb("keep", [P, CW])
        part = sb("part", [P, 3, 2, CW], BF16)
        tk = sb("tk", [P, PAIRS, 4, 2, COLS, 2])
        ps = lambda n, s: mem.enter_context(nc.psum_tensor(f"ga_{n}", s, FP32))
        pz = [ps(f"z{i}", [P, SEQ]) for i in range(2)]
        pt = [ps(f"t{i}", [P, 4, P]) for i in range(2)]
        block = mem.enter_context(nc.Block())
        PB = BATCH // 2

        @block.sync
        def _(sp):
            sp.dma_start(raw[:], w_d).then_inc(loaded, 16)
            sp.dma_start(ea[:], alog_d).then_inc(loaded, 16)
            sp.wait_ge(rows_ready, 1)
            sp.dma_start(rows_dram.rearrange("(r s) q c -> r s q c", s=3), part[:]).then_inc(stored, 16)
            sp.wait_ge(taken, 16 * 2)
            sp.dma_start(tk_dram.rearrange("a p c -> p a c"), tk[:].rearrange("p a q j c h -> p a (q j c h)")).then_inc(stored, 16)
            sp.wait_ge(stored, 32)

        @block.tensor
        def _(pe):
            pe.wait_ge(w_split, 2)
            for n in range(2 * PB):
                q, c = divmod(n, PB)
                if n >= 2:
                    pe.wait_ge(z_taken, n - 1)
                for j in range(2):
                    for k in range(KD):
                        tok = slice((2 * c + j) * SEQ, (2 * c + j + 1) * SEQ)
                        last = matmul3(nc, pz[n % 2][:], w_hi[:, k, q, j, :], w_lo[:, k, q, j, :], g.x_hi[:, k, tok],
                                       g.x_lo[:, k, tok], j == 0 and k == 0, j == 1 and k == KD - 1)
                last.then_inc(z_done, 1)
            for n in range(16):
                q, f = divmod(n, 4)
                if n == 0:
                    pe.wait_ge(quantity, 3)
                if n >= 2:
                    pe.wait_ge(taken, 2 * (n - 1))
                for c in range(4):
                    col = f * 4 + c
                    last = nc.tensor.transpose(pt[n % 2][:, c, :], (kap, tmp, gam, lam)[q][:, col * P:(col + 1) * P], g.ident[:])
                last.then_inc(turned, 1)

        @block.scalar
        def _(act):
            A = nc.scalar.activation
            for n in range(2 * PB):
                q, c = divmod(n, PB)
                act.wait_ge(z_done, n + 1)
                A((z, lam)[q][:, c * SEQ:(c + 1) * SEQ], pz[n % 2][:], ACT.Copy).then_inc(z_taken, 1)
            act.wait_ge(z_taken, 2 * PB)
            act.wait_ge(loaded, 32)
            A(lam[:], lam[:], ACT.Sigmoid).then_inc(act_sem, 1)
            A(dt[:], z[:], ACT.Abs).then_inc(act_sem, 1)
            A(ea[:], ea[:], ACT.Exp).then_inc(act_sem, 1)
            act.wait_ge(act_sem, 3)
            A(dt[:], dt[:], ACT.Exp, scale=-1.0).then_inc(act_sem, 1)
            act.wait_ge(act_sem, 4)
            A(dt[:], dt[:], ACT.Ln, bias=1.0).then_inc(act_sem, 1)
            act.wait_ge(dve_to_act, 1)
            A(tmp[:], tmp[:], ACT.Exp).then_inc(act_sem, 1)
            act.wait_ge(dve_to_act, 2)
            A(lam[:], cum[:], ACT.Exp).then_inc(quantity, 1)
            for n in range(16):
                q, f = divmod(n, 4)
                act.wait_ge(turned, n + 1)
                for j in range(2):
                    A(tk[:, :, q, j, f * 4:f * 4 + 4, :],
                      pt[n % 2][:, :, j * H1:(j + 1) * H1].rearrange("p c (a h) -> p a c h", h=2),
                      ACT.Copy).then_inc(taken, 1)

        @block.vector
        def _(dve):
            V = nc.vector
            link = Chain(dve, chain_sem)
            dve.wait_ge(loaded, 32)
            V.tensor_copy(w_hi[:], raw[:]).then_inc(w_split, 1)
            dve.wait_ge(w_split, 1)
            V.tensor_tensor(w_lo[:], raw[:], w_hi[:].bitcast(FP32), ALU.subtract).then_inc(w_split, 1)
            link(V.memset(keep[:], 1.0))
            link(V.memset(keep[:].rearrange("p (c t) -> p c t", t=P)[:, :, 0:1], 0.0))
            dve.wait_ge(act_sem, 5)
            link(V.scalar_tensor_tensor(dt[:], z[:], 0.0, dt[:], ALU.max, ALU.add))
            link.mark(V.tensor_tensor(gam[:], lam[:], dt[:], ALU.mult))
            link(V.tensor_scalar(z[:], dt[:], ea[:, 0:1], -1.0, ALU.mult, ALU.mult))
            link.mark(V.tensor_tensor_scan(cum[:], keep[:], z[:], 0.0, ALU.mult, ALU.add))
            link.mark(V.tensor_tensor(tmp[:], dt[:], gam[:], ALU.subtract))
            link.wait()
            link.mark(V.tensor_tensor(kap[:, 0:CW - 1], gam[:, 0:CW - 1], tmp[:, 1:CW], ALU.add))
            link(V.tensor_copy(kap[:, CW - 1:CW], gam[:, CW - 1:CW]))
            chunks = cum[:].rearrange("p (c t) -> p c t", t=P)
            ends = chunks[:, :, P - 1:P].broadcast_to([P, COLS, P])
            V.tensor_tensor(tmp[:].rearrange("p (c t) -> p c t", t=P), ends, chunks, ALU.subtract).then_inc(dve_to_act, 1)
            link(V.tensor_scalar(z[:], kap[:], 1e-37, None, ALU.max))
            link(V.reciprocal(z[:], z[:]))
            V.tensor_tensor(gam[:], gam[:], z[:], ALU.mult).then_inc(quantity, 1)
            dve.wait_ge(act_sem, 6)
            V.tensor_tensor(tmp[:], tmp[:], kap[:], ALU.mult).then_inc(quantity, 1)
            link(V.tensor_scalar(dt[:], dt[:], 1.0 / TURN, None, ALU.mult))
            nc.vector.tensor_copy(keep[:], cum[:]).then_inc(dve_to_act, 1)
            dve.wait_ge(dve_to_act, 2)
            for q, v in enumerate((dt, keep)):
                for s in range(2):
                    link(V.tensor_copy(part[:, s, q, :], v[:]))
                    link(V.tensor_tensor(v[:], v[:], part[:, s, q, :], ALU.subtract))
                last = V.tensor_copy(part[:, 2, q, :], v[:])
                if q == 0:
                    link(last)
            last.then_inc(rows_ready, 1)

def input_projection(nc, ctx, w_d, xp_dram, g):
    sem = lambda n: nc.alloc_semaphore(name=f"xp_{n}")
    loaded, w_split, staged, done, taken = sem("load"), sem("split"), sem("staged"), sem("done"), sem("taken")
    stored = [sem("st0"), sem("st1")]
    with ExitStack() as mem:
        sb = lambda n, s, d=FP32: mem.enter_context(nc.sbuf_tensor(f"xp_{n}", s, d))
        raw = sb("raw", [P, KD, DIN])
        w_hi, w_lo = sb("whi", [P, KD, DIN], FP32R), sb("wlo", [P, KD, DIN], FP32R)
        s_hi, s_lo = sb("shi", [P, 2, KD, P], FP32R), sb("slo", [P, 2, KD, P], FP32R)
        out = sb("outt", [P, 2, DIN])
        px = [mem.enter_context(nc.psum_tensor(f"xp_ps{i}", [P, DIN], FP32)) for i in range(2)]
        block = mem.enter_context(nc.Block())
        xp_v = xp_dram.rearrange("(n p) d -> n p d", p=P)

        @block.sync
        def _(sp):
            sp.dma_start(raw[:], w_d).then_inc(loaded, 16)
            with sp.Fori(0, TILES // 2) as i:
                for p in range(2):
                    t = i * 2 + p
                    sp.wait_ge(taken, t + 3)
                    sp.dma_start(xp_v[ds(t, 1)].rearrange("a p d -> p (a d)"), out[:, p]).then_inc(stored[p], 16)
            for p in range(2):
                sp.wait_ge(stored[p], 16 * (TILES // 2))

        @block.vector
        def _(dve):
            dve.wait_ge(loaded, 16)
            nc.vector.tensor_copy(w_hi[:], raw[:]).then_inc(w_split, 1)
            dve.wait_ge(w_split, 1)
            nc.vector.tensor_tensor(w_lo[:], raw[:], w_hi[:].bitcast(FP32), ALU.subtract).then_inc(w_split, 1)
            with dve.Fori(0, TILES // 2) as i:
                for p in range(2):
                    t = i * 2 + p
                    dve.wait_ge(done, t + 1)
                    cols = ds(t * P, P)
                    nc.vector.tensor_copy(s_hi[:, p], g.x_hi[:, :, cols].bitcast(FP32))
                    nc.vector.tensor_copy(s_lo[:, p], g.x_lo[:, :, cols].bitcast(FP32)).then_inc(staged, 1)

        @block.tensor
        def _(pe):
            pe.sem_inc(done, 2)
            pe.wait_ge(w_split, 2)
            with pe.Fori(0, TILES // 2) as i:
                for p in range(2):
                    t = i * 2 + p
                    pe.wait_ge(staged, t + 1)
                    pe.wait_ge(taken, t + 1)
                    for k in range(KD):
                        last = matmul3(nc, px[p][:], s_hi[:, p, k], s_lo[:, p, k], w_hi[:, k], w_lo[:, k],
                                       k == 0, k == KD - 1)
                    last.then_inc(done, 1)

        @block.scalar
        def _(act):
            act.sem_inc(taken, 2)
            with act.Fori(0, TILES // 2) as i:
                for p in range(2):
                    t = i * 2 + p
                    act.wait_ge(done, t + 3)
                    act.wait_ge(stored[p], 16 * i)
                    nc.scalar.activation(out[:, p], px[p][:], ACT.Copy).then_inc(taken, 1)

def output_projection(nc, ctx, src, dst, wz_d, wout_d, y_dram, g):
    sem = lambda n: nc.alloc_semaphore(name=f"op_{n}")
    loaded, w_split, staged, z_done, silu_done, gated = (sem(n) for n in ("load", "split", "staged", "z", "silu", "gated"))
    turned, yt_ready, out_done, added = sem("turned"), sem("yt"), sem("outd"), sem("added")
    stored = [sem("st0"), sem("st1")]
    in_y, in_x = [sem("iny0"), sem("iny1")], [sem("inx0"), sem("inx1")]
    KO = DIN // P
    with ExitStack() as mem:
        sb = lambda n, s, d=FP32: mem.enter_context(nc.sbuf_tensor(f"op_{n}", s, d))
        raw = sb("raw", [P, KD, DIN])
        w_hi, w_lo = sb("whi", [P, KD, DIN], FP32R), sb("wlo", [P, KD, DIN], FP32R)
        wo = sb("wo", [P, KO, DM])
        s_hi, s_lo = sb("shi", [P, 2, KD, P], FP32R), sb("slo", [P, 2, KD, P], FP32R)
        y, silu, yt, out = sb("y", [P, 2, DIN]), sb("silu", [P, 2, DIN]), sb("yt", [P, 2, KO, P]), sb("outt", [P, 2, DM])
        ps = lambda n, s: [mem.enter_context(nc.psum_tensor(f"op_ps{n}{i}", s, FP32)) for i in range(2)]
        pz, pt, po = ps("z", [P, DIN]), ps("t", [P, KO, P]), ps("o", [P, DM])
        block = mem.enter_context(nc.Block())
        y_v = y_dram.rearrange("(n p) d -> n p d", p=P)
        src_v = src.rearrange("(n p) d -> n p d", p=P)
        dst_v = dst.rearrange("(n p) d -> n p d", p=P)

        @block.sync
        def _(sp):
            sp.dma_start(raw[:], wz_d).then_inc(loaded, 16)
            sp.dma_start(wo[:], wout_d).then_inc(loaded, 16)
            with sp.Fori(0, TILES // 2) as i:
                for p in range(2):
                    t = i * 2 + p
                    sp.wait_ge(turned, i * 2)
                    sp.dma_start(y[:, p], y_v[ds(t, 1)].rearrange("a p d -> p (a d)")).then_inc(in_y[p], 16)
                    sp.wait_ge(stored[p], 16 * i)
                    sp.dma_start(out[:, p], src_v[ds(t, 1)].rearrange("a p d -> p (a d)")).then_inc(in_x[p], 16)
                for p in range(2):
                    t = i * 2 + p
                    sp.wait_ge(added, t + 1)
                    sp.dma_start(dst_v[ds(t, 1)].rearrange("a p d -> p (a d)"), out[:, p]).then_inc(stored[p], 16)
            for p in range(2):
                sp.wait_ge(stored[p], 16 * (TILES // 2))

        @block.gpsimd
        def _(pool):
            with pool.Fori(0, TILES // 2) as i:
                for p in range(2):
                    t = i * 2 + p
                    pool.wait_ge(z_done, i * 2)
                    cols = ds(t * P, P)
                    nc.gpsimd.tensor_copy(s_hi[:, p], g.x_hi[:, :, cols].bitcast(FP32))
                    nc.gpsimd.tensor_copy(s_lo[:, p], g.x_lo[:, :, cols].bitcast(FP32)).then_inc(staged, 1)

        @block.tensor
        def _(pe):
            pe.wait_ge(w_split, 2)
            pe.wait_ge(loaded, 32)
            with pe.Fori(0, TILES // 2) as i:
                for p in range(2):
                    t = i * 2 + p
                    pe.wait_ge(staged, t + 1)
                    pe.wait_ge(silu_done, i * 2)
                    for k in range(KD):
                        last = matmul3(nc, pz[p][:], s_hi[:, p, k], s_lo[:, p, k], w_hi[:, k], w_lo[:, k],
                                       k == 0, k == KD - 1)
                    last.then_inc(z_done, 1)
                for p in range(2):
                    t = i * 2 + p
                    pe.wait_ge(gated, t + 1)
                    pe.wait_ge(yt_ready, i * 2)
                    for k in range(KO):
                        last = nc.tensor.transpose(pt[p][:, k, :], y[:, p, k * P:(k + 1) * P], g.ident[:])
                    last.then_inc(turned, 1)
                for p in range(2):
                    t = i * 2 + p
                    pe.wait_ge(yt_ready, t + 1)
                    pe.wait_ge(added, i * 2)
                    for k in range(KO):
                        last = nc.tensor.matmul(po[p][:], yt[:, p, k, :], wo[:, k, :], start=k == 0, stop=k == KO - 1)
                    last.then_inc(out_done, 1)

        @block.scalar
        def _(act):
            A = nc.scalar.activation
            act.wait_ge(loaded, 32)
            A(w_hi[:], raw[:], ACT.Copy).then_inc(w_split, 1)
            nc.scalar.preload_act_table(ACT.Silu)
            with act.Fori(0, TILES // 2) as i:
                for p in range(2):
                    t = i * 2 + p
                    act.wait_ge(z_done, t + 1)
                    act.wait_ge(gated, i * 2)
                    A(silu[:, p], pz[p][:], ACT.Silu).then_inc(silu_done, 1)
                for p in range(2):
                    t = i * 2 + p
                    act.wait_ge(turned, t + 1)
                    act.wait_ge(out_done, i * 2)
                    A(yt[:, p], pt[p][:], ACT.Copy).then_inc(yt_ready, 1)

        @block.vector
        def _(dve):
            dve.wait_ge(w_split, 1)
            nc.vector.tensor_tensor(w_lo[:], raw[:], w_hi[:].bitcast(FP32), ALU.subtract).then_inc(w_split, 1)
            with dve.Fori(0, TILES // 2) as i:
                for p in range(2):
                    t = i * 2 + p
                    dve.wait_ge(silu_done, t + 1)
                    dve.wait_ge(in_y[p], 16 * i + 16)
                    nc.vector.tensor_tensor(y[:, p], y[:, p], silu[:, p], ALU.mult).then_inc(gated, 1)
                for p in range(2):
                    t = i * 2 + p
                    dve.wait_ge(out_done, t + 1)
                    dve.wait_ge(in_x[p], 16 * i + 16)
                    nc.vector.tensor_tensor(out[:, p], po[p][:], out[:, p], ALU.add).then_inc(added, 1)

def state_space(nc, ctx, w_dram, norm_d, bias_d, const_d, strict_d, blocks_d, tk_dram, rows_dram, xp_dram, y_dram, g):
    sem = lambda n: nc.alloc_semaphore(name=f"ss_{n}")
    const_in, const_ready = sem("constin"), sem("constready")
    rows_in, wraw_in, pair_in = [sem("rows0"), sem("rows1")], [sem("wraw0"), sem("wraw1")], [sem("pair0"), sem("pair1")]
    y_out = [sem("yout0"), sem("yout1")]
    w_split = sem("wsplit")
    dtb_done, th_done, bc_done, e_done, ss_done, g_done = (sem(n) for n in ("dtb", "th", "bc", "e", "ss", "g"))
    t_done, u_done, yp_done = sem("t"), sem("u"), sem("yp")
    dtb_copied, xw_done, d_done, r_done, bt_done, trig_done, abs_done = (sem(n) for n in ("dtbc", "xw", "d", "r", "bt", "trig", "abs"))
    ln_done, ae_done, aend_done = sem("ln"), sem("ae"), sem("aend")
    thdt_done, fr_done, rope_b, rope_c, gm_done, s_ready, y_ready, chain_sem = (
        sem(n) for n in ("thdt", "fr", "ropeb", "ropec", "gm", "sready", "yready", "chain"))
    sq_done, xk_done, dd_done, um_done, yb_done, pool_chain = (sem(n) for n in ("sq", "xk", "dd", "um", "yb", "pchain"))
    with ExitStack() as mem:
        sb = lambda n, s, d=FP32: mem.enter_context(nc.sbuf_tensor(f"ss_{n}", s, d))
        w_hi, w_lo = sb("whi", [P, 2, KD, WC], FP32R), sb("wlo", [P, 2, KD, WC], FP32R)
        w_raw = sb("wraw", [P, 2, KD, WCH])
        xp = sb("xp", [P, 2, TILES, PW])
        tk = sb("tk", [P, 2, 4, 2, COLS * 2])
        yo = sb("yo", [P, 2, TILES, PW])
        rows = sb("rows", [6, 2, 2, SEQ], BF16)
        norm = sb("norm", [P, 4])
        bias = sb("bias", [P, PAIRS, 4])
        con_f, con = sb("conf", [6, 5, P]), sb("con", [6, 5, P], BF16)
        strict_f, strict = sb("strictf", [P, P]), sb("strict", [P, 4, P], BF16)
        blocks = sb("blocks", [P, PW])
        eps, quarter = sb("eps", [P, 1]), sb("quarter", [P, 1])
        dtb, th, fr = sb("dtb", [P, SEQ]), sb("th", [P, SEQ]), sb("fr", [P, SEQ])
        sin, cos = sb("sin", [P, 2, SEQ]), sb("cos", [P, 2, SEQ])
        sq = sb("sq", [P, 4, SEQ])
        xw = sb("xw", [P, 2, 4, SEQ])
        r = sb("r", [P, 2, SEQ])
        tmp = sb("tmp", [P, 4, SEQ])
        rot = sb("rot", [P, 2, 4, SEQ])
        dec = sb("dec", [P, 2, 8, P])
        pairs_sum = sb("pairssum", [P, P])
        ones = sb("ones", [P, SEQ])
        own = sb("own", [P, 8, P])
        gm = sb("gm", [P, 8, P])
        bt = sb("bt", [P, 3, 2, P])
        xk, xe = sb("xk", [P, 2, TPB, PW]), sb("xe", [P, 2, TPB, PW])
        aend = sb("aend", [P, 2, TPB])
        state = sb("state", [P, 3, 2 * PW])
        inter = sb("inter", [P, 3, PW])
        ps = lambda n, s: mem.enter_context(nc.psum_tensor(f"ss_ps{n}", s, FP32))
        ring = [ps(f"r{i}", [P, SEQ]) for i in range(3)]
        pe_g = ps("eg", [P, 8, P])
        p_st = ps("st", [P, 8, P])
        p_u = ps("u", [P, SEQ])
        y_in, y_far = p_u[:, P:P + TPB * PW], p_u[:, P + TPB * PW:P + (2 * TPB - 1) * PW]
        p_ae = p_u[:, 256:256 + TPB]
        block = mem.enter_context(nc.Block())
        xp_v = xp_dram.rearrange("(t p) (a c) -> a p t c", p=P, c=PW)
        y_v = y_dram.rearrange("(t p) (a c) -> a p t c", p=P, c=PW)
        at_start = 12 + 8
        HP = H1

        @block.sync
        def _(sp):
            for dst, s in ((norm, norm_d), (bias, bias_d), (con_f, const_d), (strict_f, strict_d), (blocks, blocks_d)):
                sp.dma_start(dst[:], s).then_inc(const_in, 16)

            def load_pair(pair, par):
                sp.dma_start(xp[:, par], xp_v[ds(pair, 1)].rearrange("a p t c -> p (a t) c")).then_inc(pair_in[par], 16)
                sp.dma_start(tk[:, par].rearrange("p q j c -> p (q j c)"),
                             tk_dram[ds(pair, 1)].rearrange("a p c -> p (a c)")).then_inc(pair_in[par], 16)

            def load_chunk(pair, b, j):
                sp.dma_start(w_raw[:, j], w_dram[ds(pair, 1), :, :, ds(b * WCH, WCH)]
                             .rearrange("a p k c -> p (a k) c")).then_inc(wraw_in[j], 16)

            load_pair(0, 0)
            for b in range(BATCH):
                if b >= 2:
                    sp.wait_ge(w_split, b - 1)
                load_chunk(0, b, b % 2)
            def turns(pair, nxt, i):
                for j in range(2):
                    u = pair * BATCH + i * 2 + j
                    sp.wait_ge(w_split, u + 7)
                    load_chunk(nxt, i * 2 + j, j)
                    sp.wait_ge(e_done, u)
                    sp.dma_start(rows[:, j], rows_dram[ds((j * H1 + pair * 2) * 3, 6), :, ds(i * SEQ, SEQ)])\
                      .then_inc(rows_in[j], 16)

            with sp.Fori(0, PAIRS // 2) as pp:
                for par in range(2):
                    pair = pp * 2 + par
                    nxt = (pair + 1) % PAIRS
                    turns(pair, nxt, 0)
                    sp.wait_ge(y_ready, pair * BATCH + 2)
                    load_pair(nxt, 1 - par)
                    sp.dma_start(y_v[ds((pair + PAIRS - 1) % PAIRS, 1)].rearrange("a p t c -> p (a t) c"),
                                 yo[:, 1 - par]).then_inc(y_out[1 - par], 16)
                    with sp.Fori(1, BATCH // 2) as i:
                        turns(pair, nxt, i)
            sp.wait_ge(y_ready, UNITS + 2)
            sp.dma_start(y_v[PAIRS - 1], yo[:, 1]).then_inc(y_out[1], 16)
            sp.wait_ge(y_out[0], 16 * (PAIRS // 2))
            sp.wait_ge(y_out[1], 16 * (PAIRS // 2 + 1))
            for j in range(2):
                sp.wait_ge(pair_in[j], 32 * (PAIRS // 2 + (1 - j)))

        @block.gpsimd
        def _(pool):
            G = nc.gpsimd
            G.memset(rot[:], 0.0).then_inc(const_ready, 1)
            G.memset(dec[:, 1], 0.0).then_inc(const_ready, 1)
            G.memset(xk[:], 0.0).then_inc(const_ready, 1)
            G.memset(xe[:, 1], 0.0).then_inc(const_ready, 1)
            G.memset(aend[:, 1], 0.0).then_inc(const_ready, 1)
            G.memset(gm[:], 0.0).then_inc(const_ready, 1)
            G.memset(state[:], 0.0).then_inc(const_ready, 1)
            G.memset(xw[:, 1], 0.0).then_inc(const_ready, 1)
            G.memset(sin[:, 1], 0.0).then_inc(const_ready, 1)
            G.memset(cos[:, 1], 0.0).then_inc(const_ready, 1)
            G.memset(r[:], 0.0).then_inc(const_ready, 1)
            G.memset(own[:], 0.0).then_inc(const_ready, 1)
            G.memset(tk[:, 1], 0.0).then_inc(const_ready, 1)
            G.memset(yo[:, 1], 0.0).then_inc(const_ready, 1)

            for b in range(BATCH):
                pool.wait_ge(wraw_in[b % 2], 16 * (b // 2 + 1))
                cols = slice(b * WCH, (b + 1) * WCH)
                G.tensor_copy(w_hi[:, 0, :, cols], w_raw[:, b % 2]).then_inc(pool_chain, 1)
                pool.wait_ge(pool_chain, b + 1)
                G.tensor_tensor(w_lo[:, 0, :, cols], w_raw[:, b % 2], w_hi[:, 0, :, cols].bitcast(FP32),
                                ALU.subtract).then_inc(w_split, 1)
            pool.wait_ge(const_in, 16 * 5)

            def decays(u, j):
                pool.wait_ge(d_done, u)
                pool.wait_ge(xk_done, 2 * u)
                G.tensor_tensor(dec[:, j], dec[:, j], own[:], ALU.add).then_inc(dd_done, 1)

            def rotations(u, j):
                for e, op in ((0, ALU.subtract), (1, ALU.add)):
                    pool.wait_ge(rope_b, 2 * u + e + 1)
                    G.tensor_tensor(rot[:, j, e], rot[:, j, e], tmp[:, e], op).then_inc(yb_done, 1)

            with pool.Fori(0, UNITS // 2) as i:
                for j in range(2):
                    u = i * 2 + j
                    b, pair = u % BATCH, u // BATCH
                    par = pair % 2
                    decays(u, 1 - j)
                    rotations(u, 1 - j)
                    for q in range(2):
                        pool.wait_ge(xw_done, 4 * u + 2 * q + 6)
                        pool.wait_ge(ss_done, 2 * u)
                        G.tensor_tensor(sq[:, 2 * q], sq[:, 2 * q], sq[:, 2 * q + 1], ALU.add).then_inc(sq_done, 1)
                    pool.wait_ge(wraw_in[j], (i + 5) * 16)
                    G.tensor_copy(w_hi[:, ds(1 - par, 1), :, ds(b * WCH, WCH)], w_raw[:, j:j + 1]).then_inc(pool_chain, 1)
                    pool.wait_ge(pool_chain, u + BATCH + 1)
                    G.tensor_tensor(w_lo[:, ds(1 - par, 1), :, ds(b * WCH, WCH)], w_raw[:, j:j + 1],
                                    w_hi[:, ds(1 - par, 1), :, ds(b * WCH, WCH)].bitcast(FP32), ALU.subtract)\
                     .then_inc(w_split, 1)
                    pool.wait_ge(pair_in[0], (pair // 2 + 1) * 32)
                    pool.wait_ge(pair_in[1], ((pair + 1) // 2) * 32)
                    pool.wait_ge(yp_done, u + 1)
                    tk_of = lambda q: tk[:, ds(par, 1), q, j, ds((b // 2) * 8, 8)].rearrange("p a (g o) -> p (a g) o", o=1)
                    xp_u = xp[:, ds(par, 1), ds(b * TPB, TPB), :].rearrange("p a c (h d) -> p (a c h) d", d=P1)
                    G.tensor_tensor(xk[:, j].rearrange("p c (h d) -> p (c h) d", d=P1), xp_u,
                                    tk_of(0).broadcast_to([P, 8, P1]), ALU.mult)
                    G.tensor_tensor(xe[:, j].rearrange("p c (h d) -> p (c h) d", d=P1), xp_u,
                                    tk_of(1).broadcast_to([P, 8, P1]), ALU.mult).then_inc(xk_done, 1)
                    at_diagonal = tk[:, ds(par, 1), 2, j, ds((b // 2) * 8, 8)].rearrange("p a (c h o) -> p (a h) c o", h=2, o=1)
                    G.tensor_tensor(own[:].rearrange("p (h c) t -> p h c t", h=2),
                                    g.ident[:].rearrange("p (a o t) -> p a o t", a=1, o=1).broadcast_to([P, 2, TPB, P]),
                                    at_diagonal.broadcast_to([P, 2, TPB, P]), ALU.mult).then_inc(xk_done, 1)
            decays(UNITS, 1)
            rotations(UNITS, 1)

        @block.tensor
        def _(pe):
            M, T = nc.tensor.matmul, nc.tensor.transpose

            def project(n, w, wpar, b, k_tok=None):
                for k in range(KD):
                    cols = slice(w * P, (w + 1) * P)
                    tok = ds(b * SEQ, SEQ)
                    last = matmul3(nc, ring[n][:], w_hi[:, wpar, k, cols], w_lo[:, wpar, k, cols],
                                   g.x_hi[:, k, tok], g.x_lo[:, k, tok], k == 0, k == KD - 1)
                return last

            def scores(bank, j):
                for blk in range(4):
                    n = bank * 4 + blk
                    h, c = divmod(n, TPB)
                    at, cols = slice(h * HP, (h + 1) * HP), slice(c * P, (c + 1) * P)
                    for e in range(2):
                        last = M(pe_g[:, n, :], rot[at, j, e, cols], rot[at, j, 2 + e, cols], start=e == 0, stop=e == 1)
                return last

            nothing = lambda *_: None

            def second(u, j, rest, squares, exponents):
                pe.wait_ge(yb_done, 2 * u + 2)
                pe.wait_ge(ln_done, 2 * u)
                for c in range(3):
                    for e in range(2):
                        last = T(p_st[:, c * 2 + e, :], rot[:, j, e, c * P:(c + 1) * P], g.ident[:])
                last.then_inc(t_done, 1)
                rest()
                pe.wait_ge(bt_done, u + 1)
                squares(0)
                pe.wait_ge(xk_done, 2 * u)
                pe.wait_ge(y_ready, u + 1)
                pe.wait_ge(aend_done, u if squares is nothing else u + 1)
                for c in range(3):
                    for e in range(2):
                        last = M(p_u[:, (c * 2 + e) * PW:(c * 2 + e + 1) * PW], bt[:, c, e, :], xe[:, j, c, :],
                                 start=True, stop=True)
                last.then_inc(u_done, 1)
                squares(1)
                pe.wait_ge(rope_c, 2 * u + 2)
                pe.wait_ge(d_done, u)
                scores(0, j).then_inc(g_done, 1)
                scores(1, j).then_inc(g_done, 1)
                exponents()

            def outputs_near(u, j, head):
                pe.wait_ge(gm_done, 2 * u)
                pe.wait_ge(s_ready, u)
                pe.wait_ge(y_ready, u)
                for c in range(TPB):
                    cols = slice((c * 2 + head) * P1, (c * 2 + head + 1) * P1)
                    M(y_in[:, cols], gm[:, head * TPB + c, :], xk[:, j, c, head * P1:(head + 1) * P1], start=True, stop=True)

            def outputs_far(u, j):
                for c in range(1, TPB):
                    for e in range(2):
                        last = M(y_far[:, (c - 1) * PW:c * PW], rot[:, j, 2 + e, c * P:(c + 1) * P],
                                 state[:, c - 1, e * PW:(e + 1) * PW], start=e == 0, stop=e == 1)
                last.then_inc(yp_done, 1)

            def outputs(u, j):
                for head in range(2):
                    outputs_near(u, j, head)
                outputs_far(u, j)

            def turn(u, b, j, wpar, i):
                rw = rows[:, j]
                pe.wait_ge(rows_in[j], i)
                pe.wait_ge(xw_done, 4 * u + 2)
                M(ring[0][:], con[:, 0, :], rw[:, 0, :], start=True, stop=True).then_inc(dtb_done, 1)
                pe.wait_ge(xw_done, 4 * u + 3)
                project(1, 0, wpar, b).then_inc(th_done, 1)
                outputs_near(u, j, 0)
                pe.wait_ge(xw_done, 4 * u + 4)
                project(2, 1, wpar, b).then_inc(bc_done, 1)
                outputs_near(u, j, 1)
                pe.wait_ge(dtb_copied, u + 1)
                project(0, 2, wpar, b).then_inc(bc_done, 1)
                outputs_far(u, j)
                pe.wait_ge(thdt_done, u + 1)
                project(1, 3, wpar, b).then_inc(bc_done, 1)

                def rest():
                    pe.wait_ge(xw_done, 4 * u + 5)
                    project(2, 4, wpar, b).then_inc(bc_done, 1)
                    pe.wait_ge(y_ready, u + 1)
                    M(p_ae, con[:, 0, :], rw[:, 1, :].rearrange("p (c t) -> p c t", t=P)[:, :, P - 1],
                      start=True, stop=True).then_inc(ae_done, 1)

                def squares(q):
                    pe.wait_ge(sq_done, 2 * u + q + 1)
                    M(p_st[:, q * 4:q * 4 + 4, :].rearrange("p a b -> p (a b)"), pairs_sum[:], sq[:, 2 * q],
                      start=True, stop=True).then_inc(ss_done, 1)

                def exponents():
                    for half in range(2):
                        pe.wait_ge(gm_done, 2 * u + half + 1)
                        bank = pe_g[:, half * 4:half * 4 + 4, :]
                        M(bank.rearrange("p a b -> p (a b)"), g.ident16[:], strict[:].rearrange("p a b -> p (a b)"),
                          start=True, stop=False, skip_group_check=True)
                        for blk in range(4):
                            n = half * 4 + blk
                            h, c = divmod(n, TPB)
                            cols = slice(c * P, (c + 1) * P)
                            M(pe_g[:, n, :], con[:, 1 + h, :], rw[:, 1, cols], start=False, stop=False, skip_group_check=True)
                            last = M(pe_g[:, n, :], rw[:, 1, cols], con[:, 3 + h, :], start=False, stop=True,
                                     skip_group_check=True)
                    last.then_inc(e_done, 1)
                second(u, 1 - j, rest, squares, exponents)

            pe.wait_ge(const_ready, at_start)
            pe.sem_inc(e_done, 1)
            with pe.Fori(0, PAIRS // 2) as pp:
                for par in range(2):
                    with pe.Fori(0, BATCH // 2) as i:
                        for j in range(2):
                            b = i * 2 + j
                            u = (pp * 2 + par) * BATCH + b
                            if j == 0:
                                pe.wait_ge(w_split, (pp * 2 + par + 1) * BATCH)
                            turn(u, b, j, par, ((pp * 2 + par) * (BATCH // 2) + i + 1) * 16)
            outputs(UNITS, 0)
            second(UNITS, 1, nothing, nothing, nothing)
            outputs(UNITS + 1, 1)

        @block.scalar
        def _(act):
            A = nc.scalar.activation
            act.wait_ge(const_in, 16 * 5)
            act.wait_ge(const_ready, at_start)
            act.sem_inc(xw_done, 4)
            act.sem_inc(r_done, 2)
            nc.scalar.preload_act_table(ACT.Exp)

            def take_b(u):
                act.wait_ge(t_done, u + 1)
                act.wait_ge(u_done, u)
                A(bt[:].rearrange("p c e t -> p (c e) t"), p_st[:, 0:6, :], ACT.Copy).then_inc(bt_done, 1)

            with act.Fori(0, UNITS // 2) as i:
                for j in range(2):
                    u = i * 2 + j
                    act.wait_ge(dtb_done, u + 1)
                    act.wait_ge(thdt_done, u)
                    A(dtb[:], ring[0][:], ACT.Copy).then_inc(dtb_copied, 1)

                    def tile(n, bank):
                        act.wait_ge(bc_done, 4 * u + n + 1)
                        if n == 0:
                            act.wait_ge(ss_done, 2 * u)
                            act.wait_ge(rope_c, 2 * u)
                        A(sq[:, n], ring[bank][:], ACT.Square)
                        A(xw[:, j, n], ring[bank][:], ACT.Identity, scale=norm[:, n:n + 1]).then_inc(xw_done, 1)
                    tile(0, 2)
                    tile(1, 0)
                    tile(2, 1)
                    take_b(u)
                    tile(3, 2)
                    act.wait_ge(s_ready, u)
                    act.wait_ge(ae_done, u + 1)
                    A(aend[:, j], p_ae, ACT.Exp).then_inc(aend_done, 1)
                    act.wait_ge(fr_done, u + 1)
                    A(sin[:, j], fr[:], ACT.Sin, scale=-UNDER_TURN)
                    A(cos[:, j], fr[:], ACT.Abs).then_inc(abs_done, 1)
                    act.wait_ge(abs_done, u + 1)
                    A(cos[:, j], cos[:, j], ACT.Sin, bias=quarter[:, 0:1], scale=-UNDER_TURN).then_inc(trig_done, 1)
                    for q in range(2):
                        act.wait_ge(ss_done, 2 * u + q + 1)
                        act.wait_ge(um_done, 2 * u + 2)
                        A(r[:, q], p_st[:, q * 4:q * 4 + 4, :].rearrange("p a b -> p (a b)"), ACT.Ln,
                          scale=1.0 / N1, bias=eps[:, 0:1]).then_inc(ln_done, 1)
                    for q in range(2):
                        act.wait_ge(ln_done, 2 * u + q + 1)
                        A(r[:, q], r[:, q], ACT.Exp, scale=-0.5).then_inc(r_done, 1)
                    act.wait_ge(e_done, u + 2)
                    A(dec[:, j], pe_g[:], ACT.Exp).then_inc(d_done, 1)
            take_b(UNITS)

        @block.vector
        def _(dve):
            V = nc.vector
            dve.wait_ge(const_in, 16 * 5)
            V.tensor_copy(con[:], con_f[:]).then_inc(const_ready, 1)
            V.tensor_copy(strict[:], strict_f[:].rearrange("p (o t) -> p o t", o=1).broadcast_to([P, 4, P])).then_inc(const_ready, 1)
            V.memset(eps[:], RMS_EPS).then_inc(const_ready, 1)
            V.memset(quarter[:], math.pi / 2).then_inc(const_ready, 1)
            V.memset(ones[:], 1.0).then_inc(const_ready, 1)
            V.tensor_copy(pairs_sum[:].rearrange("p (h d) -> p h d", d=HP),
                          blocks[:].rearrange("p (h d) -> p h d", d=P1)[:, :, 0:1].broadcast_to([P, 2, HP])).then_inc(const_ready, 1)
            dve.wait_ge(const_ready, at_start)
            PER = 7

            def masked(u, j):
                dve.wait_ge(dd_done, u + 1)
                for half in range(2):
                    dve.wait_ge(g_done, 2 * u + half + 1)
                    if half == 0:
                        dve.wait_ge(yp_done, u + 1)
                    at = slice(half * 4, half * 4 + 4)
                    V.tensor_tensor(gm[:, at, :], pe_g[:, at, :], dec[:, j, at, :], ALU.mult).then_inc(gm_done, 1)

            def states(u, j, link):
                dve.wait_ge(u_done, u + 1)
                link(V.tensor_tensor(state[:].rearrange("p c (e d) -> p (c e) d", d=PW),
                                     p_u[:, 0:6 * PW].rearrange("p (g d) -> p g d", d=PW),
                                     blocks[:].rearrange("p (o d) -> p o d", o=1).broadcast_to([P, 6, PW]), ALU.mult))
                link(V.scalar_tensor_tensor(state[:, 1], state[:, 0], aend[:, j, 1:2], state[:, 1], ALU.mult, ALU.add))
                V.scalar_tensor_tensor(state[:, 2], state[:, 1], aend[:, j, 2:3], state[:, 2], ALU.mult, ALU.add)\
                 .then_inc(s_ready, 1)

            def combine(u, par, b, j, link):
                dve.wait_ge(yp_done, u + 1)
                el = tk[:, ds(par, 1), 3, j, ds((b // 2) * 8 + 2, 6)].rearrange("p a (g o) -> p (a g) o", o=1)
                link(V.tensor_tensor(inter[:].rearrange("p c (h d) -> p (c h) d", d=P1),
                                     y_far.rearrange("p (g d) -> p g d", d=P1),
                                     el.broadcast_to([P, 6, P1]), ALU.mult))
                V.tensor_copy(yo[:, ds(par, 1), ds(b * TPB, 1), :], y_in[:, 0:PW].rearrange("p (a c d) -> p a c d", a=1, c=1))
                V.tensor_tensor(yo[:, ds(par, 1), ds(b * TPB + 1, TPB - 1), :],
                                y_in[:, PW:TPB * PW].rearrange("p (a c d) -> p a c d", a=1, d=PW),
                                inter[:].rearrange("p (a c) d -> p a c d", a=1), ALU.add).then_inc(y_ready, 1)

            def rotate(u, j, pair, q, link):
                S = V.scalar_tensor_tensor
                dve.wait_ge(trig_done, u)
                dve.wait_ge(r_done, 2 * u + q + 1)
                x0, x1 = xw[:, j, 2 * q], xw[:, j, 2 * q + 1]
                V.tensor_tensor(x0, x0, r[:, q], ALU.mult)
                V.tensor_tensor(x1, x1, r[:, q], ALU.mult).then_inc(um_done, 1)
                dve.wait_ge(um_done, 2 * u + q + 1)
                b0, b1 = bias[:, ds(pair, 1), 2 * q], bias[:, ds(pair, 1), 2 * q + 1]
                dve.wait_ge(yp_done, u)
                if q == 0:
                    dve.wait_ge(yb_done, 2 * u)
                S(rot[:, j, 2 * q], x0, b0, cos[:, j], ALU.add, ALU.mult)
                first = S(tmp[:, 2 * q], x1, b1, sin[:, j], ALU.add, ALU.mult)
                if q == 0:
                    first.then_inc(rope_b, 1)
                else:
                    n = link.mark(first)
                S(rot[:, j, 2 * q + 1], x0, b0, sin[:, j], ALU.add, ALU.mult)
                second = S(tmp[:, 2 * q + 1], x1, b1, cos[:, j], ALU.add, ALU.mult)
                if q == 0:
                    second.then_inc(rope_b, 1)
                else:
                    link.mark(second)
                    link.wait(n)
                    V.tensor_tensor(rot[:, j, 2], rot[:, j, 2], tmp[:, 2], ALU.subtract).then_inc(rope_c, 1)
                    link.wait()
                    V.tensor_tensor(rot[:, j, 3], rot[:, j, 3], tmp[:, 3], ALU.add).then_inc(rope_c, 1)

            with dve.Fori(0, UNITS // 2) as i:
                for j in range(2):
                    u = i * 2 + j
                    before = (u + UNITS - 2) % UNITS
                    bpar, bb = (before // BATCH) % 2, before % BATCH
                    link = Chain(dve, chain_sem, u * PER)
                    pair = ((u + UNITS - 1) % UNITS) // BATCH
                    rotate(u, 1 - j, pair, 0, link)
                    dve.wait_ge(dtb_copied, u + 1)
                    dve.wait_ge(th_done, u + 1)
                    V.tensor_tensor(th[:], ring[1][:], dtb[:], ALU.mult).then_inc(thdt_done, 1)
                    dve.wait_ge(thdt_done, u + 1)
                    link(V.tensor_tensor_scan(th[:], ones[:], th[:], 0.0, ALU.mult, ALU.add))
                    dve.wait_ge(trig_done, u)
                    link(V.tensor_scalar(fr[:], th[:], MAGIC, None, ALU.add))
                    V.scalar_tensor_tensor(fr[:], fr[:], MAGIC, th[:], ALU.subtract, ALU.subtract).then_inc(fr_done, 1)
                    for s in range(2):
                        dve.wait_ge(y_out[s], ((u + 6) // 16) * 16)
                    combine(u, bpar, bb, j, link)
                    rotate(u, 1 - j, pair, 1, link)
                    states(u, 1 - j, link)
                    masked(u, 1 - j)
                    n_ = link.n
            assert n_ == PER, n_
            link = Chain(dve, chain_sem, UNITS * PER)
            rotate(UNITS, 1, PAIRS - 1, 0, link)
            combine(UNITS, 1, BATCH - 2, 0, link)
            rotate(UNITS, 1, PAIRS - 1, 1, link)
            states(UNITS, 1, link)
            masked(UNITS, 1)
            combine(UNITS + 1, 1, BATCH - 1, 1, link)

E1, I1 = 8, 176
WIDE = E1 * I1
ET = WIDE // P

def route(nc, ctx, gate_d, below_d, g):
    sem = lambda n: nc.alloc_semaphore(name=f"rt_{n}")
    loaded, w_split, logit_done, logit_out = sem("load"), sem("wsplit"), sem("logit"), sem("logitout")
    turned, taken, chain_sem, exp_ready, exp_done = sem("turned"), sem("taken"), sem("chain"), sem("expready"), sem("exp")
    staged, back, back_used, cleared = sem("staged"), sem("back"), sem("backused"), sem("cleared")
    with ExitStack() as mem:
        sb = lambda n, s, d=FP32: mem.enter_context(nc.sbuf_tensor(f"rt_{n}", s, d))
        raw, w_hi, w_lo = sb("raw", [P, KD, E1]), sb("whi", [P, KD, E1], FP32R), sb("wlo", [P, KD, E1], FP32R)
        below = sb("below", [P, E1, E1])
        lg = sb("lg", [E1, 2, SEQ])
        prob = sb("prob", [P, TILES, E1])
        top, total = sb("top", [P, TILES]), sb("total", [P, TILES])
        ge, gt = sb("ge", [P, TILES, E1, E1]), sb("gt", [P, TILES, E1, E1])
        rank = sb("rank", [P, TILES, E1])
        stage = sb("stage", [P, 2, TPB, E1])
        rest, part = sb("rest", [E1, 2, SEQ]), sb("part", [E1, 2, SEQ], BF16)
        ps = lambda n, s: mem.enter_context(nc.psum_tensor(f"rt_{n}", s, FP32))
        pl = [ps(f"pl{i}", [E1, SEQ]) for i in range(2)]
        pt = [ps(f"pt{i}", [P, TPB, E1]) for i in range(2)]
        pc = [ps(f"pc{i}", [E1, SEQ]) for i in range(2)]
        block = mem.enter_context(nc.Block())

        @block.sync
        def _(sp):
            sp.dma_start(raw[:], gate_d).then_inc(loaded, 16)
            sp.dma_start(below[:], below_d).then_inc(loaded, 16)

        @block.gpsimd
        def _(pool):
            nc.gpsimd.memset(g.combine[:], 0.0).then_inc(cleared, 1)

        @block.tensor
        def _(pe):
            pe.wait_ge(w_split, 2)
            with pe.Fori(0, BATCH // 2) as i:
                for p in range(2):
                    b = i * 2 + p
                    pe.wait_ge(logit_out, b + 1)
                    for k in range(KD):
                        last = matmul3(nc, pl[p][:], w_hi[:, k, :], w_lo[:, k, :], g.x_hi[:, k, ds(b * SEQ, SEQ)],
                                       g.x_lo[:, k, ds(b * SEQ, SEQ)], k == 0, k == KD - 1)
                    last.then_inc(logit_done, 1)
                for p in range(2):
                    b = i * 2 + p
                    pe.wait_ge(logit_out, b + 3)
                    pe.wait_ge(taken, b + 1)
                    for n in range(TPB):
                        last = nc.tensor.matmul(pt[p][:, n, :], lg[:, p, n * P:(n + 1) * P], g.ident[0:E1, 0:E1],
                                                start=True, stop=True)
                    last.then_inc(turned, 1)
            with pe.Fori(0, BATCH // 2) as i:
                for p in range(2):
                    b = i * 2 + p
                    pe.wait_ge(staged, b + 1)
                    pe.wait_ge(back_used, i * 2)
                    for n in range(TPB):
                        last = nc.tensor.transpose(pc[p][:, n * P:(n + 1) * P], stage[:, p, n, :], g.ident[:])
                    last.then_inc(back, 1)

        @block.scalar
        def _(act):
            act.sem_inc(logit_out, 2)
            with act.Fori(0, BATCH // 2) as i:
                for p in range(2):
                    b = i * 2 + p
                    act.wait_ge(logit_done, b + 1)
                    act.wait_ge(turned, i * 2)
                    nc.scalar.activation(lg[:, p], pl[p][:], ACT.Copy).then_inc(logit_out, 1)
            act.wait_ge(exp_ready, 1)
            nc.scalar.activation(prob[:], prob[:], ACT.Exp).then_inc(exp_done, 1)

        @block.vector
        def _(dve):
            V = nc.vector
            link = Chain(dve, chain_sem)
            dve.wait_ge(loaded, 32)
            V.tensor_copy(w_hi[:], raw[:]).then_inc(w_split, 1)
            dve.wait_ge(w_split, 1)
            V.tensor_tensor(w_lo[:], raw[:], w_hi[:].bitcast(FP32), ALU.subtract).then_inc(w_split, 1)
            dve.sem_inc(taken, 2)
            with dve.Fori(0, BATCH // 2) as i:
                for p in range(2):
                    b = i * 2 + p
                    dve.wait_ge(turned, b + 1)
                    V.tensor_copy(prob[:, ds(b * TPB, TPB), :], pt[p][:]).then_inc(taken, 1)
            dve.wait_ge(taken, BATCH + 2)
            over_e = lambda a: a[:].rearrange("p (t o) -> p t o", o=1).broadcast_to([P, TILES, E1])
            link(V.tensor_reduce(top[:], prob[:], AX.X, ALU.max))
            V.tensor_tensor(prob[:], prob[:], over_e(top), ALU.subtract).then_inc(exp_ready, 1)
            dve.wait_ge(exp_done, 1)
            link(V.tensor_reduce(total[:], prob[:], AX.X, ALU.add))
            link(V.reciprocal(total[:], total[:]))
            link(V.tensor_tensor(prob[:], prob[:], over_e(total), ALU.mult))
            p_j = prob[:].rearrange("p t (o j) -> p t o j", o=1).broadcast_to([P, TILES, E1, E1])
            p_e = prob[:].rearrange("p t (e o) -> p t e o", o=1).broadcast_to([P, TILES, E1, E1])
            low = below[:].rearrange("p (o e) j -> p o e j", o=1).broadcast_to([P, TILES, E1, E1])
            link.mark(V.tensor_tensor(ge[:], p_j, p_e, ALU.is_ge))
            link(V.tensor_tensor(gt[:], p_j, p_e, ALU.is_gt))
            link(V.tensor_tensor(ge[:], ge[:], gt[:], ALU.subtract))
            link(V.tensor_tensor(ge[:], ge[:], low, ALU.mult))
            link(V.tensor_tensor(gt[:], gt[:], ge[:], ALU.add))
            link(V.tensor_reduce(rank[:], gt[:], AX.X, ALU.add))
            link(V.scalar_tensor_tensor(prob[:], rank[:], 2.0, prob[:], ALU.is_lt, ALU.mult))
            link(V.tensor_reduce(total[:], prob[:], AX.X, ALU.add))
            link(V.reciprocal(total[:], total[:]))
            link(V.tensor_tensor(prob[:], prob[:], over_e(total), ALU.mult))
            dve.wait_ge(cleared, 1)
            base = link.n
            PER = 4
            with dve.Fori(0, BATCH // 2) as i:
                for p in range(2):
                    b = i * 2 + p
                    dve.wait_ge(back, i * 2)
                    V.tensor_copy(stage[:, p], prob[:, ds(b * TPB, TPB), :]).then_inc(staged, 1)
                for p in range(2):
                    b = i * 2 + p
                    link = Chain(dve, chain_sem, base + b * PER)
                    cols = ds(b * SEQ, SEQ)
                    dve.wait_ge(back, b + 1)
                    link(V.tensor_copy(g.combine[0:E1, cols], pc[p][:]))
                    link(V.tensor_tensor(rest[:, p], pc[p][:], g.combine[0:E1, cols], ALU.subtract))
                    link(V.tensor_copy(part[:, p], rest[:, p]))
                    link.mark(V.tensor_copy(g.combine[32:32 + E1, cols], part[:, p]))
                    V.tensor_tensor(g.combine[64:64 + E1, cols], rest[:, p], part[:, p], ALU.subtract).then_inc(back_used, 1)

def experts(nc, ctx, src, dst, w1_d, w2_d, owner_d, g):
    sem = lambda n: nc.alloc_semaphore(name=f"mo_{n}")
    w_loaded, w_split, d_loaded = sem("wload"), sem("wsplit"), sem("dload")
    gate_done, up_done, bc_done, silu_done, t_done, h_done = (sem(n) for n in ("gate", "up", "bc", "silu", "t", "h"))
    down_step, out_done = sem("down"), sem("out")
    stored, res_loaded = [sem("st0"), sem("st1")], [sem("res0"), sem("res1")]
    with ExitStack() as mem:
        sb = lambda n, s, d=FP32: mem.enter_context(nc.sbuf_tensor(f"mo_{n}", s, d))
        w_hi, w_lo = ([sb(f"w{n}{q}", [P, KD, WIDE], FP32R) for q in "gu"] for n in ("hi", "lo"))
        raw = sb("raw", [P, WIDE])
        wd = sb("wd", [P, ET, DM])
        owner_f, owner = sb("ownf", [96, ET, P]), sb("own", [96, ET, P], BF16)
        silu, h = sb("silu", [P, 2, SEQ]), sb("h", [P, 2, SEQ])
        out = sb("outt", [P, 2, TPB, DM])
        ps = lambda n, s: mem.enter_context(nc.psum_tensor(f"mo_{n}", s, FP32))
        pg, pu, pb = ([ps(f"p{n}{i}", [P, SEQ]) for i in range(2)] for n in "gub")
        pd = ps("pd", [P, TPB, DM])
        block = mem.enter_context(nc.Block())
        src_v = src.rearrange("(b n p) d -> b p n d", p=P, n=TPB)
        dst_v = dst.rearrange("(b n p) d -> b p n d", p=P, n=TPB)
        parts = [(q, k) for q in range(2) for k in range(KD)]

        @block.sync
        def _(sp):
            sp.dma_start(wd[:], w2_d).then_inc(d_loaded, 16)
            sp.dma_start(owner_f[:], owner_d).then_inc(d_loaded, 16)
            for n, (q, k) in enumerate(parts):
                if n:
                    sp.wait_ge(w_split, 2 * n)
                sp.dma_start(raw[:], w1_d[:, q, k, :]).then_inc(w_loaded, 16)
            with sp.Fori(0, BATCH // 2) as i:
                for p in range(2):
                    b = i * 2 + p
                    sp.wait_ge(stored[p], 16 * i)
                    sp.dma_start(out[:, p], src_v[ds(b, 1)].rearrange("a p n d -> p (a n) d")).then_inc(res_loaded[p], 16)
                for p in range(2):
                    b = i * 2 + p
                    sp.wait_ge(out_done, b + 1)
                    sp.dma_start(dst_v[ds(b, 1)].rearrange("a p n d -> p (a n) d"), out[:, p]).then_inc(stored[p], 16)
            for p in range(2):
                sp.wait_ge(stored[p], 16 * (BATCH // 2))

        @block.gpsimd
        def _(pool):
            for n in range(len(parts)):
                q, k = parts[n]
                pool.wait_ge(w_split, 2 * n + 1)
                nc.gpsimd.tensor_tensor(w_lo[q][:, k, :], raw[:], w_hi[q][:, k, :].bitcast(FP32),
                                        ALU.subtract).then_inc(w_split, 1)

        def product(w, b, s, psum):
            for k in range(KD):
                cols = slice(s * P, (s + 1) * P)
                last = matmul3(nc, psum, w_hi[w][:, k, cols], w_lo[w][:, k, cols], g.x_hi[:, k, ds(b * SEQ, SEQ)],
                               g.x_lo[:, k, ds(b * SEQ, SEQ)], k == 0, k == KD - 1)
            return last

        @block.tensor
        def _(pe):
            pe.wait_ge(w_split, 2 * len(parts))
            pe.wait_ge(d_loaded, 33)

            def down(b, q, s):
                pe.wait_ge(h_done, b * ET + s + 3)
                for n in range(TPB):
                    last = nc.tensor.matmul(pd[:, n, :], h[:, q % 2, n * P:(n + 1) * P], wd[:, s, :],
                                            start=s == 0 and n % 2 == 0, stop=s == ET - 1 and n % 2 == 1,
                                            skip_group_check=True)
                last.then_inc(down_step, 1)

            pe.sem_inc(down_step, 2)
            with pe.Fori(0, BATCH // 2) as i:
                for q in range(2 * ET):
                    p, s = divmod(q, ET)
                    b = i * 2 + p
                    n = b * ET + s
                    pe.wait_ge(silu_done, n + 1)
                    product(0, b, s, pg[q % 2][:]).then_inc(gate_done, 1)
                    pe.wait_ge(h_done, n + 1)
                    product(1, b, s, pu[q % 2][:]).then_inc(up_done, 1)
                    nc.tensor.matmul(pb[q % 2][:], owner[:, s, :], g.combine[:, ds(b * SEQ, SEQ)],
                                     start=True, stop=True).then_inc(bc_done, 1)
                    if s == 1:
                        pe.wait_ge(out_done, b)
                    if s:
                        down(b, q - 1, s - 1)
                    if s == ET - 1:
                        down(b, q, s)

        @block.scalar
        def _(act):
            act.sem_inc(silu_done, 2)
            for n, (q, k) in enumerate(parts):
                act.wait_ge(w_loaded, 16 * (n + 1))
                nc.scalar.activation(w_hi[q][:, k, :], raw[:], ACT.Copy).then_inc(w_split, 1)
                if n < len(parts) - 1:
                    act.wait_ge(w_split, 2 * n + 2)
            nc.scalar.preload_act_table(ACT.Silu)
            with act.Fori(0, BATCH // 2) as i:
                for q in range(2 * ET):
                    n = i * (2 * ET) + q
                    act.wait_ge(gate_done, n + 1)
                    act.wait_ge(h_done, n + 1)
                    nc.scalar.activation(silu[:, q % 2], pg[q % 2][:], ACT.Silu).then_inc(silu_done, 1)

        @block.vector
        def _(dve):
            V = nc.vector
            dve.wait_ge(d_loaded, 32)
            V.tensor_copy(owner[:], owner_f[:]).then_inc(d_loaded, 1)
            dve.sem_inc(h_done, 2)
            with dve.Fori(0, BATCH // 2) as i:
                for q in range(2 * ET):
                    p, s = divmod(q, ET)
                    b = i * 2 + p
                    n = b * ET + s
                    dve.wait_ge(silu_done, n + 3)
                    dve.wait_ge(up_done, n + 1)
                    V.tensor_tensor(silu[:, q % 2], pu[q % 2][:], silu[:, q % 2], ALU.mult).then_inc(t_done, 1)
                    dve.wait_ge(t_done, n + 1)
                    dve.wait_ge(bc_done, n + 1)
                    dve.wait_ge(down_step, n + 1)
                    V.tensor_tensor(h[:, q % 2], pb[q % 2][:], silu[:, q % 2], ALU.mult).then_inc(h_done, 1)
                    if s == ET - 1:
                        dve.wait_ge(down_step, (b + 1) * ET + 2)
                        dve.wait_ge(res_loaded[p], i * 16 + 16)
                        V.tensor_tensor(out[:, p], pd[:], out[:, p], ALU.add).then_inc(out_done, 1)

def ffn0_weights(gate, up, down):
    def cols(w):
        w = w.reshape(KD, P, GT, P, GROUP).transpose(1, 0, 2, 4, 3)
        return np.ascontiguousarray(w).reshape(P, KD, I0)
    d = down.reshape(GT, P, GROUP, DM).transpose(1, 0, 2, 3)
    return cols(gate), cols(up), np.ascontiguousarray(d).reshape(P, SLOTS, DM)

def moe_weights(gate_w, w1, w2):
    wt = np.ascontiguousarray(gate_w.T.reshape(KD, P, E1).transpose(1, 0, 2))
    w = w1.reshape(E1, 2, I1, KD, P).transpose(4, 1, 3, 0, 2)
    d = w2.transpose(0, 2, 1).reshape(ET, P, DM).transpose(1, 0, 2)
    below = np.broadcast_to(np.tril(np.ones((E1, E1), np.float32), -1), (P, E1, E1))
    owner = np.zeros((3, 32, ET, P), np.float32)
    rows = np.arange(WIDE)
    owner[:, rows // I1, rows // P, rows % P] = 1.0
    return (wt, np.ascontiguousarray(w).reshape(P, 2, KD, WIDE), np.ascontiguousarray(d),
            np.ascontiguousarray(below), owner.reshape(96, ET, P))

def attention0_weights(q_sem, k_sem, q_geo, k_geo, v, o):
    half = DH // 2
    quarter = half // 2

    def cols(sem, geo):
        sem, geo = sem.reshape(H0, half, DM), geo.reshape(H0, half, DM)
        plain = np.concatenate([sem, geo], 1)
        turned = np.concatenate([np.zeros_like(sem), geo[:, quarter:], geo[:, :quarter]], 1)
        both = np.stack([plain, turned])
        both = np.concatenate([both, both], 2).reshape(2 * G0 * P, DM)
        return both

    w = np.concatenate([cols(q_sem, q_geo), cols(k_sem, k_geo), v])
    w = np.ascontiguousarray(w.T.reshape(KD, P, -1).transpose(1, 0, 2))
    return w, np.ascontiguousarray(o.T.reshape(KD, P, DM).transpose(1, 0, 2))

def attention0_tables():
    half = DH // 2
    quarter = half // 2
    inv = (1.0 / np.float32(10000.0) ** (np.arange(0, half, 2, dtype=np.float32) / np.float32(half))).astype(np.float32)
    freq = (np.arange(SEQ, dtype=np.float32)[:, None] * inv[None, :]).astype(np.float32)
    cos, sin = np.cos(freq).T, np.sin(freq).T
    one, nil = np.ones((half, SEQ), np.float32), np.zeros((half, SEQ), np.float32)
    c = np.concatenate([one, cos, cos])
    s = np.concatenate([nil, -sin, sin])
    c, s = np.tile(c, (2 * HG, 1)), np.tile(s, (2 * HG, 1))
    scale = np.float32(DH ** -0.5)
    tables = np.stack([c * scale, s * scale, c, s], 1).astype(np.float32)
    lower = np.where(np.arange(P) % (2 * DH) >= DH, -1.0, 0.0).astype(np.float32)[:, None]
    above = np.where(np.arange(P)[None, :] > np.arange(P)[:, None], -3e38, 0.0).astype(np.float32)
    return tables, np.ascontiguousarray(lower), above

def kmajor(w):
    return np.ascontiguousarray(w.T.reshape(-1, P, w.shape[0]).transpose(1, 0, 2))

def gate_weights(wdt, wlam, a_log):
    w = np.zeros((2, 2, 2, H1, DM), np.float32)
    for j in range(2):
        w[0, j, j], w[1, j, j] = wdt, wlam
    w = w.reshape(2, 2, P, KD, P).transpose(4, 3, 0, 1, 2)
    return np.ascontiguousarray(w), np.ascontiguousarray(np.tile(a_log, 2)[:, None])

def state_weights(wth, wb, wc):
    half = N1 // 2
    parts = [wth.reshape(PAIRS, 2, half, DM)]
    for w in (wb, wc):
        w = w.reshape(PAIRS, 2, half, 2, DM)
        parts += [w[:, :, :, 0], w[:, :, :, 1]]
    w = np.stack(parts, 1)
    return np.ascontiguousarray(w.reshape(PAIRS, WC, KD, P).transpose(0, 3, 2, 1))

def state_norm(bn, cn):
    return np.ascontiguousarray(np.stack([np.tile(w[e::2], 2) for w in (bn, cn) for e in range(2)], 1))

def state_bias(b, c):
    b = np.stack([w.reshape(PAIRS, P, 2)[:, :, e] for w in (b, c) for e in range(2)], 2)
    return np.ascontiguousarray(b.transpose(1, 0, 2))

def state_constants():
    con = np.zeros((6, 5, P), np.float32)
    for h in range(2):
        rows = slice(3 * h, 3 * h + 3)
        con[rows, 0, h * H1:(h + 1) * H1] = 1.0
        con[rows, 1 + h] = 1.0
        con[rows, 3 + h] = -1.0
    t = np.arange(P)
    strict = np.where(t[None, :] > t[:, None], 0.0, -3e38).astype(np.float32)
    blocks = (t[:, None] // H1 == np.arange(PW)[None, :] // P1).astype(np.float32)
    return con, strict, np.ascontiguousarray(blocks)

@contextmanager
def phase(nc):
    before = nc.snapshot_sems()
    yield
    nc.clear_and_free_semaphores(nc.allocated_since(before))
    nc.all_engine_barrier()

def program(nc, i, scratch, out):
    x1, x2, x3, tk, rows, xp, y = scratch
    with ExitStack() as ctx:
        g = constants(nc, ctx)
        with phase(nc):
            layernorm_transposed(nc, ctx, "ln0", i["x"], g)
        with phase(nc):
            causal_attention(nc, ctx, i["x"], x1, i["w_qkv"], i["w_o"], i["rope"], i["lower"], i["above"], g)
        with phase(nc):
            layernorm_transposed(nc, ctx, "ln1", x1, g)
        with phase(nc):
            sparse_swiglu(nc, ctx, x1, x2, i["w_gate"], i["w_up"], i["w_down"], g)
        with phase(nc):
            layernorm_transposed(nc, ctx, "ln2", x2, g)
        with phase(nc):
            gates(nc, ctx, i["w_dt"], i["a_log"], tk, rows, g)
        with phase(nc):
            input_projection(nc, ctx, i["w_x"], xp, g)
        with phase(nc):
            state_space(nc, ctx, i["w_state"], i["state_norm"], i["state_bias"], i["state_con"], i["strict"], i["blocks"],
                        tk, rows, xp, y, g)
        with phase(nc):
            output_projection(nc, ctx, x2, x3, i["w_z"], i["w_out"], y, g)
        with phase(nc):
            layernorm_transposed(nc, ctx, "ln3", x3, g)
        g.combine = ctx.enter_context(nc.sbuf_tensor("combine", [96, TOK], BF16))
        with phase(nc):
            route(nc, ctx, i["w_route"], i["below"], g)
        with phase(nc):
            experts(nc, ctx, x3, out, i["w_1"], i["w_2"], i["owner"], g)

def kernel(**inputs):
    from concourse.bacc import Bacc
    from concourse.bass_utils import run_bass_kernel_spmd

    a = {n: np.ascontiguousarray(v) for n, v in inputs.items()}
    x = a["L0_attn_x"]
    i = {"x": x.reshape(TOK, DM)}
    i["w_qkv"], i["w_o"] = attention0_weights(*(a[f"L0_attn_{n}"] for n in ("Wq_sem", "Wk_sem", "Wq_geo", "Wk_geo", "Wv", "Wo")))
    i["rope"], i["lower"], i["above"] = attention0_tables()
    i["w_gate"], i["w_up"], i["w_down"] = ffn0_weights(*(a[f"L0_ffn_{n}"] for n in ("w_gate", "w_up", "w_down")))
    i["w_dt"], i["a_log"] = gate_weights(a["L1_attn_Wdt"], a["L1_attn_Wlam"], a["L1_attn_A_log"])
    i["w_x"], i["w_z"], i["w_out"] = (kmajor(a[f"L1_attn_{n}"]) for n in ("Wx", "Wz", "Wout"))
    i["w_state"] = state_weights(a["L1_attn_Wth"], a["L1_attn_WB"], a["L1_attn_WC"])
    i["state_norm"] = state_norm(a["L1_attn_Bn_w"], a["L1_attn_Cn_w"])
    i["state_bias"] = state_bias(a["L1_attn_B_bias"], a["L1_attn_C_bias"])
    i["state_con"], i["strict"], i["blocks"] = state_constants()
    i["w_route"], i["w_1"], i["w_2"], i["below"], i["owner"] = moe_weights(a["L1_ffn_gate_w"], a["L1_ffn_w1"], a["L1_ffn_w2"])

    nc = Bacc("TRN2", target_bir_lowering=False, num_devices=1)
    arrays = {f"in_{n}": np.ascontiguousarray(v) for n, v in i.items()}
    ins = {n: nc.dram_tensor(f"in_{n}", list(v.shape), FP32, kind="ExternalInput").ap() for n, v in i.items()}
    inner = lambda n, s, d=FP32: nc.dram_tensor(n, s, d, kind="Internal").ap()
    scratch = [inner(f"x{n}", [TOK, DM]) for n in (1, 2, 3)]
    scratch += [inner("token_gates", [PAIRS, P, 256]), inner("gate_rows", [384, 2, CW], BF16),
                inner("x_heads", [TOK, DIN]), inner("y_heads", [TOK, DIN])]
    out = nc.dram_tensor("out", [TOK, DM], FP32, kind="ExternalOutput").ap()
    program(nc, ins, scratch, out)
    r = run_bass_kernel_spmd(nc, [arrays], core_ids=[0])
    return r.results[0]["out"].reshape(x.shape)
```
